# Optimizing a Trainium2 kernel written in Bass

```python
import numpy as np
import jax
import jax.numpy as jnp

def _softmax(x, axis=-1):
    return jax.nn.softmax(x, axis=axis)

def _gelu(x):
    return jax.nn.gelu(x, approximate=True)

def _silu(x):
    return jax.nn.silu(x)

def _sigmoid(x):
    return jax.nn.sigmoid(x)

def _layernorm(x, axis=-1, eps=1e-05):
    m = jnp.mean(x, axis=axis, keepdims=True)
    v = jnp.var(x, axis=axis, keepdims=True)
    return (x - m) / jnp.sqrt(v + eps)

def _scatter_add(tgt, idx, src, axis=0):
    return tgt.at[idx].add(src)

def _segment_sum(src, seg, n):
    return jax.ops.segment_sum(src, seg, n)
kernel_name = 'mk_gnn_resnorm_d4_gnn_r32_ea3413'

def setup_inputs(seed: int=0):
    np.random.seed(seed)
    _w = jnp.asarray

    def _rec_inputs():
        import jax
        import jax.numpy as jnp
        _gk = jax.random.key(seed)
        x = -0.000202 + 1 * jax.random.normal(jax.random.fold_in(_gk, 1), (3125, 128), jnp.float32)
        _s = jax.random.randint(jax.random.fold_in(_gk, 2), (50000,), 0, 3125, jnp.int32)
        _d = jax.random.randint(jax.random.fold_in(_gk, 3), (50000,), 0, 3125, jnp.int32)
        _loop = jnp.arange(3125, dtype=jnp.int32)
        src = jnp.concatenate([_s, _d, _loop])
        dst = jnp.concatenate([_d, _s, _loop])
        _o = jnp.argsort(dst, stable=True)
        src = src[_o]
        dst = dst[_o]
        edge_attr_16 = -1.40915e-05 + 1.00011 * jax.random.normal(jax.random.fold_in(_gk, 12), (103125, 16), jnp.float32)
        edge_weight = jax.random.uniform(jax.random.fold_in(_gk, 14), (103125,), jnp.float32, 0.0, 0.999999)
        return (x, src, dst, edge_attr_16, edge_weight)
    x, src, dst, edge_attr_16, edge_weight = _rec_inputs()

    def _L0_gnn_setup():
        import jax, jax.numpy as jnp
        import numpy as np
        N_NODES = 50000
        N_EDGES = 25000
        D_FEAT = 128
        HIDDEN = 128
        BN_EPS = 1e-05

        def _gcn_conv(h, row, col, norm, W, b, n_nodes):
            m = norm[:, None] * (h @ W)[row]
            return jax.ops.segment_sum(m, col, num_segments=n_nodes) + b
        key = jax.random.key(seed)
        ks = jax.random.split(key, 12)
        s_in = 1.0 / np.sqrt(D_FEAT)
        s_h = 1.0 / np.sqrt(HIDDEN)
        return {'x': jax.random.normal(ks[0], (N_NODES, D_FEAT), dtype=jnp.float32), 'edge_index': jax.random.randint(ks[1], (2, N_EDGES), 0, N_NODES, dtype=jnp.int64), 'W_enc': jax.random.uniform(ks[2], (D_FEAT, HIDDEN), jnp.float32, -s_in, s_in), 'b_enc': jax.random.uniform(ks[3], (HIDDEN,), jnp.float32, -s_in, s_in), 'bn_gamma': 1.0 + 0.1 * jax.random.normal(ks[4], (HIDDEN,), jnp.float32), 'bn_beta': 0.1 * jax.random.normal(ks[5], (HIDDEN,), jnp.float32), 'bn_mean': 0.1 * jax.random.normal(ks[6], (HIDDEN,), jnp.float32), 'bn_var': jnp.ones((HIDDEN,), jnp.float32), 'W1': jax.random.uniform(ks[7], (HIDDEN, HIDDEN), jnp.float32, -s_h, s_h), 'b1': jnp.zeros((HIDDEN,), jnp.float32), 'W2': jax.random.uniform(ks[8], (HIDDEN, HIDDEN), jnp.float32, -s_h, s_h), 'b2': jnp.zeros((HIDDEN,), jnp.float32)}
    _L0_gnn_all = _L0_gnn_setup()
    _L0_gnn_in = {k: v for k, v in _L0_gnn_all.items() if k in ('W_enc', 'b_enc', 'bn_gamma', 'bn_beta', 'bn_mean', 'bn_var', 'W1', 'b1', 'W2', 'b2')}
    del _L0_gnn_all

    def _L1_gnn_setup():
        import jax, jax.numpy as jnp
        import numpy as np
        N_NODES = 50000
        N_EDGES = 25000
        D_IN = 128
        D_OUT = 128
        key = jax.random.key(seed)
        ks = jax.random.split(key, 7)
        feat = jax.random.normal(ks[0], (N_NODES, D_IN), dtype=jnp.float32)
        edge_src = jax.random.randint(ks[1], (N_EDGES,), 0, N_NODES, dtype=jnp.int32)
        edge_dst = jax.random.randint(ks[2], (N_EDGES,), 0, N_NODES, dtype=jnp.int32)
        edge_weight = jax.random.uniform(ks[3], (N_EDGES,), dtype=jnp.float32)
        gain = float(np.sqrt(2.0))
        bound = gain * float(np.sqrt(6.0 / (D_IN + D_OUT)))
        W_neigh = jax.random.uniform(ks[4], (D_OUT, D_IN), dtype=jnp.float32, minval=-bound, maxval=bound)
        W_self = jax.random.uniform(ks[5], (D_OUT, D_IN), dtype=jnp.float32, minval=-bound, maxval=bound)
        b_self = jnp.zeros((D_OUT,), dtype=jnp.float32)
        return {'feat': feat, 'edge_src': edge_src, 'edge_dst': edge_dst, 'edge_weight': edge_weight, 'W_neigh': W_neigh, 'W_self': W_self, 'b_self': b_self}
    _L1_gnn_all = _L1_gnn_setup()
    _L1_gnn_in = {k: v for k, v in _L1_gnn_all.items() if k in ('W_neigh', 'W_self', 'b_self')}
    del _L1_gnn_all

    def _L2_gnn_setup():
        import jax, jax.numpy as jnp
        import numpy as np
        N_LAYERS = 5
        key = jax.random.key(seed)
        ks = jax.random.split(key, 8)
        N, E, D, EIN = (1250, 20000, 128, 16)
        x = jax.random.normal(ks[0], (N, D), dtype=jnp.float32)
        src = jax.random.randint(ks[1], (E,), 0, N)
        dst = (src + 1 + jax.random.randint(ks[2], (E,), 0, N - 1)) % N
        edge_index = jnp.stack([src, dst], axis=0)
        edge_attr = jax.random.normal(ks[3], (E, EIN), dtype=jnp.float32)
        weights = jax.random.normal(ks[4], (N_LAYERS, D, D), dtype=jnp.float32) * (1.0 / np.sqrt(D))
        biases = jnp.zeros((N_LAYERS, D), dtype=jnp.float32)
        edge_ws = jax.random.normal(ks[5], (N_LAYERS, D, EIN), dtype=jnp.float32) * (1.0 / np.sqrt(EIN))
        edge_bs = jnp.zeros((N_LAYERS, D), dtype=jnp.float32)
        return {'x': x, 'edge_index': edge_index, 'edge_attr': edge_attr, 'weights': weights, 'biases': biases, 'edge_ws': edge_ws, 'edge_bs': edge_bs}
    _L2_gnn_all = _L2_gnn_setup()
    _L2_gnn_in = {k: v for k, v in _L2_gnn_all.items() if k in ('weights', 'biases', 'edge_ws', 'edge_bs')}
    del _L2_gnn_all

    def _L3_gnn_setup():
        import jax, jax.numpy as jnp
        import numpy as np
        N_NODES = 3125
        N_EDGES = 25000
        D_IN = 128
        D_OUT = 128
        E_DIM = 16
        key = jax.random.key(seed)
        k1, k2, k3, k4, k5 = jax.random.split(key, 5)
        x = jax.random.normal(k1, (N_NODES, D_IN), dtype=jnp.float32)
        edge_index = jax.random.randint(k2, (2, N_EDGES), 0, N_NODES, dtype=jnp.int64)
        edge_attr = jax.random.normal(k3, (N_EDGES, E_DIM), dtype=jnp.float32)
        W = jax.random.uniform(k4, (D_IN, D_OUT), dtype=jnp.float32, minval=-1.0, maxval=1.0) * float(np.sqrt(6.0 / (D_IN + D_OUT)))
        edge_w = jax.random.uniform(k5, (E_DIM, D_OUT), dtype=jnp.float32, minval=-1.0, maxval=1.0) * float(np.sqrt(6.0 / (E_DIM + D_OUT)))
        b = jnp.zeros((D_OUT,), dtype=jnp.float32)
        return {'x': x, 'edge_index': edge_index, 'edge_attr': edge_attr, 'W': W, 'edge_w': edge_w, 'b': b}
    _L3_gnn_all = _L3_gnn_setup()
    _L3_gnn_in = {k: v for k, v in _L3_gnn_all.items() if k in ('W', 'edge_w', 'b')}
    del _L3_gnn_all
    return {'x': x, 'src': src, 'dst': dst, 'edge_attr_16': edge_attr_16, 'edge_weight': edge_weight, 'L0_gnn_W_enc': _L0_gnn_in['W_enc'], 'L0_gnn_b_enc': _L0_gnn_in['b_enc'], 'L0_gnn_bn_gamma': _L0_gnn_in['bn_gamma'], 'L0_gnn_bn_beta': _L0_gnn_in['bn_beta'], 'L0_gnn_bn_mean': _L0_gnn_in['bn_mean'], 'L0_gnn_bn_var': _L0_gnn_in['bn_var'], 'L0_gnn_W1': _L0_gnn_in['W1'], 'L0_gnn_b1': _L0_gnn_in['b1'], 'L0_gnn_W2': _L0_gnn_in['W2'], 'L0_gnn_b2': _L0_gnn_in['b2'], 'L1_gnn_W_neigh': _L1_gnn_in['W_neigh'], 'L1_gnn_W_self': _L1_gnn_in['W_self'], 'L1_gnn_b_self': _L1_gnn_in['b_self'], 'L2_gnn_weights': _L2_gnn_in['weights'], 'L2_gnn_biases': _L2_gnn_in['biases'], 'L2_gnn_edge_ws': _L2_gnn_in['edge_ws'], 'L2_gnn_edge_bs': _L2_gnn_in['edge_bs'], 'L3_gnn_W': _L3_gnn_in['W'], 'L3_gnn_edge_w': _L3_gnn_in['edge_w'], 'L3_gnn_b': _L3_gnn_in['b']}

def reference(x, src, dst, edge_attr_16, edge_weight, L0_gnn_W_enc, L0_gnn_b_enc, L0_gnn_bn_gamma, L0_gnn_bn_beta, L0_gnn_bn_mean, L0_gnn_bn_var, L0_gnn_W1, L0_gnn_b1, L0_gnn_W2, L0_gnn_b2, L1_gnn_W_neigh, L1_gnn_W_self, L1_gnn_b_self, L2_gnn_weights, L2_gnn_biases, L2_gnn_edge_ws, L2_gnn_edge_bs, L3_gnn_W, L3_gnn_edge_w, L3_gnn_b):
    import jax
    import jax.numpy as jnp

    def _L0_gnn_ref(x, edge_index, W_enc, b_enc, bn_gamma, bn_beta, bn_mean, bn_var, W1, b1, W2, b2):
        import jax, jax.numpy as jnp
        import numpy as np
        N_NODES = 50000
        N_EDGES = 25000
        D_FEAT = 128
        HIDDEN = 128
        BN_EPS = 1e-05

        def _gcn_conv(h, row, col, norm, W, b, n_nodes):
            m = norm[:, None] * (h @ W)[row]
            return jax.ops.segment_sum(m, col, num_segments=n_nodes) + b
        n = x.shape[0]
        loops = jnp.arange(n, dtype=edge_index.dtype)
        row = jnp.concatenate([edge_index[0], loops])
        col = jnp.concatenate([edge_index[1], loops])
        deg = jax.ops.segment_sum(jnp.ones(row.shape[0], jnp.float32), col, num_segments=n)
        dis = jnp.where(deg > 0, jax.lax.rsqrt(jnp.maximum(deg, 1.0)), 0.0)
        norm = dis[row] * dis[col]
        h = jax.nn.relu(x @ W_enc + b_enc)
        h = (h - bn_mean) * jax.lax.rsqrt(bn_var + BN_EPS) * bn_gamma + bn_beta
        h = _gcn_conv(h, row, col, norm, W1, b1, n)
        h = jax.nn.relu(h)
        h = _gcn_conv(h, row, col, norm, W2, b2, n)
        return h

    def _L1_gnn_ref(feat, edge_src, edge_dst, edge_weight, W_neigh, W_self, b_self):
        import jax, jax.numpy as jnp
        import numpy as np
        N_NODES = 50000
        N_EDGES = 25000
        D_IN = 128
        D_OUT = 128
        n = feat.shape[0]
        msg = feat[edge_src] * edge_weight[:, None]
        neigh_sum = jax.ops.segment_sum(msg, edge_dst, num_segments=n)
        deg = jax.ops.segment_sum(jnp.ones_like(edge_weight), edge_dst, num_segments=n)
        h_neigh = neigh_sum / jnp.maximum(deg, 1.0)[:, None]
        h_neigh = h_neigh @ W_neigh.T
        rst = feat @ W_self.T + b_self + h_neigh
        return rst

    def _L2_gnn_ref(x, edge_index, edge_attr, weights, biases, edge_ws, edge_bs):
        import jax, jax.numpy as jnp
        import numpy as np
        N_LAYERS = 5
        N, D = x.shape
        EIN = edge_attr.shape[1]
        loop = jnp.arange(N)
        src = jnp.concatenate([edge_index[0], loop])
        dst = jnp.concatenate([edge_index[1], loop])
        ones = jnp.ones(src.shape[0], dtype=x.dtype)
        deg = jax.ops.segment_sum(ones, src, num_segments=N)
        dis = jnp.where(deg > 0, jax.lax.rsqrt(deg), jnp.zeros_like(deg))
        norm = (dis[src] * dis[dst])[:, None]
        ea_full = jnp.concatenate([edge_attr, jnp.zeros((N, EIN), dtype=edge_attr.dtype)], axis=0)
        h = x
        for l in range(N_LAYERS):
            edge_emb = ea_full @ edge_ws[l].T + edge_bs[l]
            hx = h @ weights[l]
            msg = norm * (hx[src] + edge_emb)
            out = jax.ops.segment_sum(msg, dst, num_segments=N) + biases[l]
            h = out if l == N_LAYERS - 1 else jax.nn.relu(out)
        return h

    def _L3_gnn_ref(x, edge_index, edge_attr, W, edge_w, b):
        import jax, jax.numpy as jnp
        import numpy as np
        N_NODES = 3125
        N_EDGES = 25000
        D_IN = 128
        D_OUT = 128
        E_DIM = 16
        src, dst = (edge_index[0], edge_index[1])
        xw = x @ W
        ew = edge_attr @ edge_w
        msg = xw[src] * ew
        out = jax.ops.segment_sum(msg, dst, num_segments=x.shape[0])
        out = out + b
        return out
    edge_index = jnp.stack([src, dst])
    x = _layernorm(x + _L0_gnn_ref(x, edge_index, L0_gnn_W_enc, L0_gnn_b_enc, L0_gnn_bn_gamma, L0_gnn_bn_beta, L0_gnn_bn_mean, L0_gnn_bn_var, L0_gnn_W1, L0_gnn_b1, L0_gnn_W2, L0_gnn_b2), axis=-1)
    x = _layernorm(x + _L1_gnn_ref(x, src, dst, edge_weight, L1_gnn_W_neigh, L1_gnn_W_self, L1_gnn_b_self), axis=-1)
    x = _layernorm(x + _L2_gnn_ref(x, edge_index, edge_attr_16, L2_gnn_weights, L2_gnn_biases, L2_gnn_edge_ws, L2_gnn_edge_bs), axis=-1)
    x = _layernorm(x + _L3_gnn_ref(x, edge_index, edge_attr_16, L3_gnn_W, L3_gnn_edge_w, L3_gnn_b), axis=-1)
    return x

_drawn_inputs = setup_inputs


def setup_inputs(seed=0):
    import zlib

    import numpy as np

    out = dict(_drawn_inputs(seed))
    spreads = {'L0_gnn_bn_var': (1.0, 0.6),
     'L0_gnn_b1': (0.0, 0.8),
     'L0_gnn_b2': (0.0, 0.32),
     'L1_gnn_b_self': (0.0, 0.1),
     'L2_gnn_biases': (0.0, 0.1),
     'L2_gnn_edge_bs': (0.0, 0.1),
     'L3_gnn_b': (0.0, 0.1)}
    factors = {'L0_gnn_W_enc': 8.0, 'L0_gnn_b_enc': 8.0, 'L0_gnn_bn_gamma': 8.0, 'L0_gnn_bn_beta': 7.146}
    for name, (base, spread) in spreads.items():
        noise = np.random.default_rng([zlib.crc32(name.encode()), seed]).standard_normal(out[name].shape)
        drawn = base * np.exp(spread * noise) if base else spread * noise
        out[name] = jnp.asarray(drawn.astype(out[name].dtype))
    for name, factor in factors.items():
        out[name] = (out[name] * factor).astype(out[name].dtype)
    return out
```

```python
from contextlib import ExitStack

import concourse.bass as bass
from concourse import mybir
import numpy as np

F32 = mybir.dt.float32
BF16 = mybir.dt.bfloat16
I32 = mybir.dt.int32
ALU = mybir.AluOpType
ACT = mybir.ActivationFunctionType
AX = mybir.AxisListType

P = 128
N = 3125
NT = -(-N // P)
NP = NT * P
NLAST = N - (NT - 1) * P
E = 103125
EC = E // P
ET = EC + 1
ELAST = E - P * EC
EK = 16
PK = EK + 2
GT = 5
NG = NT // GT
EPS = 1e-5
DUMP = NP

LN_STAGES = (2, 3, 8)
NONE, WEIGHT, ATTR, PROD = range(4)


def steps():
    out = [("turn", "X", "PT"), ("dense", 0)]
    for st, kind, scale, loop in ((1, NONE, "dis", True), (2, NONE, "dis", True)):
        out += [("sum", kind, scale, loop), ("turn", "AG", "PT"), ("dense", st)]
    out += [("turn", "X", "XT"), ("sum", WEIGHT, "inv", False), ("turn", "AG", "PT")]
    out += [("sum", ATTR, "dis2", False), ("turn", "AG", "AUG"), ("dense", 3)]
    for st in range(4, 9):
        out += [("sum", NONE, "dis2", True), ("turn", "AG", "PT"), ("dense", st)]
    out += [("turn", "X", "PT"), ("dense", 9), ("sum", PROD, None, False), ("final",)]
    return out


def host_constants():
    c = np.zeros((P, 4 * P + 1), np.float32)
    c[:, 0:P] = np.eye(P)
    c[:, P:2 * P] = 1.0
    c[:, 2 * P:3 * P] = np.arange(P)[None, :]
    c[:, 3 * P:4 * P] = np.tril(np.ones((P, P)), -1)
    c[:, 4 * P] = np.arange(P) + DUMP
    s = np.zeros((PK, 3, P), np.float32)
    s[EK + 1, NONE, :] = 1.0
    s[EK, WEIGHT, :] = 1.0
    s[:EK, ATTR, :EK] = np.eye(EK)
    s[EK + 1, ATTR, EK] = 1.0
    return c, s


def build(nc, a, out):
    with ExitStack() as ctx:
        def sb(name, shape, dt=F32):
            return ctx.enter_context(nc.sbuf_tensor(name, shape, dt))

        def sem(name):
            return ctx.enter_context(nc.semaphore(name))

        const = sb("const", [P, 4 * P + 1])
        ident, ones, iota, tril = (const[:, i * P:(i + 1) * P] for i in range(4))
        dump_row = const[:, 4 * P:4 * P + 1]
        sels = sb("sels", [PK, 4, P])
        X = sb("X", [P, NT, P])
        T = sb("T", [P, NT, P])
        AG = sb("AG", [P, NT, P])
        Y = sb("Y", [P, NT, P])
        PT = sb("PT", [P, NP])
        XT = sb("XT", [P, NP])
        AUG = sb("AUG", [P, NP])
        W = sb("W", [P, 11, P])
        WRAW = sb("WRAW", [P, 2, P])
        EWR = sb("EWR", [P, 5, EK])
        WEDGE = sb("WEDGE", [EK + 1, 5, P])
        bias = sb("bias", [1, 10, P])
        rows = sb("rows", [P, 5, P])
        bn = sb("bn", [P, 4, P])
        src_i = sb("src_i", [P, ET], I32)
        dst_i = sb("dst_i", [P, ET], I32)
        part_i = sb("part_i", [P, ET], I32)
        dst_f = sb("dst_f", [P, ET])
        low = sb("low", [P, ET], BF16)
        high = sb("high", [P, ET], BF16)
        weight = sb("weight", [P, ET])
        attr = sb("attr", [P, ET, EK])
        deg = sb("deg", [P, 6, NT])
        hot_low = sb("hot_low", [P, 2, P], BF16)
        hot_high = sb("hot_high", [P, 2, 32], BF16)
        iota_b = sb("iota_b", [P, P], BF16)
        src_col = sb("src_col", [P, 1], I32)
        pay_col = sb("pay_col", [P, PK])
        diag = sb("diag", [P, P])
        same = sb("same", [P, P])
        before = sb("before", [P, P])
        n_before = sb("n_before", [P, 1])
        to_dump = sb("to_dump", [P, 1])
        row_f = sb("row_f", [P, 1])
        row_col = sb("row_col", [P, 1], I32)
        pay_t = sb("pay_t", [PK, P])
        gathered = sb("gathered", [P, P])
        msg = sb("msg", [P, P])
        joined = sb("joined", [P, P])
        zeros = sb("zeros", [P, P])
        stats = sb("stats", [P, NT, 6])
        mv = sb("mv", [P, NT, 2])
        sd = sb("sd", [P, 2, NT])
        roots = sb("roots", [P, 256])

        z = ctx.enter_context(nc.psum_tensor("z", [P, 2, 2 * 512], F32))
        ps_hist = ctx.enter_context(nc.psum_tensor("ps_hist", [P, 512], F32))
        ps_row = ctx.enter_context(nc.psum_tensor("ps_row", [P, 512], F32))
        ps_mul = ctx.enter_context(nc.psum_tensor("ps_mul", [P, 512], F32))
        ps_sum = ctx.enter_context(nc.psum_tensor("ps_sum", [P, 512], F32))

        table = nc.dram_tensor("table", [NP, P], F32).ap()
        sums = nc.dram_tensor("sums", [NP + P, P], F32).ap()

        loaded = sem("loaded")
        x_loaded = sem("x_loaded")
        dve_done = sem("dve_done")
        act_done = sem("act_done")
        z_ready = sem("z_ready")
        z_free_act = sem("z_free_act")
        z_free_dve = sem("z_free_dve")
        hot_ready = sem("hot_ready")
        hot_used = sem("hot_used")
        pe_row = sem("pe_row")
        pe_pay = sem("pe_pay")
        pe_mul = sem("pe_mul")
        pe_sum = sem("pe_sum")
        cols_ready = sem("cols_ready")
        pay_ready = sem("pay_ready")
        same_ready = sem("same_ready")
        msg_ready = sem("msg_ready")
        joined_ready = sem("joined_ready")
        stored = sem("stored")
        roots_asked = sem("roots_asked")
        counted = sem("counted")
        tile_through = sem("tile_through")
        pool_turn = sem("pool_turn")
        roots_done = sem("roots_done")
        sd_asked = sem("sd_asked")
        sd_root = sem("sd_root")

        order = steps()
        n_sums = sum(s[0] == "sum" for s in order)
        gather_done = [sem(f"gather_done{i}") for i in range(n_sums)]
        scatter_done = [sem(f"scatter_done{i}") for i in range(n_sums)]
        table_done = sem("table_done")
        zeroed = sem("zeroed")
        summed = sem("summed")
        t_ready = sem("t_ready")
        ag_ready = sem("ag_ready")
        x_ready = sem("x_ready")

        fills = ["dve"] * 2
        for s in order:
            if s[0] == "turn":
                fills += ["act"] * NG
            elif s[0] == "dense":
                fills += (["dve"] if s[1] in LN_STAGES else ["act"]) * NG

        def free_count(k):
            return sum(f == fills[k] for f in fills[:k + 1])

        z_free = {"act": z_free_act, "dve": z_free_dve}

        def tile(k, i):
            return z[:, k % 2, i * P:(i + 1) * P]

        def region(k):
            return z[:, k % 2, 0:GT * P]

        ag_turned = []
        kk = 2
        for s in order:
            if s[0] == "turn":
                kk += NG
                if s[1] == "AG":
                    ag_turned.append(free_count(kk - 1))
            elif s[0] == "dense":
                kk += NG

        block = ctx.enter_context(nc.Block())
        N_LOADS = []

        @block.sync
        def _(sp):
            def load(dst, src, s=loaded):
                sp.dma_start(dst, src).then_inc(s, 16)
                if s is loaded:
                    N_LOADS.append(1)
            load(const[:, :], a["c_mat"])
            load(sels[:, 0:3, :], a["c_sel"])
            for i, n in enumerate(("L0_gnn_W_enc", "L0_gnn_W1", "L0_gnn_W2")):
                load(W[:, i, :], a[n])
            load(W[:, 4:9, :], a["L2_gnn_weights"].rearrange("l a b -> a l b"))
            load(W[:, 9, :], a["L3_gnn_W"])
            load(WRAW[:, 0, :], a["L1_gnn_W_neigh"])
            load(WRAW[:, 1, :], a["L1_gnn_W_self"])
            load(EWR[:, :, :], a["L2_gnn_edge_ws"].rearrange("l d e -> d l e"))
            load(WEDGE[EK:EK + 1, :, :], a["L2_gnn_edge_bs"].rearrange("(o l) d -> o l d", o=1))
            for i, n in ((0, "L0_gnn_b_enc"), (1, "L0_gnn_b1"), (2, "L0_gnn_b2"), (3, "L1_gnn_b_self")):
                load(bias[:, i, :], a[n].rearrange("(o d) -> o d", o=1))
            load(bias[:, 4:9, :], a["L2_gnn_biases"].rearrange("(o l) d -> o l d", o=1))
            for i, n in enumerate(("L0_gnn_bn_gamma", "L0_gnn_bn_beta", "L0_gnn_bn_mean", "L0_gnn_bn_var", "L3_gnn_b")):
                load(rows[:, i, :], a[n].rearrange("(o d) -> o d", o=1).broadcast_to([P, P]))
            sp.wait_ge(dve_done, 8)
            load(X[:, 0:NT - 1, :], a["x"][0:(NT - 1) * P, :].rearrange("(j p) f -> p j f", p=P))
            load(X[0:NLAST, NT - 1, :], a["x"][(NT - 1) * P:N, :])
            load(sels[0:EK, PROD, :], a["L3_gnn_edge_w"])
            for dst, name in ((src_i, "src"), (dst_i, "dst"), (weight, "edge_weight")):
                load(dst[:, 0:EC], a[name][0:P * EC].rearrange("(p t) -> p t", t=EC))
                load(dst[0:ELAST, EC:ET], a[name][P * EC:E].rearrange("(p o) -> p o", o=1))
            attr_d = a["edge_attr_16"]
            load(attr[:, 0:EC, :], attr_d[0:P * EC, :].rearrange("(p t) k -> p t k", t=EC))
            load(attr[0:ELAST, EC, :], attr_d[P * EC:E, :])
            k = 0
            for s in order:
                if s[0] == "sum":
                    sp.wait_ge(t_ready, k + 1)
                    if k:
                        sp.wait_ge(summed, 16 * k)
                    sp.dma_start(table.rearrange("(j p) f -> p j f", p=P), T[:, :, :]).then_inc(table_done, 16)
                    sp.dma_start(sums.rearrange("(j p) f -> p j f", p=P),
                                 zeros[:, :].unsqueeze(1).broadcast_to([P, NT + 1, P])).then_inc(zeroed, 16)
                    sp.wait_ge(scatter_done[k], 16 * ET)
                    if k:
                        sp.wait_ge(ag_ready, k)
                        sp.wait_ge(z_free_act, ag_turned[k - 1])
                    sp.dma_start(AG[:, :, :], sums[0:NP, :].rearrange("(j p) f -> p j f", p=P)).then_inc(summed, 16)
                    k += 1
            sp.wait_ge(x_ready, 4)
            sp.dma_start(out[0:(NT - 1) * P, :].rearrange("(j p) f -> p j f", p=P),
                         AG[:, 0:NT - 1, :]).then_inc(stored, 16)
            sp.dma_start(out[(NT - 1) * P:N, :], AG[0:NLAST, NT - 1, :]).then_inc(stored, 16)
            sp.wait_ge(stored, 32)

        @block.gpsimd
        def _(pool):
            pool.sem_inc(tile_through, 1)
            k = 0
            for s in order:
                if s[0] != "sum":
                    continue
                with pool.Fori(0, ET) as t:
                    pool.wait_ge(cols_ready, t + (k * ET + 1))
                    pool.sem_inc(pool_turn, 1)
                    pool.wait_ge(table_done, 16 * (k + 1))
                    pool.indirect_dma_start(
                        out=gathered[:, :], out_offset=None, in_=table[:, :],
                        in_offset=bass.IndirectOffsetOnAxis(ap=src_col[:, 0:1], axis=0)).then_inc(gather_done[k], 16)
                    pool.wait_ge(joined_ready, t + (k * ET + 1))
                    pool.sem_inc(pool_turn, 1)
                    pool.wait_ge(zeroed, 16 * (k + 1))
                    pool.indirect_dma_start(
                        out=sums[:, :], out_offset=bass.IndirectOffsetOnAxis(ap=row_col[:, 0:1], axis=0),
                        in_=joined[:, :], in_offset=None, compute_op=ALU.add).then_inc(scatter_done[k], 16)
                    pool.wait_ge(scatter_done[k], t * 16 + 16)
                    pool.sem_inc(tile_through, 1)
                k += 1

        TD = 12

        @block.vector
        def _(v):
            n = [0]

            def link(ins, wait=True):
                n[0] += 1
                ins.then_inc(dve_done, 1)
                if wait:
                    v.wait_ge(dve_done, n[0])

            link(v.memset(X[:, NT - 1, :], 0.0), False)
            link(v.memset(src_i[:, EC:ET], N), False)
            link(v.memset(sels[:, PROD, :], 0.0), False)
            link(v.memset(dst_i[:, EC:ET], N), False)
            link(v.memset(weight[:, EC:ET], 0.0), False)
            link(v.memset(attr[:, EC:ET, :], 0.0), False)
            link(v.memset(zeros[:, :], 0.0), False)
            link(v.memset(pay_col[:, EK + 1:PK], 1.0))
            v.wait_ge(loaded, 16 * len(N_LOADS))
            link(v.tensor_copy(iota_b[:, :], iota))
            link(v.tensor_copy(dst_f[:, :], dst_i[:, :]))

            def histogram(which, slot, base):
                link(v.tensor_scalar(part_i[:, :], which[:, :], P - 1, None, ALU.bitwise_and))
                link(v.tensor_copy(low[:, :], part_i[:, :]))
                link(v.tensor_scalar(part_i[:, :], which[:, :], 7, None, ALU.logical_shift_right))
                link(v.tensor_copy(high[:, :], part_i[:, :]))
                with v.Fori(0, ET // 2) as t2:
                    for b in range(2):
                        t = t2 * 2 + b
                        v.wait_ge(hot_used, t + (base + 1))
                        v.tensor_tensor(hot_low[:, b, :], iota_b[:, :],
                                        low[:, bass.ds(t, 1)].broadcast_to([P, P]), ALU.is_equal)
                        v.tensor_tensor(hot_high[:, b, 0:NT], iota_b[:, 0:NT],
                                        high[:, bass.ds(t, 1)].broadcast_to([P, NT]), ALU.is_equal).then_inc(hot_ready, 1)
                v.wait_ge(hot_used, base + ET + 2)
                link(v.tensor_copy(deg[:, slot, :], ps_hist[:, 0:NT]))
                v.sem_inc(counted, 1)
            histogram(dst_i, 0, 0)
            histogram(src_i, 1, ET)
            link(v.tensor_scalar(deg[:, 5, :], deg[:, 0, :], 1.0, None, ALU.max))
            link(v.reciprocal(deg[:, 4, :], deg[:, 5, :]))
            link(v.tensor_scalar(deg[:, 2:4, :], deg[:, 0:2, :], 1.0, None, ALU.add))
            link(v.tensor_scalar(bn[:, 0, :], rows[:, 3, :], EPS, None, ALU.add), False)
            v.wait_ge(dve_done, n[0])
            v.sem_inc(roots_asked, 1)
            v.wait_ge(roots_done, 2)
            link(v.reciprocal(deg[:, 2:4, :], roots[:, 0:2 * NT].rearrange("p (a b) -> p a b", a=2)))
            link(v.reciprocal(bn[:, 1, :], roots[:, 64:64 + P]))
            link(v.tensor_tensor(bn[:, 2, :], bn[:, 1, :], rows[:, 0, :], ALU.mult))
            link(v.tensor_tensor(bn[:, 3, :], bn[:, 2, :], rows[:, 2, :], ALU.mult))
            link(v.tensor_tensor(bn[:, 3, :], rows[:, 1, :], bn[:, 3, :], ALU.subtract))
            v.wait_ge(z_ready, 1)
            link(v.tensor_copy(W[:, 3, :], z[:, 0, 0:P]))
            link(v.tensor_copy(W[:, 10, :], z[:, 0, P:2 * P]))
            v.sem_inc(z_free_dve, 1)
            v.wait_ge(z_ready, 2)
            link(v.tensor_copy(WEDGE[0:EK, :, :], z[0:EK, 1, 0:5 * P].rearrange("p (l d) -> p l d", l=5)))
            v.sem_inc(z_free_dve, 1)

            def scale_of(name):
                return {"dis": 2, "dis2": 3, "inv": 4}[name]

            def each_node(kind):
                return deg[:, scale_of(kind), :].unsqueeze(2).broadcast_to([P, NT, P])

            def norm(k0, out):
                for g in range(NG):
                    v.wait_ge(z_ready, k0 + g + 1)
                    sl = slice(g * GT, (g + 1) * GT)
                    link(v.tensor_tensor(Y[:, sl, :], region(k0 + g).rearrange("p (t f) -> p t f", t=GT),
                                         X[:, sl, :], ALU.add))
                    v.sem_inc(z_free_dve, 1)
                norm_rows(out)

            def norm_rows(out):
                for j in range(NT):
                    v.bn_stats(stats[:, j, :], Y[:, j, :]).then_inc(dve_done, 1)
                n[0] += NT
                v.wait_ge(dve_done, n[0])
                for j in range(NT):
                    v.bn_aggr(mv[:, j, :], stats[:, j, :]).then_inc(dve_done, 1)
                n[0] += NT
                v.wait_ge(dve_done, n[0])
                link(v.tensor_scalar(sd[:, 0, :], mv[:, :, 1], EPS, None, ALU.add))
                v.sem_inc(sd_asked, 1)
                norms[0] += 1
                v.wait_ge(sd_root, norms[0])
                link(v.reciprocal(sd[:, 0, :], sd[:, 1, :]))
                for j in range(NT):
                    v.tensor_scalar(out[:, j, :], Y[:, j, :], mv[:, j, 0:1], sd[:, 0, j:j + 1],
                                    ALU.subtract, ALU.mult).then_inc(dve_done, 1)
                n[0] += NT
                v.wait_ge(dve_done, n[0])
                v.sem_inc(x_ready, 1)

            norms = [0]
            k, z_k = 0, 2
            for s in order:
                if s[0] == "turn":
                    z_k += NG
                elif s[0] == "dense":
                    if s[1] in LN_STAGES:
                        if k:
                            v.wait_ge(table_done, 16 * k)
                        norm(z_k, X)
                        if s[1] == 2:
                            link(v.tensor_copy(T[:, :, :], X[:, :, :]))
                            v.sem_inc(t_ready, 1)
                        elif s[1] == 3:
                            link(v.tensor_tensor(T[:, :, :], X[:, :, :], each_node("dis2"), ALU.mult))
                            v.sem_inc(t_ready, 1)
                    else:
                        v.wait_ge(z_free_act, free_count(z_k + NG - 1))
                        if s[1] == 0:
                            link(v.tensor_tensor(T[:, :, :], T[:, :, :], bn[:, 2:3, :].broadcast_to([P, NT, P]), ALU.mult))
                            link(v.tensor_tensor(T[:, :, :], T[:, :, :], bn[:, 3:4, :].broadcast_to([P, NT, P]), ALU.add))
                            link(v.tensor_tensor(T[:, :, :], T[:, :, :], each_node("dis"), ALU.mult))
                        v.sem_inc(t_ready, 1)
                    z_k += NG
                elif s[0] == "sum":
                    kind = s[1]
                    if kind == ATTR:
                        v.wait_ge(table_done, 16 * k)
                        link(v.tensor_copy(Y[:, :, :], each_node("dis2")))
                        link(v.tensor_copy(T[:, :, :], Y[:, :, :]))
                        v.sem_inc(t_ready, 1)
                    base = n[0]
                    first = k * ET
                    with v.Fori(0, ET) as t:
                        def done(i):
                            v.wait_ge(dve_done, t * TD + (base + i))
                        v.wait_ge(tile_through, t + (first + 1))
                        v.tensor_copy(src_col[:, :], src_i[:, bass.ds(t, 1)]).then_inc(dve_done, 1)
                        v.tensor_copy(row_f[:, :], dst_f[:, bass.ds(t, 1)]).then_inc(dve_done, 1)
                        v.tensor_copy(pay_col[:, 0:EK], attr[:, bass.ds(t, 1), :].rearrange("p o k -> p (o k)")).then_inc(dve_done, 1)
                        v.tensor_copy(pay_col[:, EK:EK + 1], weight[:, bass.ds(t, 1)]).then_inc(dve_done, 1)
                        done(4)
                        v.tensor_scalar(diag[:, :], ident, row_f[:, 0:1], None, ALU.mult).then_inc(dve_done, 1)
                        done(5)
                        v.sem_inc(cols_ready, 1)
                        v.wait_ge(pe_row, t + (first + 1))
                        v.tensor_scalar(same[:, :], ps_row[:, 0:P], row_f[:, 0:1], None, ALU.is_equal).then_inc(dve_done, 1)
                        done(6)
                        v.tensor_tensor_reduce(before[:, :], same[:, :], tril, 1.0, 0.0, ALU.mult, ALU.add,
                                               n_before[:, :]).then_inc(dve_done, 1)
                        v.wait_ge(pe_pay, t + (first + 1))
                        v.tensor_copy(pay_t[:, :], ps_mul[0:PK, 256:256 + P]).then_inc(pay_ready, 1)
                        done(7)
                        v.tensor_scalar(n_before[:, :], n_before[:, :], 1.0, None, ALU.min).then_inc(dve_done, 1)
                        v.tensor_tensor(to_dump[:, :], dump_row, row_f[:, :], ALU.subtract).then_inc(dve_done, 1)
                        done(9)
                        v.tensor_tensor(to_dump[:, :], to_dump[:, :], n_before[:, :], ALU.mult).then_inc(dve_done, 1)
                        done(10)
                        v.tensor_tensor(row_col[:, :], to_dump[:, :], row_f[:, :], ALU.add).then_inc(dve_done, 1)
                        v.wait_ge(gather_done[k], t * 16 + 16)
                        v.wait_ge(pe_mul, t + (first + 1))
                        v.tensor_tensor(msg[:, :], gathered[:, :], ps_mul[:, 0:P], ALU.mult).then_inc(msg_ready, 1)
                        v.wait_ge(pe_sum, t + (first + 1))
                        v.tensor_copy(joined[:, :], ps_sum[:, 0:P]).then_inc(dve_done, 1)
                        done(12)
                        v.sem_inc(joined_ready, 1)
                    n[0] += TD * ET
                    k += 1
                    v.wait_ge(summed, 16 * k)
                    if kind == PROD:
                        continue
                    if kind == ATTR:
                        link(v.tensor_tensor(AG[:, :, EK:EK + 1], AG[:, :, EK:EK + 1], T[:, :, 0:1], ALU.add))
                    elif s[3]:
                        link(v.tensor_tensor(AG[:, :, :], AG[:, :, :], T[:, :, :], ALU.add))
                    link(v.tensor_tensor(AG[:, :, :], AG[:, :, :], each_node(s[2]), ALU.mult))
                    v.sem_inc(ag_ready, 1)
                elif s[0] == "final":
                    link(v.tensor_tensor(AG[:, :, :], AG[:, :, :], rows[:, 4:5, :].broadcast_to([P, NT, P]), ALU.add))
                    link(v.tensor_tensor(Y[:, :, :], AG[:, :, :], X[:, :, :], ALU.add))
                    norm_rows(AG)

        @block.scalar
        def _(act):
            act.wait_ge(roots_asked, 1)
            act.activation(roots[:, 0:2 * NT], deg[:, 2:4, :].rearrange("p a b -> p (a b)"), ACT.Sqrt).then_inc(roots_done, 1)
            act.activation(roots[:, 64:64 + P], bn[:, 0, :], ACT.Sqrt).then_inc(roots_done, 1)
            z_k, k, norms = 2, 0, 0
            for s in order:
                if s[0] == "turn":
                    to = {"PT": PT, "XT": XT, "AUG": AUG}[s[2]]
                    for g in range(NG):
                        act.wait_ge(z_ready, z_k + g + 1)
                        act.copy(to[:, g * GT * P:(g + 1) * GT * P], region(z_k + g)).then_inc(z_free_act, 1)
                    z_k += NG
                elif s[0] == "dense":
                    st = s[1]
                    if st in LN_STAGES:
                        norms += 1
                        act.wait_ge(sd_asked, norms)
                        act.activation(sd[:, 1, :], sd[:, 0, :], ACT.Sqrt).then_inc(sd_root, 1)
                    else:
                        if k:
                            act.wait_ge(table_done, 16 * k)
                            act.wait_ge(ag_ready, k)
                        for g in range(NG):
                            act.wait_ge(z_ready, z_k + g + 1)
                            for i in range(GT):
                                j = g * GT + i
                                scale = 1.0 if st in (0, 9) else deg[:, 2 if st < 3 else 3, j:j + 1]
                                ins = act.activation(T[:, j, :], tile(z_k + g, i), ACT.Copy if st == 9 else ACT.Relu, scale=scale)
                            ins.then_inc(z_free_act, 1)
                    z_k += NG
                elif s[0] == "sum":
                    k += 1
                elif s[0] == "final":
                    norms += 1
                    act.wait_ge(sd_asked, norms)
                    act.activation(sd[:, 1, :], sd[:, 0, :], ACT.Sqrt).then_inc(sd_root, 1)

        @block.tensor
        def _(pe):
            pe.sem_inc(hot_used, 2)
            pe.wait_ge(loaded, 16 * len(N_LOADS))
            for h in range(2):
                pe.matmul(ps_hist[:, 0:NT], zeros[:, :], zeros[:, 0:NT], start=True, stop=False, skip_group_check=True)
                with pe.Fori(0, ET // 2) as t2:
                    for b in range(2):
                        t = t2 * 2 + b
                        pe.wait_ge(hot_ready, t + (h * ET + 1))
                        pe.matmul(ps_hist[:, 0:NT], hot_low[:, b, :], hot_high[:, b, 0:NT], start=False, stop=False,
                                  skip_group_check=True).then_inc(hot_used, 1)
                if h == 0:
                    pe.wait_ge(counted, 1)
            pe.transpose(z[:, 0, 0:P], WRAW[:, 0, :], ident)
            pe.transpose(z[:, 0, P:2 * P], WRAW[:, 1, :], ident).then_inc(z_ready, 1)
            for i in range(5):
                ins = pe.transpose(z[0:EK, 1, i * P:(i + 1) * P], EWR[:, i, :], ident)
            ins.then_inc(z_ready, 1)
            z_k, k, x_n = 2, 0, 0
            ag_k = 0
            last_pt = last_xt = last_aug = 0
            for s in order:
                if s[0] == "turn":
                    src = {"X": X, "AG": AG}[s[1]]
                    if s[1] == "AG":
                        ag_k += 1
                        pe.wait_ge(ag_ready, ag_k)
                    elif x_n:
                        pe.wait_ge(x_ready, x_n)
                    for g in range(NG):
                        pe.wait_ge(z_free[fills[z_k + g - 2]], free_count(z_k + g - 2))
                        for i in range(GT):
                            ins = pe.transpose(tile(z_k + g, i), src[:, g * GT + i, :], ident)
                        ins.then_inc(z_ready, 1)
                    z_k += NG
                    turned = free_count(z_k - 1)
                elif s[0] == "dense":
                    st = s[1]
                    pe.wait_ge(z_free_act, turned)
                    if st in LN_STAGES:
                        x_n += 1
                    for g in range(NG):
                        pe.wait_ge(z_free[fills[z_k + g - 2]], free_count(z_k + g - 2))
                        for i in range(GT):
                            c = slice((g * GT + i) * P, (g * GT + i + 1) * P)
                            to = tile(z_k + g, i)
                            ins = pe.matmul(to, PT[:, c], W[:, st, :], start=True, stop=(st == 9))
                            if st == 3:
                                pe.matmul(to, XT[:, c], W[:, 10, :], start=False, stop=False)
                            if st >= 4 and st < 9:
                                pe.matmul(to, AUG[0:EK + 1, c], WEDGE[:, st - 4, :], start=False, stop=False)
                            if st < 9:
                                ins = pe.matmul(to, ones[0:1, :], bias[0:1, st, :], start=False, stop=True)
                        ins.then_inc(z_ready, 1)
                    z_k += NG
                elif s[0] == "sum":
                    first = k * ET
                    with pe.Fori(0, ET) as t:
                        pe.wait_ge(cols_ready, t + (first + 1))
                        pe.matmul(ps_row[:, 0:P], ones, diag[:, :], start=True, stop=True).then_inc(pe_row, 1)
                        pe.transpose(ps_mul[0:PK, 256:256 + P], pay_col[:, :], ident).then_inc(pe_pay, 1)
                        pe.wait_ge(pay_ready, t + (first + 1))
                        pe.matmul(ps_mul[:, 0:P], pay_t[:, :], sels[:, s[1], :], start=True, stop=True).then_inc(pe_mul, 1)
                        pe.wait_ge(msg_ready, t + (first + 1))
                        pe.matmul(ps_sum[:, 0:P], same[:, :], msg[:, :], start=True, stop=True).then_inc(pe_sum, 1)
                    k += 1


_OUT = "out_0_dram"


def kernel(**inputs):
    import concourse.bacc as bacc
    from concourse.bass_utils import run_bass_kernel_spmd

    nc = bacc.Bacc("TRN2", target_bir_lowering=False, num_devices=1)
    c_mat, c_sel = host_constants()
    arrays, args = {}, {}
    for name, a in {**inputs, "c_mat": c_mat, "c_sel": c_sel}.items():
        a = np.ascontiguousarray(a)
        arrays[f"in_{name}_dram"] = a
        args[name] = nc.dram_tensor(f"in_{name}_dram", a.shape, mybir.dt.from_np(a.dtype), kind="ExternalInput").ap()
    out = nc.dram_tensor(_OUT, (N, P), F32, kind="ExternalOutput").ap()
    build(nc, args, out)
    return run_bass_kernel_spmd(nc, [arrays], core_ids=[0]).results[0][_OUT]
```

```python
from contextlib import ExitStack

import concourse.bass as bass
from concourse import mybir
import numpy as np

F32 = mybir.dt.float32
BF16 = mybir.dt.bfloat16
FP8 = mybir.dt.float8e4
I32 = mybir.dt.int32
ALU = mybir.AluOpType
ACT = mybir.ActivationFunctionType
AX = mybir.AxisListType

P = 128
N = 3125
NT = -(-N // P)
NP = NT * P
NLAST = N - (NT - 1) * P
E = 103125
EC = E // P
ET = EC + 1
ELAST = E - P * EC
EK = 16
EPS = 1e-5

SLOTS = 64
ROWS = E // SLOTS + 2
PAIRS = (NT + 1) // 2
NPX = 2 * PAIRS * P
COLS = PAIRS * P
CB = 8
CG = 16
U = 8
NU = -(-ET // U)
WIN = 48
UB = 15
USTEP = 31
WOFF = 22
HB = 13
CH = 4
CHUNKS = [(c, min(CH, NT - c)) for c in range(0, NT, CH)]
SG = 5
NSG = NT // SG


PK = EK + 2
GT = 5
NG = NT // GT
DUMP = NP

LN_STAGES = (2, 3, 8)
NONE, WEIGHT, ATTR, PROD = range(4)


def window_step(k):
    return int(round(k * P * USTEP / (U * P)))


def host_fast():
    c = np.zeros((P, 4 * P), np.float32)
    c[:, 0:P] = np.eye(P)
    c[:, P:2 * P] = 1.0
    c[:, 2 * P:3 * P] = np.arange(P)[None, :]
    c[:, 3 * P:4 * P] = np.triu(np.ones((P, P)), 1)
    base = np.zeros((1, NU * U), np.float32)
    for u in range(NU):
        for k in range(U):
            base[0, u * U + k] = USTEP * u + window_step(k) - WOFF
    return {"c_fast": c, "c_base": base}


def dense_items():
    out = []
    for st, who in (("enc", "act"), ("gcn1", "act"), ("gcn2", "dve"), ("self", "dve")):
        out += [(st, c, w, who) for c, w in CHUNKS]
    out += [("neigh", 2 * q, min(2, NT - 2 * q), "dve") for q in range(PAIRS)]
    for l in range(5):
        out += [(f"edge{l}", c, w, "act" if l < 4 else "dve") for c, w in CHUNKS]
    out += [("last", c, w, "act") for c, w in CHUNKS]
    return out


def quick_program(nc, a, out, verdict, sems):
    with ExitStack() as ctx:
        def sb(name, shape, dt=F32):
            return ctx.enter_context(nc.sbuf_tensor("quick_" + name, shape, dt))

        def sem(name):
            return sems.enter_context(nc.semaphore("quick_" + name))

        const = sb("const", [P, 4 * P])
        ident, ones, iota, below = (const[:, i * P:(i + 1) * P] for i in range(4))
        A8 = sb("A8", [P, NT, NP], FP8)
        X = sb("X", [P, NT, P])
        T = sb("T", [P, NT, P])
        T3 = sb("T3", [P, NT, 3, P], BF16)
        PTc = sb("PTc", [P, 2, CH * P])
        W = sb("W", [P, 11, P])
        WEDGE = sb("WEDGE", [EK + 3, 5, P])
        big = sb("big", [P, 4 * NT * P])
        hot_low = sb("hot_low", [P, 2, CB * P], BF16)
        hot_high = sb("hot_high", [P, 2, 4, CB * NT], BF16)
        iota_b = sb("iota_b", [P, P], BF16)
        ident_b = sb("ident_b", [P, P], BF16)
        src_e = sb("src_e", [P, NU * U], I32)
        rel_e = sb("rel_e", [P, NU * U])
        dis_e = sb("dis_e", [P, NU * U])
        deg = sb("deg", [P, 10, NT])
        offs = sb("offs", [P, 8, NT])
        row_i = sb("row_i", [P, 3, NT], I32)
        stats = sb("stats", [P, NT, 6])
        mv = sb("mv", [P, NT, 2])
        sd = sb("sd", [P, 2, NT])
        flags = sb("flags", [P, 8 + NT])
        idx = sb("idx", [P, 3, U], I32)
        got = sb("got", [P, 3, U])
        zero_b = sb("zero_b", [1, 512], BF16)
        root = sb("root", [P, 2, NT])

        DEG_IN, DEG_OUT1, DIS, DIS2, INV, DISSQ, DIS2SQ, SQ, SQ2, IN1 = range(10)

        work = A8[:, :, :].rearrange("p j n -> p (j n)")[:, 0:16 * NT * P].bitcast(F32)
        RAW = work[:, 0:2 * NT * P].bitcast(I32).rearrange("p (j s) -> p j s", j=NT)
        RAWW = work[:, 0:2 * NT * P].rearrange("p (j s) -> p j s", j=NT)[:, :, 2 * SLOTS:4 * SLOTS]
        M1 = work[:, 2 * NT * P:3 * NT * P].rearrange("p (j s) -> p j s", j=NT)
        M2 = work[:, 3 * NT * P:4 * NT * P].rearrange("p (j s) -> p j s", j=NT)
        hist_low = big[:, 0:HB * P].bitcast(BF16).rearrange("p (b t l) -> p b t l", b=2, t=HB)
        hist_high = big[:, HB * P:HB * P + HB * NT].bitcast(BF16).rearrange("p (b t l) -> p b t l", b=2, t=HB)
        WRAW = big[:, 3800:4056].rearrange("p (b f) -> p b f", b=2)
        EWR = big[:, 4056:4136].rearrange("p (l k) -> p l k", l=5)
        rows = big[:, 4500:4500 + 4 * P].rearrange("p (r f) -> p r f", r=4)
        dst_p = big[:, 5100:5100 + ET].bitcast(I32)
        dst_n = big[:, 6000:6000 + ET].bitcast(I32)
        part_i = big[:, 6900:6900 + ET].bitcast(I32)
        part_f = big[:, 7800:7800 + ET].bitcast(BF16).rearrange("p (b t) -> p b t", b=2)
        pos_i = big[:, 2000:2000 + 14 * P].bitcast(I32).rearrange("p (a g c) -> p a g c", a=2, g=7)
        pos_f = T[:, 0:14, :].rearrange("p (a g) c -> p a g c", a=2)
        base_b = dis_e
        flat = T3[:, :, :, :].rearrange("p a b c -> p (a b c)")[:, 0:5 * 2 * PAIRS * SLOTS].rearrange(
            "p (k j s) -> p k j s", k=5, j=2 * PAIRS)
        wlists = T3[:, :, :, :].rearrange("p a b c -> p (a b c)")[:, 0:5 * COLS].rearrange("p (k m) -> p k m", k=5)
        lists = big[:, 0:5 * COLS // 2].bitcast(BF16).rearrange("p (k m) -> p k m", k=5)
        zero_i = big[0:3, 4200:4200 + 4 * SLOTS].bitcast(I32)
        bias = big[0:1, 11800:11800 + 4 * P].rearrange("p (r f) -> p r f", r=4)
        root_bn = big[:, 11284:11284 + 2 * P].rearrange("p (r f) -> p r f", r=2)
        bn = big[:, 10900:10900 + 3 * P].rearrange("p (r f) -> p r f", r=3)
        sq_row = big[0:1, 4500:4500 + NP]
        scratch = big[:, 7700:7700 + NP].bitcast(BF16).rearrange("p (b n) -> p b n", b=2)
        AW = big[:, :].rearrange("p (b j c) -> p b j c", b=4, j=NT)
        AUG = big[0:EK + 3, 0:NP]
        ea_u = big[:, NP:NP + 3 * P].rearrange("p (b t k) -> p b t k", b=3, t=U)
        eas = big[:, NP + 400:NP + 400 + 3 * 136].rearrange("p (b t k) -> p b t k", b=3, t=U)
        hot_d = big[:, NP + 900:NP + 900 + 3 * U * WIN].rearrange("p (b t w) -> p b t w", b=3, t=U)
        G = big[:, 2 * NP:2 * NP + 3 * U * P].rearrange("p (b t f) -> p b t f", b=3, t=U)
        EWB = big[:, 3 * NP:3 * NP + U * P].rearrange("p (t f) -> p t f", t=U)
        ea_t = big[:, 3 * NP + U * P:3 * NP + (U + 3) * P].rearrange("p (b c) -> p b c", b=3)
        b3_row = big[:, 3 * NP + 1500:3 * NP + 1500 + P]
        sum_t = T[:, :, :].rearrange("p j f -> p (j f)")

        ps = ctx.enter_context(nc.psum_tensor("quick_ps", [P, 8, 512], F32))
        psb = ps[:, :, :].rearrange("p b c -> p (b c)").bitcast(BF16).rearrange("p (b c) -> p b c", b=8)

        rows_d = nc.dram_tensor("quick_rows", [ROWS, 4 * SLOTS], I32).ap()
        dis_d = nc.dram_tensor("quick_dis", [NP, 1], F32).ap()
        roots_d = nc.dram_tensor("quick_roots", [3, NP], F32).ap()
        table_d = nc.dram_tensor("quick_table", [NP, P], F32).ap()
        wlist_d = nc.dram_tensor("quick_wlist", [P, 5, COLS], BF16).ap()

        S = {}

        class Sems:
            pass

        for name in ("loaded", "x_loaded", "filled", "dst_in", "pos_in", "dve_done", "act_done", "w_turned", "w_taken",
                     "hist_ready", "hist_used", "ptr_ready", "ptr_taken", "rows_ready", "pads_in", "table_in", "lists_in",
                     "flat_ready", "turn_ready", "turn_taken", "wl_out", "wl_in",
                     "hot_ready", "hot_used", "grp_ready", "grp_free", "adj_ready",
                     "p_ready", "pt_ready", "z_ready", "z_free_act", "z_free_dve",
                     "t_ready", "hi_ready", "r_ready", "mid_ready", "t3_ready", "root_asked", "root_done",
                     "pos_turned", "pos_taken", "sums_in", "sq_out", "sq_in", "dis_out", "row_in",
                     "got0", "got1", "got2", "dis_e_ready", "pos_done", "ptr_go", "max_free", "stats_in", "flag_go", "ea0", "ea1", "ea2", "ea_taken", "eas_ready", "unit_used",
                     "attr_done", "aug_ready", "aug_rows", "ewb_zero", "x_ready",
                     "g0", "g1", "g2", "et_ready", "et_in", "e_ready", "hotd_ready", "msg_ready", "gathered_used",
                     "banks_zero", "sum_done", "sum_taken", "out_ready", "stored", "flag_mm", "flag_ready", "scr", "high_ready", "pool_turn", "xw_out"):
            S[name] = sem(name)

        def c_(name):
            return S[name]

        items = dense_items()
        NI = len(items)
        first_item, item_count, place = {}, {}, []
        for k, it in enumerate(items):
            first_item.setdefault(it[0], k)
            place.append(item_count.get(it[0], 0))
            item_count[it[0]] = place[-1] + 1

        def z_taken(k):
            who = items[k][3]
            return S["z_free_" + who], sum(i[3] == who for i in items[:k + 1])

        def before(k):
            return max((i for i in range(k) if place[i] % 2 == place[k] % 2), default=None)

        STAGES = list(first_item)
        SPLITS = ["gcn1", "gcn2", "edge0", "edge1", "edge2", "edge3", "edge4"]
        SOURCE = {"gcn1": "enc", "gcn2": "gcn1", "edge0": "neigh", "edge1": "edge0", "edge2": "edge1",
                  "edge3": "edge2", "edge4": "edge3"}

        def p_bank(k):
            return ps[:, place[k] % 2, :]

        def z_bank(k):
            return ps[:, 2 + place[k] % 2, :]

        def tiles_done_act(st):
            return sum(item_count[s] for s in STAGES[:STAGES.index(st) + 1] if items[first_item[s]][3] == "act")

        LOADED = [0]
        block = ctx.enter_context(nc.Block())

        @block.sync
        def _(sp):
            def load(dst, src, s="loaded"):
                LOADED[0] += s == "loaded"
                return sp.dma_start(dst, src).then_inc(S[s], 16)

            sp.wait_ge(c_("filled"), 1)
            load(dst_p[:, 0:EC], a["dst"][0:P * EC].rearrange("(p t) -> p t", t=EC), "dst_in")
            load(dst_p[0:ELAST, EC:ET], a["dst"][P * EC:E].rearrange("(p o) -> p o", o=1), "dst_in")
            load(dst_n[:, 0:EC], a["dst"][1:P * EC + 1].rearrange("(p t) -> p t", t=EC), "dst_in")
            load(dst_n[0:ELAST - 1, EC:ET], a["dst"][P * EC + 1:E].rearrange("(p o) -> p o", o=1), "dst_in")
            load(const[:, :], a["c_fast"])
            load(X[:, 0:NT - 1, :], a["x"][0:(NT - 1) * P, :].rearrange("(j p) f -> p j f", p=P))
            load(X[0:NLAST, NT - 1, :], a["x"][(NT - 1) * P:N, :])
            for i, n in enumerate(("L0_gnn_W_enc", "L0_gnn_W1", "L0_gnn_W2")):
                load(W[:, i, :], a[n])
            load(W[:, 4:9, :], a["L2_gnn_weights"].rearrange("l a b -> a l b"))
            load(W[:, 9, :], a["L3_gnn_W"])
            load(WRAW[:, 0, :], a["L1_gnn_W_neigh"])
            load(WRAW[:, 1, :], a["L1_gnn_W_self"])
            load(EWR[:, :, :], a["L2_gnn_edge_ws"].rearrange("l d e -> d l e"))
            load(WEDGE[EK:EK + 1, :, :], a["L2_gnn_edge_bs"].rearrange("(o l) d -> o l d", o=1))
            load(WEDGE[EK + 1:EK + 2, :, :], a["L2_gnn_biases"].rearrange("(o l) d -> o l d", o=1))
            load(WEDGE[EK + 2:EK + 3, :, :], a["L2_gnn_edge_bs"].rearrange("(o l) d -> o l d", o=1))
            for i, n in enumerate(("L0_gnn_b_enc", "L0_gnn_b1", "L0_gnn_b2", "L1_gnn_b_self")):
                load(bias[:, i, :], a[n].rearrange("(o d) -> o d", o=1))
            for i, n in enumerate(("L0_gnn_bn_gamma", "L0_gnn_bn_beta", "L0_gnn_bn_mean", "L0_gnn_bn_var")):
                load(rows[:, i, :], a[n].rearrange("(o d) -> o d", o=1).broadcast_to([P, P]))
            load(base_b[:, :], a["c_base"].broadcast_to([P, NU * U]))
            n_full = E // SLOTS
            rest = E - n_full * SLOTS
            src_d = a["src"]
            w_d = a["edge_weight"].bitcast(I32)
            load(rows_d[n_full - 1:ROWS, :], zero_i[:, :], "pads_in")
            sp.wait_ge(c_("pads_in"), 16)
            for col, d in ((0, src_d), (2 * SLOTS, w_d)):
                load(rows_d[0:n_full, col:col + SLOTS], d[0:n_full * SLOTS].rearrange("(r s) -> r s", s=SLOTS), "table_in")
                load(rows_d[0:n_full - 1, col + SLOTS:col + 2 * SLOTS],
                     d[SLOTS:n_full * SLOTS].rearrange("(r s) -> r s", s=SLOTS), "table_in")
                tail = d[n_full * SLOTS:E].rearrange("(o s) -> o s", o=1)
                load(rows_d[n_full:n_full + 1, col:col + rest], tail, "table_in")
                load(rows_d[n_full - 1:n_full, col + SLOTS:col + SLOTS + rest], tail, "table_in")
            for k, n in ((0, "src"), (1, "dst")):
                for g in range(6):
                    load(pos_i[:, k, g, :], a[n][g * P * P:(g + 1) * P * P].rearrange("(t c) -> t c", c=P), "pos_in")
                rem = EC - 6 * P
                load(pos_i[0:rem, k, 6, :], a[n][6 * P * P:P * EC].rearrange("(t c) -> t c", c=P), "pos_in")
                load(pos_i[rem:rem + 1, k, 6, 0:ELAST], a[n][P * EC:E].rearrange("(o c) -> o c", o=1), "pos_in")
            sp.wait_ge(c_("sq_out"), 1)
            sp.dma_start(roots_d[0:1, :].rearrange("o (j p) -> p (o j)", p=P), deg[:, SQ, :], allow_slow_non_contiguous=True).then_inc(c_("sq_in"), 16)
            sp.wait_ge(c_("sq_in"), 16)
            sp.wait_ge(c_("turn_taken"), 10)
            sp.dma_start(sq_row, roots_d[0:1, :]).then_inc(c_("sq_in"), 16)
            sp.dma_start(wlist_d[:, :, :], lists[:, :, :]).then_inc(c_("wl_out"), 16)
            sp.wait_ge(c_("dis_out"), 1)
            sp.dma_start(dis_d.rearrange("(j p) o -> p (j o)", p=P), deg[:, DIS2, :], allow_slow_non_contiguous=True).then_inc(c_("row_in"), 16)
            sp.dma_start(roots_d[1:2, :].rearrange("o (j p) -> p (o j)", p=P), deg[:, SQ2, :], allow_slow_non_contiguous=True).then_inc(c_("row_in"), 16)
            sp.dma_start(roots_d[2:3, :].rearrange("o (j p) -> p (o j)", p=P), deg[:, DIS2, :], allow_slow_non_contiguous=True).then_inc(c_("row_in"), 16)
            sp.wait_ge(c_("p_ready"), first_item["gcn2"] + item_count["gcn2"])
            sp.wait_ge(c_("wl_out"), 16)
            sp.dma_start(wlists[:, :, :], wlist_d[:, :, :]).then_inc(c_("wl_in"), 16)
            sp.wait_ge(c_("p_ready"), first_item["neigh"] + item_count["neigh"])
            sp.wait_ge(c_("row_in"), 48)
            sp.dma_start(AUG[EK + 1:EK + 3, :], roots_d[1:3, :]).then_inc(c_("aug_rows"), 16)
            sp.dma_start(b3_row, a["L3_gnn_b"].rearrange("(o d) -> o d", o=1).broadcast_to([P, P])).then_inc(c_("aug_rows"), 16)

            ea_d = a["edge_attr_16"]

            def unit(u, r, taken):
                sp.wait_ge(c_("ea_taken"), taken)
                sp.dma_start(ea_u[:, r, :, :], ea_d[bass.ds(u * (U * P), U * P), :].rearrange(
                    "(t p) k -> p t k", p=P)).then_inc(S[f"ea{r}"], 16)

            def all_units(base):
                with sp.Fori(0, NU // 3) as i:
                    for r in range(3):
                        unit(i * 3 + r, r, i * 3 + (r + 1 + base))
                unit(NU - 2, 0, NU - 2 + 1 + base)
                sp.wait_ge(c_("ea_taken"), NU + base)
                full = EC - (NU - 1) * U
                sp.dma_start(ea_u[:, 1, 0:full, :], ea_d[(NU - 1) * U * P:P * EC, :].rearrange(
                    "(t p) k -> p t k", p=P)).then_inc(S["ea1"], 16)
                sp.dma_start(ea_u[0:ELAST, 1, full, :], ea_d[P * EC:E, :]).then_inc(S["ea1"], 16)

            all_units(0)
            sp.wait_ge(c_("ewb_zero"), 1)
            for t in range(U):
                sp.dma_start(EWB[t * EK:(t + 1) * EK, t, :], a["L3_gnn_edge_w"]).then_inc(c_("ewb_zero"), 16)
            sp.wait_ge(c_("z_free_act"), tiles_done_act("last"))
            sp.dma_start(table_d.rearrange("(j p) f -> p j f", p=P), T[:, :, :]).then_inc(c_("xw_out"), 16)
            sp.wait_ge(c_("ea_taken"), NU + 3)
            all_units(NU)
            sp.wait_ge(c_("out_ready"), 1)
            sp.dma_start(out[0:(NT - 1) * P, :].rearrange("(j p) f -> p j f", p=P),
                         X[:, 0:NT - 1, :]).then_inc(c_("stored"), 16)
            sp.dma_start(out[(NT - 1) * P:N, :], X[0:NLAST, NT - 1, :]).then_inc(c_("stored"), 16)
            sp.wait_ge(c_("stored"), 32)

        def wide(ap, n):
            return ap.unsqueeze(2).broadcast_to([ap.shape[0], ap.shape[1], n])

        def windows():
            step = USTEP * UB
            copies, adds = [], []
            for b in range(-(-NU // UB)):
                lo = WOFF + WOFF if b else WOFF
                hi = min(step + 2 * WOFF, NP - (step * b - WOFF))
                copies.append((b, lo, hi, step * b - WOFF + lo))
                if b:
                    adds.append((b, 0, 2 * WOFF, step * b - WOFF))
            return copies, adds

        @block.gpsimd
        def _(pool):
            turns = [0]

            def fetch(k, r, u, out_of, table, sem_name):
                pool.tensor_copy(idx[:, r, :], src_e[:, bass.ds(u * U, U)]).then_inc(c_("pool_turn"), 1)
                pool.wait_ge(c_("pool_turn"), k)
                pool.sem_inc(c_("scr"), 1)
                for t in range(U):
                    pool.indirect_dma_start(out=out_of(r, t), out_offset=None, in_=table[:, :],
                                            in_offset=bass.IndirectOffsetOnAxis(ap=idx[:, r, t:t + 1], axis=0)
                                            ).then_inc(S[sem_name + str(r)], 16)

            pool.wait_ge(c_("rows_ready"), 1)
            pool.wait_ge(c_("table_in"), 8 * 16)
            for j in range(NT):
                pool.indirect_dma_start(out=RAW[:, j, :], out_offset=None, in_=rows_d[:, :],
                                        in_offset=bass.IndirectOffsetOnAxis(ap=row_i[:, 1, j:j + 1], axis=0)
                                        ).then_inc(c_("lists_in"), 16)
            pool.wait_ge(c_("row_in"), 48)
            pool.wait_ge(c_("pos_done"), 1)

            def keep(r, u, n):
                pool.wait_ge(S[f"got{r}"], n)
                pool.tensor_copy(dis_e[:, bass.ds(u * U, U)], got[:, r, :]).then_inc(c_("dis_e_ready"), 1)

            fetch(1, 0, 0, lambda r, t: got[:, r, t:t + 1], dis_d, "got")
            with pool.Fori(0, NU // 3) as i:
                for d in (1, 2, 3):
                    u = i * 3 + d
                    fetch(i * 3 + (d + 1), d % 3, u, lambda r, t: got[:, r, t:t + 1], dis_d, "got")
                    keep((d - 1) % 3, i * 3 + (d - 1), i * (16 * U) + 16 * U)
            fetch(NU, (NU - 1) % 3, NU - 1, lambda r, t: got[:, r, t:t + 1], dis_d, "got")
            keep((NU - 2) % 3, NU - 2, 16 * U * ((NU - 2) // 3 + 1))
            keep((NU - 1) % 3, NU - 1, 16 * U * ((NU - 1) // 3 + 1))
            pool.wait_ge(c_("xw_out"), 16)

            def rows_of(u, r, k):
                pool.wait_ge(c_("gathered_used"), k)
                pool.sem_inc(c_("scr"), 1)
                fetch(k + NU, r, u, lambda r, t: G[:, r, t, :], table_d, "g")

            with pool.Fori(0, NU // 3) as i:
                for r in range(3):
                    rows_of(i * 3 + r, r, i * 3 + (r + 1))
            rows_of(NU - 2, 0, NU - 1)
            rows_of(NU - 1, 1, NU)

        @block.vector
        def _(v):
            n = [0]

            def link(ins, wait=True):
                n[0] += 1
                ins.then_inc(c_("dve_done"), 1)
                if wait:
                    v.wait_ge(c_("dve_done"), n[0])

            tt, ts = v.tensor_tensor, v.tensor_scalar
            link(v.memset(dst_p[:, EC:ET], N), False)
            link(v.memset(dst_n[:, EC:ET], N), False)
            link(v.memset(pos_i[:, 0, :, :], 0), False)
            link(v.memset(pos_i[:, 1, :, :], -1000), False)
            link(v.memset(zero_i[:, :], 0), False)
            link(v.memset(zero_b[:, :], 0.0), False)
            link(v.memset(deg[:, :, :], 1.0), False)
            link(v.memset(X[:, NT - 1, :], 0.0))
            v.sem_inc(c_("filled"), 1)
            v.sem_inc(c_("ea_taken"), 3)
            v.wait_ge(c_("dst_in"), 64)
            link(ts(part_i[:, :], dst_p[:, :], P - 1, None, ALU.bitwise_and))
            link(v.tensor_copy(part_f[:, 0, :], part_i[:, :]))
            link(ts(part_i[:, :], dst_p[:, :], 7, None, ALU.logical_shift_right))
            link(v.tensor_copy(part_f[:, 1, :], part_i[:, :]))
            v.wait_ge(c_("loaded"), LOADED[0] * 16)
            link(v.tensor_copy(iota_b[:, :], iota), False)
            link(v.tensor_copy(ident_b[:, :], ident))
            with v.Fori(0, ET // HB // 2) as i:
                for b in range(2):
                    col = (i * 2 + b) * HB
                    v.wait_ge(c_("hist_used"), i * 2 + (b + 1))
                    tt(hist_low[:, b, :, :], iota_b[:, :].unsqueeze(1).broadcast_to([P, HB, P]),
                       wide(part_f[:, 0, bass.ds(col, HB)], P), ALU.is_equal)
                    tt(hist_high[:, b, :, :], iota_b[:, 0:NT].unsqueeze(1).broadcast_to([P, HB, NT]),
                       wide(part_f[:, 1, bass.ds(col, HB)], NT), ALU.is_equal).then_inc(c_("hist_ready"), 1)
            v.wait_ge(c_("hist_used"), ET // HB + 2)
            link(v.tensor_copy(deg[:, DEG_IN, :], ps[:, 4, 0:NT]))
            v.sem_inc(c_("ptr_go"), 1)
            link(tt(part_i[:, :].bitcast(F32), dst_n[:, :], dst_p[:, :], ALU.is_lt))
            link(v.tensor_reduce(flags[:, 0:1], part_i[:, :].bitcast(F32), AX.X, ALU.max), False)
            link(v.tensor_reduce(flags[:, 1:2], deg[:, DEG_IN, :], AX.X, ALU.max), False)
            link(ts(deg[:, IN1, :], deg[:, DEG_IN, :], 1.0, None, ALU.add))
            link(ts(deg[:, INV, :], deg[:, DEG_IN, :], 1.0, None, ALU.max))
            link(v.reciprocal(deg[:, INV, :], deg[:, INV, :]), False)
            link(v.reciprocal(deg[:, DISSQ, :], deg[:, IN1, :]), False)
            link(v.tensor_copy(root[:, 0, 0:NT], deg[:, IN1, :]), False)
            link(ts(root_bn[:, 0, :], rows[:, 3, :], EPS, None, ALU.add))
            v.sem_inc(c_("root_asked"), 1)
            v.wait_ge(c_("ptr_ready"), 1)
            link(v.tensor_copy(offs[:, 0, :], ps[:, 4, 64:64 + NT]), False)
            link(v.tensor_copy(offs[:, 1, :], ps[:, 4, 32:32 + NT]))
            link(tt(offs[:, 1, :], offs[:, 1, :], offs[:, 0, :], ALU.subtract))
            cur, nxt = 0, 2
            for sh in (1, 2, 4, 8, 16):
                link(v.tensor_copy(offs[:, nxt, 0:sh], offs[:, cur, 0:sh]), False)
                link(tt(offs[:, nxt, sh:NT], offs[:, cur, sh:NT], offs[:, cur, 0:NT - sh], ALU.add))
                cur, nxt = nxt, cur
            link(tt(offs[:, 3, :], offs[:, cur, :], offs[:, 1, :], ALU.add))
            link(v.tensor_copy(row_i[:, 0, :], offs[:, 3, :]))
            link(ts(row_i[:, 1, :], row_i[:, 0, :], 6, None, ALU.logical_shift_right), False)
            link(ts(row_i[:, 2, :], row_i[:, 0, :], SLOTS - 1, None, ALU.bitwise_and))
            link(v.tensor_copy(offs[:, 4, :], row_i[:, 2, :]))
            link(tt(offs[:, 5, :], offs[:, 4, :], deg[:, DEG_IN, :], ALU.add))
            v.wait_ge(c_("w_turned"), 1)
            link(v.tensor_copy(W[:, 3, :], ps[:, 5, 0:P]), False)
            link(v.tensor_copy(W[:, 10, :], ps[:, 5, P:2 * P]), False)
            link(v.tensor_copy(WEDGE[0:EK, 0:4, :], ps[0:EK, 6, :].rearrange("p (l d) -> p l d", l=4)), False)
            link(v.tensor_copy(WEDGE[0:EK, 4, :], ps[0:EK, 7, 0:P]))
            v.wait_ge(c_("root_done"), 1)
            link(v.tensor_copy(deg[:, SQ, :], root[:, 1, 0:NT]), False)
            link(v.reciprocal(deg[:, DIS, :], root[:, 1, 0:NT]), False)
            link(v.reciprocal(bn[:, 0, :], root_bn[:, 1, :]))
            link(tt(bn[:, 1, :], bn[:, 0, :], rows[:, 0, :], ALU.mult))
            link(tt(bn[:, 2, :], bn[:, 1, :], rows[:, 2, :], ALU.mult))
            link(tt(bn[:, 2, :], rows[:, 1, :], bn[:, 2, :], ALU.subtract))
            v.sem_inc(c_("rows_ready"), 1)
            v.sem_inc(c_("sq_out"), 1)
            v.wait_ge(c_("pos_in"), 16 * 16)
            link(v.tensor_copy(pos_f[:, :, :, :], pos_i[:, :, :, :]))
            v.sem_inc(c_("w_taken"), 1)
            v.wait_ge(c_("pos_turned"), 1)
            link(v.tensor_copy(src_e[:, 0:512], ps[:, 4, :]), False)
            link(v.tensor_copy(src_e[:, 512:NU * U], ps[:, 5, 0:NU * U - 512]), False)
            link(tt(rel_e[:, 0:512], ps[:, 6, :], base_b[:, 0:512], ALU.subtract), False)
            link(tt(rel_e[:, 512:NU * U], ps[:, 7, 0:NU * U - 512], base_b[:, 512:NU * U], ALU.subtract))
            v.sem_inc(c_("pos_done"), 1)
            link(v.memset(flags[:, 2:8], 0.0))
            link(v.tensor_reduce(flags[:, 2:3], rel_e[:, 0:EC], AX.X, ALU.max), False)
            link(v.tensor_reduce(flags[:, 3:4], rel_e[:, 0:EC], AX.X, ALU.min), False)
            link(v.tensor_copy(flags[0:ELAST, 4:5], rel_e[0:ELAST, EC:ET]), False)
            v.wait_ge(c_("z_free_act"), tiles_done_act("enc"))
            link(tt(T[:, :, :], T[:, :, :], bn[:, 1:2, :].broadcast_to([P, NT, P]), ALU.mult))
            link(tt(T[:, :, :], T[:, :, :], bn[:, 2:3, :].broadcast_to([P, NT, P]), ALU.add))
            link(tt(T[:, :, :], T[:, :, :], wide(deg[:, DIS, :], P), ALU.mult))
            v.sem_inc(c_("x_ready"), 1)

            v.wait_ge(c_("lists_in"), NT * 16)
            spread = iota.unsqueeze(1).broadcast_to([P, NT, P])
            link(tt(M1, spread, wide(offs[:, 4, :], P), ALU.is_ge), False)
            link(tt(M2, spread, wide(offs[:, 5, :], P), ALU.is_lt))
            link(tt(M1, M1, M2, ALU.mult))
            link(v.scalar_tensor_tensor(out=M2, in0=RAW[:, :, 0:2 * SLOTS], scalar=1.0, in1=M1, op0=ALU.add, op1=ALU.mult))
            one, two = M2[:, :, 0:SLOTS], M2[:, :, SLOTS:2 * SLOTS]
            link(tt(one, one, two, ALU.add))
            link(ts(two.bitcast(I32), one, -1.0, None, ALU.add))
            link(v.memset(flat[:, :, NT, :], 0.0), False)
            link(ts(one.bitcast(I32), two.bitcast(I32), P - 1, None, ALU.bitwise_and))
            link(v.tensor_copy(flat[:, 0, 0:NT, :], one.bitcast(I32)))
            link(ts(one.bitcast(I32), two.bitcast(I32), 7, None, ALU.arith_shift_right))
            link(v.tensor_copy(flat[:, 1, 0:NT, :], one.bitcast(I32)))
            link(v.memset(flat[:, 1, NT, :], -1.0))
            v.sem_inc(c_("flat_ready"), 1)
            link(tt(M2, RAWW, M1, ALU.mult))
            link(tt(one, one, two, ALU.add))
            link(v.tensor_copy(flat[:, 2, 0:NT, :], one))
            link(tt(two, one, flat[:, 2, 0:NT, :], ALU.subtract))
            link(v.tensor_copy(flat[:, 3, 0:NT, :], two))
            link(tt(flat[:, 4, 0:NT, :], two, flat[:, 3, 0:NT, :], ALU.subtract))
            v.sem_inc(c_("flat_ready"), 1)

            def low_hot(b, m, lists=lists):
                return tt(hot_low[:, b, :].rearrange("p (c l) -> p c l", c=CB),
                          iota_b[:, :].unsqueeze(1).broadcast_to([P, CB, P]),
                          wide(lists[:, 0, bass.ds(m, CB)], P), ALU.is_equal)

            def high_hot(b, m, lists=lists):
                return tt(hot_high[:, b, 0, :].rearrange("p (c j) -> p c j", c=CB),
                          iota_b[:, 0:NT].unsqueeze(1).broadcast_to([P, CB, NT]),
                          wide(lists[:, 1, bass.ds(m, CB)], NT), ALU.is_equal)

            v.wait_ge(c_("turn_taken"), 4)
            with v.Fori(0, COLS // CB // 2) as i:
                for b in range(2):
                    v.wait_ge(c_("hot_used"), i * 2 + (b + 1))
                    low_hot(b, (i * 2 + b) * CB)
                    high_hot(b, (i * 2 + b) * CB).then_inc(c_("hot_ready"), 1)
            v.wait_ge(c_("grp_free"), COLS // CG + 2)
            for j in range(NT):
                tt(A8[:, j, j * P:(j + 1) * P], A8[:, j, j * P:(j + 1) * P], ident_b[:, :], ALU.add, saturate=False).then_inc(c_("adj_ready"), 1)

            def split(st):
                base = SPLITS.index(st) * NSG

                def rest(g):
                    v.wait_ge(c_("hi_ready"), base + g + 1)
                    sl = slice(g * SG, (g + 1) * SG)
                    tt(T[:, sl, :], T[:, sl, :], T3[:, sl, 0, :], ALU.subtract).then_inc(c_("r_ready"), 1)

                def last(g):
                    v.wait_ge(c_("mid_ready"), base + g + 1)
                    sl = slice(g * SG, (g + 1) * SG)
                    tt(T3[:, sl, 2, :], T[:, sl, :], T3[:, sl, 1, :], ALU.subtract).then_inc(c_("t3_ready"), 1)

                for g in range(NSG):
                    rest(g)
                    if g:
                        last(g - 1)
                last(NSG - 1)

            def take(st, scale, tiles=None):
                for k in range(first_item[st], first_item[st] + item_count[st]):
                    if tiles is not None and k != tiles:
                        continue
                    c, w = items[k][1:3]
                    v.wait_ge(c_("z_ready"), k + 1)
                    for i in range(w):
                        ins = v.scalar_tensor_tensor(out=X[:, c + i, :], in0=z_bank(k)[:, i * P:(i + 1) * P],
                                                     scalar=deg[:, scale, c + i:c + i + 1], in1=X[:, c + i, :],
                                                     op0=ALU.mult, op1=ALU.add)
                    ins.then_inc(c_("z_free_dve"), 1)
                    v.wait_ge(*z_taken(k))
                    stats_of(c, w)

            def stats_of(c, w):
                for i in range(w):
                    ins = v.bn_stats(stats[:, c + i, :], X[:, c + i, :])
                link(ins)
                for i in range(w):
                    ins = v.bn_aggr(mv[:, c + i, :], stats[:, c + i, :])
                link(ins, False)

            roots = [1]

            def norm(out_t):
                v.wait_ge(c_("dve_done"), n[0])
                link(ts(root[:, 0, 0:NT], mv[:, :, 1], EPS, None, ALU.add))
                v.sem_inc(c_("root_asked"), 1)
                roots[0] += 1
                v.wait_ge(c_("root_done"), roots[0])
                link(v.reciprocal(sd[:, 0, :], root[:, 1, 0:NT]))
                for j in range(NT):
                    ins = ts(out_t[:, j, :], X[:, j, :], mv[:, j, 0:1], sd[:, 0, j:j + 1], ALU.subtract, ALU.mult)
                link(ins)

            split("gcn1")
            for j in range(NT + 1):
                if j == NT:
                    link(ts(deg[:, DEG_OUT1, :], deg[:, DEG_OUT1, :], 1.0, None, ALU.max))
                    link(v.tensor_copy(root[:, 0, 0:NT], deg[:, DEG_OUT1, :]), False)
                    link(v.reciprocal(deg[:, DIS2SQ, :], deg[:, DEG_OUT1, :]))
                    v.sem_inc(c_("root_asked"), 1)
                    roots[0] += 1
                    v.wait_ge(c_("root_done"), roots[0])
                    link(v.tensor_copy(deg[:, SQ2, :], root[:, 1, 0:NT]), False)
                    link(v.reciprocal(deg[:, DIS2, :], root[:, 1, 0:NT]))
                    v.sem_inc(c_("dis_out"), 1)
                    break
                v.wait_ge(c_("sums_in"), j + 1)
                v.tensor_reduce(flags[:, 8 + j:9 + j], scratch[:, j % 2, 0:N], AX.X, ALU.max).then_inc(c_("max_free"), 1)
            v.wait_ge(c_("max_free"), NT)
            split("gcn2")
            take("gcn2", DIS)
            norm(T)
            v.sem_inc(c_("x_ready"), 1)
            for k in range(first_item["self"], first_item["self"] + item_count["self"]):
                c, w = items[k][1:3]
                v.wait_ge(c_("z_ready"), k + 1)
                tt(X[:, c:c + w, :], z_bank(k)[:, 0:w * P].rearrange("p (t f) -> p t f", t=w), T[:, c:c + w, :],
                   ALU.add).then_inc(c_("z_free_dve"), 1)
            v.wait_ge(c_("wl_in"), 16)
            done0 = COLS // CB
            for q in range(PAIRS):
                with v.Fori(0, P // CB // 2) as i:
                    for b in range(2):
                        at = i * 2 + (b + q * (P // CB))
                        m = (i * 2 + b) * CB + q * P
                        v.wait_ge(c_("hot_used"), i * 2 + (b + q * (P // CB) + done0 + 1))
                        high_hot(b, m, wlists).then_inc(c_("high_ready"), 1)
                        low_hot(b, m, wlists)
                        v.wait_ge(c_("high_ready"), i * 2 + (b + q * (P // CB) + 1))
                        for part in range(3):
                            ins = tt(hot_high[:, b, 1 + part, :].rearrange("p (c j) -> p c j", c=CB),
                                     hot_high[:, b, 0, :].rearrange("p (c j) -> p c j", c=CB),
                                     wide(wlists[:, 2 + part, bass.ds(m, CB)], NT), ALU.mult)
                        ins.then_inc(c_("hot_ready"), 1)
                if q > 1:
                    take("neigh", INV, first_item["neigh"] + q - 2)
            for q in (PAIRS - 2, PAIRS - 1):
                take("neigh", INV, first_item["neigh"] + q)
            norm(X)
            link(tt(T[:, :, :], X[:, :, :], wide(deg[:, DIS2, :], P), ALU.mult))
            v.sem_inc(c_("x_ready"), 1)

            v.wait_ge(c_("aug_rows"), 32)
            link(v.memset(EWB[:, :, :], 0.0))
            v.sem_inc(c_("ewb_zero"), 1)

            def windows_hot(u, r):
                return tt(hot_d[:, r, :, :], iota[:, 0:WIN].unsqueeze(1).broadcast_to([P, U, WIN]),
                          wide(rel_e[:, bass.ds(u * U, U)], WIN), ALU.is_equal)

            def attr_unit(u, r, k, got_n):
                v.wait_ge(S[f"ea{r}"], got_n)
                v.wait_ge(c_("dis_e_ready"), k)
                v.wait_ge(c_("unit_used"), k)
                tt(eas[:, r, :, 0:EK], ea_u[:, r, :, :], wide(dis_e[:, bass.ds(u * U, U)], EK), ALU.mult).then_inc(c_("ea_taken"), 1)
                v.tensor_copy(eas[:, r, :, EK], dis_e[:, bass.ds(u * U, U)])
                windows_hot(u, r).then_inc(c_("eas_ready"), 1)

            with v.Fori(0, NU // 3) as i:
                for r in range(3):
                    attr_unit(i * 3 + r, r, i * 3 + (r + 1), i * 16 + 16)
            attr_unit(NU - 2, 0, NU - 1, 16 * (NU // 3 + 1))
            attr_unit(NU - 1, 1, NU, 16 * (NU // 3) + 32)
            v.wait_ge(c_("unit_used"), NU + 3)
            copies, adds = windows()
            for b, lo, hi, node in copies:
                link(v.tensor_copy(AUG[0:EK + 1, node:node + hi - lo], ps[0:EK + 1, b, lo:hi]), False)
            v.wait_ge(c_("dve_done"), n[0])
            for b, lo, hi, node in adds:
                link(tt(AUG[0:EK + 1, node:node + hi - lo], AUG[0:EK + 1, node:node + hi - lo], ps[0:EK + 1, b, lo:hi], ALU.add), False)
            v.wait_ge(c_("dve_done"), n[0])
            v.sem_inc(c_("aug_ready"), 1)

            for l in range(5):
                split(f"edge{l}")
            take("edge4", DIS2)
            norm(X)
            v.sem_inc(c_("x_ready"), 1)
            link(ts(flags[:, 5:6], flags[:, 1:2], float(SLOTS), None, ALU.is_gt))
            link(ts(flags[:, 6:7], flags[:, 2:3], float(WIN - 1), None, ALU.is_gt))
            link(ts(flags[:, 7:8], flags[:, 3:4], 0.0, None, ALU.is_lt))
            link(ts(flags[:, 1:2], flags[:, 4:5], float(WIN - 1), None, ALU.is_gt))
            link(ts(flags[:, 2:3], flags[:, 4:5], 0.0, None, ALU.is_lt))
            link(ts(flags[:, 8:8 + NT], flags[:, 8:8 + NT], 15.0, None, ALU.is_gt))
            link(v.memset(flags[:, 3:5], 0.0))
            link(v.tensor_reduce(sd[:, 1, 0:1], flags[:, :], AX.X, ALU.max))
            v.sem_inc(c_("flag_go"), 1)
            v.wait_ge(c_("flag_mm"), 1)
            link(ts(verdict[0:1, 0:1], ps[0:1, 4, 0:1], 0.0, None, ALU.is_gt))
            v.sem_inc(c_("flag_ready"), 1)
            v.wait_ge(c_("pt_ready"), NI)
            link(tt(X[:, :, :], X[:, :, :], b3_row.unsqueeze(1).broadcast_to([P, NT, P]), ALU.add))
            v.sem_inc(c_("msg_ready"), 1)

            def product_unit(u, r, k, k2, got_n):
                v.wait_ge(c_("gathered_used"), k)
                windows_hot(u, r).then_inc(c_("hotd_ready"), 1)
                v.wait_ge(S[f"g{r}"], got_n)
                for h in range(2):
                    v.wait_ge(c_("e_ready"), k2 + h)
                    sl = G[:, r, 4 * h:4 * h + 4, :]
                    tt(sl, sl, ps[:, 7, :].rearrange("p (t f) -> p t f", t=4), ALU.mult).then_inc(c_("msg_ready"), 1)
                    if h == 0:
                        v.sem_inc(c_("ea_taken"), 1)

            with v.Fori(0, NU // 3) as i:
                for r in range(3):
                    product_unit(i * 3 + r, r, i * 3 + (r + 1), i * 6 + (2 * r + 1), i * (16 * U) + 16 * U)
            product_unit(NU - 2, 0, NU - 1, 2 * (NU - 2) + 1, 16 * U * (NU // 3 + 1))
            product_unit(NU - 1, 1, NU, 2 * (NU - 1) + 1, 16 * U * (NU // 3 + 1))
            v.wait_ge(c_("gathered_used"), NU + 3)
            for b, lo, hi, node in copies:
                link(v.tensor_copy(sum_t[:, node:node + hi - lo], ps[:, b, lo:hi]), False)
            v.wait_ge(c_("dve_done"), n[0])
            for b, lo, hi, node in adds:
                link(tt(sum_t[:, node:node + hi - lo], sum_t[:, node:node + hi - lo], ps[:, b, lo:hi], ALU.add), False)
            v.wait_ge(c_("dve_done"), n[0])
            v.sem_inc(c_("sum_taken"), 1)
            for m, (c, w) in enumerate(CHUNKS):
                v.wait_ge(c_("sum_done"), m + 1)
                link(tt(X[:, c:c + w, :], X[:, c:c + w, :], ps[:, m, 0:w * P].rearrange("p (t f) -> p t f", t=w), ALU.add))
                stats_of(c, w)
            norm(X)
            v.sem_inc(c_("out_ready"), 1)

        @block.scalar
        def _(act):
            def root_of():
                roots[0] += 1
                act.wait_ge(c_("root_asked"), roots[0])
                if roots[0] == 1:
                    act.activation(root_bn[:, 1, :], root_bn[:, 0, :], ACT.Sqrt)
                act.activation(root[:, 1, :], root[:, 0, :], ACT.Sqrt).then_inc(c_("root_done"), 1)

            def move(k):
                act.wait_ge(c_("p_ready"), k + 1)
                if before(k) is not None:
                    act.wait_ge(c_("z_ready"), before(k) + 1)
                w = items[k][2] * P
                act.copy(PTc[:, place[k] % 2, 0:w], p_bank(k)[:, 0:w]).then_inc(c_("pt_ready"), 1)

            def take(k):
                st, c, w, _ = items[k]
                act.wait_ge(c_("z_ready"), k + 1)
                scale = {"gcn1": DISSQ}.get(st, DIS2SQ)
                if st in ("enc", "last"):
                    ins = act.activation(T[:, c:c + w, :].rearrange("p t f -> p (t f)"), z_bank(k)[:, 0:w * P],
                                         ACT.Relu if st == "enc" else ACT.Copy)
                    ins.then_inc(c_("z_free_act"), 1)
                else:
                    for i in range(w):
                        ins = act.activation(T[:, c + i, :], z_bank(k)[:, i * P:(i + 1) * P], ACT.Relu,
                                             scale=deg[:, scale, c + i:c + i + 1])
                    ins.then_inc(c_("z_free_act"), 1)

            def stage(st, extra=None):
                ks = range(first_item[st], first_item[st] + item_count[st])
                for k in ks:
                    move(k)
                    if items[k][3] == "act" and k > ks[0]:
                        take(k - 1)
                    if extra:
                        extra(k - ks[0])
                if items[ks[-1]][3] == "act":
                    take(ks[-1])

            def split(st):
                base = SPLITS.index(st) * NSG
                src_st = SOURCE[st]
                if src_st == "enc":
                    act.wait_ge(c_("x_ready"), 1)
                    act.wait_ge(c_("turn_taken"), 10)
                elif src_st == "neigh":
                    act.wait_ge(c_("x_ready"), 3)
                else:
                    act.wait_ge(*z_taken(first_item[src_st] + item_count[src_st] - 1))
                for g in range(NSG):
                    sl = slice(g * SG, (g + 1) * SG)
                    act.copy(T3[:, sl, 0, :], T[:, sl, :]).then_inc(c_("hi_ready"), 1)
                    if g:
                        mid(base, g - 1)
                mid(base, NSG - 1)

            def mid(base, g):
                sl = slice(g * SG, (g + 1) * SG)
                act.wait_ge(c_("r_ready"), base + g + 1)
                act.copy(T3[:, sl, 1, :], T[:, sl, :]).then_inc(c_("mid_ready"), 1)

            roots = [0]
            act.sem_inc(c_("grp_free"), 2)
            root_of()
            stage("enc")
            for m in range(10):
                k, half = m // 2, m % 2
                w = (8 if half == 0 else PAIRS - 8) * P
                act.wait_ge(c_("turn_ready"), m + 1)
                to = lists[:, k, half * 8 * P:half * 8 * P + w]
                act.copy(to, psb[:, 4 + m % 4, 0:w]).then_inc(c_("turn_taken"), 1)

            def from_group(g, out_a, out_b, **narrow):
                for h, to in enumerate((out_a, out_b)):
                    if to is not None:
                        ins = act.activation(to, ps[:, 4 + 2 * g + h, 0:CG * NT].rearrange("p (c j) -> p j c", c=CG),
                                             ACT.Copy, **narrow)
                ins.then_inc(c_("grp_free"), 1)

            for m in range(COLS // CG):
                q, g = m // (P // CG), m % 2
                col = q * 2 * P + m % (P // CG) * CG
                second = None if q == PAIRS - 1 else A8[:, :, col + P:col + P + CG]
                act.wait_ge(c_("hot_used"), 2 * m + 2 + 2)
                from_group(g, A8[:, :, col:col + CG], second, saturate=False)
            split("gcn1")

            def row_sums(i):
                for j in range(4 * i, min(4 * i + 4, NT)):
                    act.wait_ge(c_("adj_ready"), NT)
                    if j >= 2:
                        act.wait_ge(c_("max_free"), j - 1)
                    act.activation(scratch[:, j % 2, 0:N], A8[:, j, 0:N], ACT.Copy,
                                   accum_out=deg[:, DEG_OUT1, j:j + 1]).then_inc(c_("sums_in"), 1)

            stage("gcn1", row_sums)
            root_of()
            split("gcn2")
            stage("gcn2")
            root_of()
            stage("self")
            act.wait_ge(c_("wl_in"), 16)
            g0 = COLS // CB
            for q in range(PAIRS):
                if q > 1:
                    act.wait_ge(c_("p_ready"), first_item["neigh"] + q - 1)
                with act.Fori(0, P // CG // 2) as i:
                    for g in range(2):
                        act.wait_ge(c_("hot_used"), i * 4 + (2 * g + 2 + 2 + g0 + q * (P // CB)))
                        col = i * (2 * CG) + g * CG
                        ab = 2 * (q % 2)
                        from_group(g, AW[:, ab, :, bass.ds(col, CG)], AW[:, ab + 1, :, bass.ds(col, CG)])
                if q:
                    move(first_item["neigh"] + q - 1)
            move(first_item["neigh"] + PAIRS - 1)
            root_of()
            for l in range(5):
                split(f"edge{l}")
                stage(f"edge{l}")
            root_of()
            stage("last")

            def turn_unit(r, k):
                act.wait_ge(c_("et_ready"), k)
                act.copy(ea_t[:, r, :], ps[:, 7, 0:P]).then_inc(c_("et_in"), 1)

            with act.Fori(0, NU // 3) as i:
                for r in range(3):
                    turn_unit(r, i * 3 + (r + 1))
            turn_unit(0, NU - 1)
            turn_unit(1, NU)
            root_of()

        @block.tensor
        def _(pe):
            mm = pe.matmul
            pe.sem_inc(c_("hist_used"), 2)
            pe.sem_inc(c_("hot_used"), 2)
            pe.sem_inc(c_("unit_used"), 3)
            pe.sem_inc(c_("gathered_used"), 3)

            def zero_bank(b):
                return mm(ps[:, b, :], zero_b[0:1, 0:P], zero_b[0:1, :], start=True, stop=False, skip_group_check=True)

            pe.wait_ge(c_("filled"), 1)
            zero_bank(4)
            with pe.Fori(0, ET // HB // 2) as i:
                for b in range(2):
                    pe.wait_ge(c_("hist_ready"), i * 2 + (b + 1))
                    for t in range(HB):
                        ins = mm(ps[:, 4, 0:NT], hist_low[:, b, t, :], hist_high[:, b, t, :], start=False, stop=False,
                                 skip_group_check=True)
                    ins.then_inc(c_("hist_used"), 1)
            pe.wait_ge(c_("loaded"), LOADED[0] * 16)
            pe.transpose(ps[:, 5, 0:P], WRAW[:, 0, :], ident)
            pe.transpose(ps[:, 5, P:2 * P], WRAW[:, 1, :], ident)
            for l in range(5):
                ins = pe.transpose(ps[0:EK, 6 + l // 4, (l % 4) * P:(l % 4 + 1) * P], EWR[:, l, :], ident)
            ins.then_inc(c_("w_turned"), 1)
            pe.wait_ge(c_("ptr_go"), 1)
            mm(ps[:, 4, 32:32 + NT], below, deg[:, DEG_IN, :], start=True, stop=True)
            mm(ps[:, 4, 64:64 + NT], ones, deg[:, DEG_IN, :], start=True, stop=True).then_inc(c_("ptr_ready"), 1)

            def product(k):
                st, c, w, _ = items[k]
                pe.wait_ge(c_("pt_ready"), k + 1)
                if before(k) is not None:
                    pe.wait_ge(*z_taken(before(k)))
                if st == "edge0" and place[k] == 0:
                    pe.wait_ge(c_("aug_rows"), 32)
                for i in range(w):
                    to = z_bank(k)[:, i * P:(i + 1) * P]
                    rows_in = PTc[:, place[k] % 2, i * P:(i + 1) * P]
                    nodes = slice((c + i) * P, (c + i + 1) * P)
                    wi = {"enc": 0, "gcn1": 1, "gcn2": 2, "neigh": 3, "self": 10, "last": 9}.get(st)
                    if wi is None:
                        wi = 4 + int(st[4:])
                    alone = st in ("neigh", "last")
                    ins = mm(to, rows_in, W[:, wi, :], start=True, stop=alone)
                    if st in ("enc", "self"):
                        ins = mm(to, ones[0:1, :], bias[:, 0 if st == "enc" else 3, :], start=False, stop=True)
                    elif st in ("gcn1", "gcn2"):
                        ins = mm(to, sq_row[:, nodes], bias[:, wi, :], start=False, stop=True)
                    elif not alone:
                        ins = mm(to, AUG[:, nodes], WEDGE[:, wi - 4, :], start=False, stop=True)
                ins.then_inc(c_("z_ready"), 1)

            def buffers_free(k):
                if before(k) is not None:
                    pe.wait_ge(c_("pt_ready"), before(k) + 1)

            def turn(k, src):
                _, c, w, _ = items[k]
                buffers_free(k)
                for i in range(w):
                    ins = pe.transpose(p_bank(k)[:, i * P:(i + 1) * P], src[:, c + i, :], ident)
                ins.then_inc(c_("p_ready"), 1)

            def spread(k):
                st, c, w, _ = items[k]
                buffers_free(k)
                for j in range(NT):
                    if place[k] == 0 and j % SG == 0:
                        pe.wait_ge(c_("t3_ready"), SPLITS.index(st) * NSG + j // SG + 1)
                    for part in range(3):
                        ins = mm(p_bank(k)[:, 0:w * P], T3[:, j, part, :], A8[:, j, c * P:(c + w) * P],
                                 start=(j == 0 and part == 0), stop=(j == NT - 1 and part == 2))
                ins.then_inc(c_("p_ready"), 1)

            def stage(st, fill):
                ks = range(first_item[st], first_item[st] + item_count[st])
                for k in ks:
                    fill(k)
                    if k > ks[0]:
                        product(k - 1)
                product(ks[-1])

            pe.wait_ge(c_("w_taken"), 1)
            for a_i in range(2):
                for g in range(7):
                    ins = pe.transpose(ps[:, 4 + 2 * a_i + g // 4, (g % 4) * P:(g % 4 + 1) * P], pos_f[:, a_i, g, :], ident)
            ins.then_inc(c_("pos_turned"), 1)
            stage("enc", lambda k: turn(k, X))
            pe.wait_ge(c_("pos_done"), 1)
            for m in range(10):
                k, half = m // 2, m % 2
                if m in (0, 4):
                    pe.wait_ge(c_("flat_ready"), 1 + m // 4)
                if m >= 4:
                    pe.wait_ge(c_("turn_taken"), m - 3)
                for q in range(8 * half, min(8 * half + 8, PAIRS)):
                    ins = pe.transpose(psb[:, 4 + m % 4, (q % 8) * P:(q % 8 + 1) * P],
                                       flat[:, k, 2 * q:2 * q + 2, :].rearrange("p j s -> p (j s)"), ident_b[:, :])
                ins.then_inc(c_("turn_ready"), 1)
            pe.wait_ge(c_("turn_taken"), 10)

            def group(g, b0, first, parts):
                pe.wait_ge(c_("grp_free"), first)
                for b in range(2):
                    pe.wait_ge(c_("hot_ready"), b0 + b)
                    for c in range(CB):
                        at = (b * CB + c) * NT
                        for h in range(2):
                            sl = slice(h * SLOTS, (h + 1) * SLOTS)
                            for n_p, part in enumerate(parts):
                                ins = mm(ps[:, 4 + 2 * g + h, at:at + NT], hot_low[sl, b, c * P:(c + 1) * P],
                                         hot_high[sl, b, part, c * NT:(c + 1) * NT],
                                         start=(n_p == 0), stop=(n_p == len(parts) - 1))
                    ins.then_inc(c_("hot_used"), 1)

            with pe.Fori(0, COLS // CG // 2) as i:
                for g in range(2):
                    group(g, i * 4 + (2 * g + 1), i * 2 + (g + 1), (0,))
            pe.wait_ge(c_("adj_ready"), NT)
            pe.wait_ge(c_("sq_in"), 32)
            stage("gcn1", spread)
            stage("gcn2", spread)
            pe.wait_ge(c_("x_ready"), 2)
            stage("self", lambda k: turn(k, T))

            def neigh(k):
                _, c, w, _ = items[k]
                q = place[k]
                buffers_free(k)
                pe.wait_ge(c_("grp_free"), COLS // CG + (q + 1) * (P // CG) + 2)
                for i in range(w):
                    for j in range(NT):
                        ins = mm(p_bank(k)[:, i * P:(i + 1) * P], T[:, j, :], AW[:, 2 * (q % 2) + i, j, :],
                                 start=(j == 0), stop=(j == NT - 1))
                ins.then_inc(c_("p_ready"), 1)

            k0 = first_item["neigh"]
            for q in range(PAIRS):
                with pe.Fori(0, P // CG // 2) as i:
                    for g in range(2):
                        group(g, i * 4 + (2 * g + 1 + COLS // CB + q * (P // CB)),
                              i * 2 + (g + 1 + COLS // CG + q * (P // CG)), (1, 2, 3))
                if q:
                    neigh(k0 + q - 1)
                if q > 1:
                    product(k0 + q - 2)
            neigh(k0 + PAIRS - 1)
            product(k0 + PAIRS - 2)
            product(k0 + PAIRS - 1)

            def by_bank(unit):
                for b in range(-(-NU // UB)):
                    m = min(UB, NU - b * UB)
                    with pe.Fori(0, m // 3) as i:
                        for r in range(3):
                            unit(b, i * (3 * USTEP) + r * USTEP, r, i * 3 + (b * UB + r), i)
                    for r in range(m % 3):
                        unit(b, (m // 3 * 3 + r) * USTEP, r, b * UB + m // 3 * 3 + r, None)

            pe.wait_ge(c_("x_ready"), 3)
            pe.wait_ge(c_("grp_free"), 2 * (COLS // CG) + 2)
            for b in range(7):
                zero_bank(b)

            def attr_unit(b, col, r, u, _):
                pe.wait_ge(c_("eas_ready"), u + 1)
                for t in range(U):
                    ins = mm(ps[0:EK + 1, b, bass.ds(col + window_step(t), WIN)], eas[:, r, t, :], hot_d[:, r, t, :],
                             start=False, stop=False, skip_group_check=True)
                ins.then_inc(c_("unit_used"), 1)

            by_bank(attr_unit)
            pe.wait_ge(c_("aug_ready"), 1)
            for l in range(5):
                stage(f"edge{l}", spread)
            pe.wait_ge(c_("x_ready"), 4)
            stage("last", lambda k: turn(k, X))
            pe.wait_ge(c_("flag_go"), 1)
            mm(ps[0:1, 4, 0:1], sd[:, 1, 0:1], ones[:, 0:1], start=True, stop=True).then_inc(c_("flag_mm"), 1)
            pe.wait_ge(c_("flag_ready"), 1)
            pe.wait_ge(*z_taken(NI - 1))
            pe.wait_ge(c_("ewb_zero"), 1 + 16 * U)
            for b in range(7):
                zero_bank(b)
            per_ring = [16 * 34, 16 * 33 + 32, 16 * 33]

            def product_unit(b, col, r, u, i):
                if i is None:
                    pe.wait_ge(S[f"ea{r}"], per_ring[r] + (16 * (u // 3) + 16 if u < NU - 1 else 16 * (u // 3) + 32))
                else:
                    pe.wait_ge(S[f"ea{r}"], i * 16 + (per_ring[r] + 16 + 16 * (b * UB // 3)))
                pe.wait_ge(c_("msg_ready"), u * 2 + 1)
                pe.transpose(ps[:, 7, 0:P], ea_u[:, r, :, :].rearrange("p t k -> p (t k)"), ident).then_inc(c_("et_ready"), 1)
                pe.wait_ge(c_("et_in"), u + 1)
                for h in range(2):
                    if h:
                        pe.wait_ge(c_("msg_ready"), u * 2 + 2)
                    for t in range(4):
                        ins = mm(ps[:, 7, t * P:(t + 1) * P], ea_t[:, r, :], EWB[:, 4 * h + t, :], start=True, stop=True)
                    ins.then_inc(c_("e_ready"), 1)
                pe.wait_ge(c_("hotd_ready"), u + 1)
                for t in range(U):
                    if t == 4:
                        pe.wait_ge(c_("msg_ready"), u * 2 + 3)
                    ins = mm(ps[:, b, bass.ds(col + window_step(t), WIN)], G[:, r, t, :], hot_d[:, r, t, :],
                             start=False, stop=False, skip_group_check=True)
                ins.then_inc(c_("gathered_used"), 1)

            by_bank(product_unit)
            pe.wait_ge(c_("sum_taken"), 1)
            for m, (c, w) in enumerate(CHUNKS):
                for i in range(w):
                    ins = pe.transpose(ps[:, m, i * P:(i + 1) * P], sum_t[:, (c + i) * P:(c + i + 1) * P], ident)
                ins.then_inc(c_("sum_done"), 1)


def steps():
    out = [("turn", "X", "PT"), ("dense", 0)]
    for st, kind, scale, loop in ((1, NONE, "dis", True), (2, NONE, "dis", True)):
        out += [("sum", kind, scale, loop), ("turn", "AG", "PT"), ("dense", st)]
    out += [("turn", "X", "XT"), ("sum", WEIGHT, "inv", False), ("turn", "AG", "PT")]
    out += [("sum", ATTR, "dis2", False), ("turn", "AG", "AUG"), ("dense", 3)]
    for st in range(4, 9):
        out += [("sum", NONE, "dis2", True), ("turn", "AG", "PT"), ("dense", st)]
    out += [("turn", "X", "PT"), ("dense", 9), ("sum", PROD, None, False), ("final",)]
    return out


def host_constants():
    c = np.zeros((P, 4 * P + 1), np.float32)
    c[:, 0:P] = np.eye(P)
    c[:, P:2 * P] = 1.0
    c[:, 2 * P:3 * P] = np.arange(P)[None, :]
    c[:, 3 * P:4 * P] = np.tril(np.ones((P, P)), -1)
    c[:, 4 * P] = np.arange(P) + DUMP
    s = np.zeros((PK, 3, P), np.float32)
    s[EK + 1, NONE, :] = 1.0
    s[EK, WEIGHT, :] = 1.0
    s[:EK, ATTR, :EK] = np.eye(EK)
    s[EK + 1, ATTR, EK] = 1.0
    return c, s


def general_program(nc, a, out, verdict, sems):
    with ExitStack() as ctx:
        def sb(name, shape, dt=F32):
            return ctx.enter_context(nc.sbuf_tensor(name, shape, dt))

        def sem(name):
            return sems.enter_context(nc.semaphore(name))

        const = sb("const", [P, 4 * P + 1])
        ident, ones, iota, tril = (const[:, i * P:(i + 1) * P] for i in range(4))
        dump_row = const[:, 4 * P:4 * P + 1]
        sels = sb("sels", [PK, 4, P])
        X = sb("X", [P, NT, P])
        T = sb("T", [P, NT, P])
        AG = sb("AG", [P, NT, P])
        Y = sb("Y", [P, NT, P])
        PT = sb("PT", [P, NP])
        XT = sb("XT", [P, NP])
        AUG = sb("AUG", [P, NP])
        W = sb("W", [P, 11, P])
        WRAW = sb("WRAW", [P, 2, P])
        EWR = sb("EWR", [P, 5, EK])
        WEDGE = sb("WEDGE", [EK + 1, 5, P])
        bias = sb("bias", [1, 10, P])
        rows = sb("rows", [P, 5, P])
        bn = sb("bn", [P, 4, P])
        src_i = sb("src_i", [P, ET], I32)
        dst_i = sb("dst_i", [P, ET], I32)
        part_i = sb("part_i", [P, ET], I32)
        dst_f = sb("dst_f", [P, ET])
        low = sb("low", [P, ET], BF16)
        high = sb("high", [P, ET], BF16)
        weight = sb("weight", [P, ET])
        attr = sb("attr", [P, ET, EK])
        deg = sb("deg", [P, 6, NT])
        hot_low = sb("hot_low", [P, 2, P], BF16)
        hot_high = sb("hot_high", [P, 2, 32], BF16)
        iota_b = sb("iota_b", [P, P], BF16)
        src_col = sb("src_col", [P, 1], I32)
        pay_col = sb("pay_col", [P, PK])
        diag = sb("diag", [P, P])
        same = sb("same", [P, P])
        before = sb("before", [P, P])
        n_before = sb("n_before", [P, 1])
        to_dump = sb("to_dump", [P, 1])
        row_f = sb("row_f", [P, 1])
        row_col = sb("row_col", [P, 1], I32)
        pay_t = sb("pay_t", [PK, P])
        gathered = sb("gathered", [P, P])
        msg = sb("msg", [P, P])
        joined = sb("joined", [P, P])
        zeros = sb("zeros", [P, P])
        stats = sb("stats", [P, NT, 6])
        mv = sb("mv", [P, NT, 2])
        sd = sb("sd", [P, 2, NT])
        roots = sb("roots", [P, 256])

        z = ctx.enter_context(nc.psum_tensor("z", [P, 2, 2 * 512], F32))
        ps_hist = ctx.enter_context(nc.psum_tensor("ps_hist", [P, 512], F32))
        ps_row = ctx.enter_context(nc.psum_tensor("ps_row", [P, 512], F32))
        ps_mul = ctx.enter_context(nc.psum_tensor("ps_mul", [P, 512], F32))
        ps_sum = ctx.enter_context(nc.psum_tensor("ps_sum", [P, 512], F32))

        table = nc.dram_tensor("table", [NP, P], F32).ap()
        sums = nc.dram_tensor("sums", [NP + P, P], F32).ap()

        loaded = sem("loaded")
        x_loaded = sem("x_loaded")
        dve_done = sem("dve_done")
        act_done = sem("act_done")
        z_ready = sem("z_ready")
        z_free_act = sem("z_free_act")
        z_free_dve = sem("z_free_dve")
        hot_ready = sem("hot_ready")
        hot_used = sem("hot_used")
        pe_row = sem("pe_row")
        pe_pay = sem("pe_pay")
        pe_mul = sem("pe_mul")
        pe_sum = sem("pe_sum")
        cols_ready = sem("cols_ready")
        pay_ready = sem("pay_ready")
        same_ready = sem("same_ready")
        msg_ready = sem("msg_ready")
        joined_ready = sem("joined_ready")
        stored = sem("stored")
        roots_asked = sem("roots_asked")
        counted = sem("counted")
        tile_through = sem("tile_through")
        pool_turn = sem("pool_turn")
        roots_done = sem("roots_done")
        sd_asked = sem("sd_asked")
        sd_root = sem("sd_root")

        order = steps()
        n_sums = sum(s[0] == "sum" for s in order)
        gather_done = [sem(f"gather_done{i}") for i in range(n_sums)]
        scatter_done = [sem(f"scatter_done{i}") for i in range(n_sums)]
        table_done = sem("table_done")
        zeroed = sem("zeroed")
        summed = sem("summed")
        t_ready = sem("t_ready")
        ag_ready = sem("ag_ready")
        x_ready = sem("x_ready")

        fills = ["dve"] * 2
        for s in order:
            if s[0] == "turn":
                fills += ["act"] * NG
            elif s[0] == "dense":
                fills += (["dve"] if s[1] in LN_STAGES else ["act"]) * NG

        def free_count(k):
            return sum(f == fills[k] for f in fills[:k + 1])

        z_free = {"act": z_free_act, "dve": z_free_dve}

        def tile(k, i):
            return z[:, k % 2, i * P:(i + 1) * P]

        def region(k):
            return z[:, k % 2, 0:GT * P]

        ag_turned = []
        kk = 2
        for s in order:
            if s[0] == "turn":
                kk += NG
                if s[1] == "AG":
                    ag_turned.append(free_count(kk - 1))
            elif s[0] == "dense":
                kk += NG

        block = ctx.enter_context(nc.Block())
        N_LOADS = []

        def wanted(engine):
            return engine.value_load(verdict[0:1, 0:1], min_val=0, max_val=1)

        @block.sync
        def _(sp):
            with sp.If(wanted(sp) == 1):
                def load(dst, src, s=loaded):
                    sp.dma_start(dst, src).then_inc(s, 16)
                    if s is loaded:
                        N_LOADS.append(1)
                load(const[:, :], a["c_mat"])
                load(sels[:, 0:3, :], a["c_sel"])
                for i, n in enumerate(("L0_gnn_W_enc", "L0_gnn_W1", "L0_gnn_W2")):
                    load(W[:, i, :], a[n])
                load(W[:, 4:9, :], a["L2_gnn_weights"].rearrange("l a b -> a l b"))
                load(W[:, 9, :], a["L3_gnn_W"])
                load(WRAW[:, 0, :], a["L1_gnn_W_neigh"])
                load(WRAW[:, 1, :], a["L1_gnn_W_self"])
                load(EWR[:, :, :], a["L2_gnn_edge_ws"].rearrange("l d e -> d l e"))
                load(WEDGE[EK:EK + 1, :, :], a["L2_gnn_edge_bs"].rearrange("(o l) d -> o l d", o=1))
                for i, n in ((0, "L0_gnn_b_enc"), (1, "L0_gnn_b1"), (2, "L0_gnn_b2"), (3, "L1_gnn_b_self")):
                    load(bias[:, i, :], a[n].rearrange("(o d) -> o d", o=1))
                load(bias[:, 4:9, :], a["L2_gnn_biases"].rearrange("(o l) d -> o l d", o=1))
                for i, n in enumerate(("L0_gnn_bn_gamma", "L0_gnn_bn_beta", "L0_gnn_bn_mean", "L0_gnn_bn_var", "L3_gnn_b")):
                    load(rows[:, i, :], a[n].rearrange("(o d) -> o d", o=1).broadcast_to([P, P]))
                sp.wait_ge(dve_done, 8)
                load(X[:, 0:NT - 1, :], a["x"][0:(NT - 1) * P, :].rearrange("(j p) f -> p j f", p=P))
                load(X[0:NLAST, NT - 1, :], a["x"][(NT - 1) * P:N, :])
                load(sels[0:EK, PROD, :], a["L3_gnn_edge_w"])
                for dst, name in ((src_i, "src"), (dst_i, "dst"), (weight, "edge_weight")):
                    load(dst[:, 0:EC], a[name][0:P * EC].rearrange("(p t) -> p t", t=EC))
                    load(dst[0:ELAST, EC:ET], a[name][P * EC:E].rearrange("(p o) -> p o", o=1))
                attr_d = a["edge_attr_16"]
                load(attr[:, 0:EC, :], attr_d[0:P * EC, :].rearrange("(p t) k -> p t k", t=EC))
                load(attr[0:ELAST, EC, :], attr_d[P * EC:E, :])
                k = 0
                for s in order:
                    if s[0] == "sum":
                        sp.wait_ge(t_ready, k + 1)
                        if k:
                            sp.wait_ge(summed, 16 * k)
                        sp.dma_start(table.rearrange("(j p) f -> p j f", p=P), T[:, :, :]).then_inc(table_done, 16)
                        sp.dma_start(sums.rearrange("(j p) f -> p j f", p=P),
                                     zeros[:, :].unsqueeze(1).broadcast_to([P, NT + 1, P])).then_inc(zeroed, 16)
                        sp.wait_ge(scatter_done[k], 16 * ET)
                        if k:
                            sp.wait_ge(ag_ready, k)
                            sp.wait_ge(z_free_act, ag_turned[k - 1])
                        sp.dma_start(AG[:, :, :], sums[0:NP, :].rearrange("(j p) f -> p j f", p=P)).then_inc(summed, 16)
                        k += 1
                sp.wait_ge(x_ready, 4)
                sp.dma_start(out[0:(NT - 1) * P, :].rearrange("(j p) f -> p j f", p=P),
                             AG[:, 0:NT - 1, :]).then_inc(stored, 16)
                sp.dma_start(out[(NT - 1) * P:N, :], AG[0:NLAST, NT - 1, :]).then_inc(stored, 16)
                sp.wait_ge(stored, 32)
            sp.end_ifs()

        @block.gpsimd
        def _(pool):
            with pool.If(wanted(pool) == 1):
                pool.sem_inc(tile_through, 1)
                k = 0
                for s in order:
                    if s[0] != "sum":
                        continue
                    with pool.Fori(0, ET) as t:
                        pool.wait_ge(cols_ready, t + (k * ET + 1))
                        pool.sem_inc(pool_turn, 1)
                        pool.wait_ge(table_done, 16 * (k + 1))
                        pool.indirect_dma_start(
                            out=gathered[:, :], out_offset=None, in_=table[:, :],
                            in_offset=bass.IndirectOffsetOnAxis(ap=src_col[:, 0:1], axis=0)).then_inc(gather_done[k], 16)
                        pool.wait_ge(joined_ready, t + (k * ET + 1))
                        pool.sem_inc(pool_turn, 1)
                        pool.wait_ge(zeroed, 16 * (k + 1))
                        pool.indirect_dma_start(
                            out=sums[:, :], out_offset=bass.IndirectOffsetOnAxis(ap=row_col[:, 0:1], axis=0),
                            in_=joined[:, :], in_offset=None, compute_op=ALU.add).then_inc(scatter_done[k], 16)
                        pool.wait_ge(scatter_done[k], t * 16 + 16)
                        pool.sem_inc(tile_through, 1)
                    k += 1
            pool.end_ifs()

        TD = 12

        @block.vector
        def _(v):
            with v.If(wanted(v) == 1):
                n = [0]

                def link(ins, wait=True):
                    n[0] += 1
                    ins.then_inc(dve_done, 1)
                    if wait:
                        v.wait_ge(dve_done, n[0])

                link(v.memset(X[:, NT - 1, :], 0.0), False)
                link(v.memset(src_i[:, EC:ET], N), False)
                link(v.memset(sels[:, PROD, :], 0.0), False)
                link(v.memset(dst_i[:, EC:ET], N), False)
                link(v.memset(weight[:, EC:ET], 0.0), False)
                link(v.memset(attr[:, EC:ET, :], 0.0), False)
                link(v.memset(zeros[:, :], 0.0), False)
                link(v.memset(pay_col[:, EK + 1:PK], 1.0))
                v.wait_ge(loaded, 16 * len(N_LOADS))
                link(v.tensor_copy(iota_b[:, :], iota))
                link(v.tensor_copy(dst_f[:, :], dst_i[:, :]))

                def histogram(which, slot, base):
                    link(v.tensor_scalar(part_i[:, :], which[:, :], P - 1, None, ALU.bitwise_and))
                    link(v.tensor_copy(low[:, :], part_i[:, :]))
                    link(v.tensor_scalar(part_i[:, :], which[:, :], 7, None, ALU.logical_shift_right))
                    link(v.tensor_copy(high[:, :], part_i[:, :]))
                    with v.Fori(0, ET // 2) as t2:
                        for b in range(2):
                            t = t2 * 2 + b
                            v.wait_ge(hot_used, t + (base + 1))
                            v.tensor_tensor(hot_low[:, b, :], iota_b[:, :],
                                            low[:, bass.ds(t, 1)].broadcast_to([P, P]), ALU.is_equal)
                            v.tensor_tensor(hot_high[:, b, 0:NT], iota_b[:, 0:NT],
                                            high[:, bass.ds(t, 1)].broadcast_to([P, NT]), ALU.is_equal).then_inc(hot_ready, 1)
                    v.wait_ge(hot_used, base + ET + 2)
                    link(v.tensor_copy(deg[:, slot, :], ps_hist[:, 0:NT]))
                    v.sem_inc(counted, 1)
                histogram(dst_i, 0, 0)
                histogram(src_i, 1, ET)
                link(v.tensor_scalar(deg[:, 5, :], deg[:, 0, :], 1.0, None, ALU.max))
                link(v.reciprocal(deg[:, 4, :], deg[:, 5, :]))
                link(v.tensor_scalar(deg[:, 2:4, :], deg[:, 0:2, :], 1.0, None, ALU.add))
                link(v.tensor_scalar(bn[:, 0, :], rows[:, 3, :], EPS, None, ALU.add), False)
                v.wait_ge(dve_done, n[0])
                v.sem_inc(roots_asked, 1)
                v.wait_ge(roots_done, 2)
                link(v.reciprocal(deg[:, 2:4, :], roots[:, 0:2 * NT].rearrange("p (a b) -> p a b", a=2)))
                link(v.reciprocal(bn[:, 1, :], roots[:, 64:64 + P]))
                link(v.tensor_tensor(bn[:, 2, :], bn[:, 1, :], rows[:, 0, :], ALU.mult))
                link(v.tensor_tensor(bn[:, 3, :], bn[:, 2, :], rows[:, 2, :], ALU.mult))
                link(v.tensor_tensor(bn[:, 3, :], rows[:, 1, :], bn[:, 3, :], ALU.subtract))
                v.wait_ge(z_ready, 1)
                link(v.tensor_copy(W[:, 3, :], z[:, 0, 0:P]))
                link(v.tensor_copy(W[:, 10, :], z[:, 0, P:2 * P]))
                v.sem_inc(z_free_dve, 1)
                v.wait_ge(z_ready, 2)
                link(v.tensor_copy(WEDGE[0:EK, :, :], z[0:EK, 1, 0:5 * P].rearrange("p (l d) -> p l d", l=5)))
                v.sem_inc(z_free_dve, 1)

                def scale_of(name):
                    return {"dis": 2, "dis2": 3, "inv": 4}[name]

                def each_node(kind):
                    return deg[:, scale_of(kind), :].unsqueeze(2).broadcast_to([P, NT, P])

                def norm(k0, out):
                    for g in range(NG):
                        v.wait_ge(z_ready, k0 + g + 1)
                        sl = slice(g * GT, (g + 1) * GT)
                        link(v.tensor_tensor(Y[:, sl, :], region(k0 + g).rearrange("p (t f) -> p t f", t=GT),
                                             X[:, sl, :], ALU.add))
                        v.sem_inc(z_free_dve, 1)
                    norm_rows(out)

                def norm_rows(out):
                    for j in range(NT):
                        v.bn_stats(stats[:, j, :], Y[:, j, :]).then_inc(dve_done, 1)
                    n[0] += NT
                    v.wait_ge(dve_done, n[0])
                    for j in range(NT):
                        v.bn_aggr(mv[:, j, :], stats[:, j, :]).then_inc(dve_done, 1)
                    n[0] += NT
                    v.wait_ge(dve_done, n[0])
                    link(v.tensor_scalar(sd[:, 0, :], mv[:, :, 1], EPS, None, ALU.add))
                    v.sem_inc(sd_asked, 1)
                    norms[0] += 1
                    v.wait_ge(sd_root, norms[0])
                    link(v.reciprocal(sd[:, 0, :], sd[:, 1, :]))
                    for j in range(NT):
                        v.tensor_scalar(out[:, j, :], Y[:, j, :], mv[:, j, 0:1], sd[:, 0, j:j + 1],
                                        ALU.subtract, ALU.mult).then_inc(dve_done, 1)
                    n[0] += NT
                    v.wait_ge(dve_done, n[0])
                    v.sem_inc(x_ready, 1)

                norms = [0]
                k, z_k = 0, 2
                for s in order:
                    if s[0] == "turn":
                        z_k += NG
                    elif s[0] == "dense":
                        if s[1] in LN_STAGES:
                            if k:
                                v.wait_ge(table_done, 16 * k)
                            norm(z_k, X)
                            if s[1] == 2:
                                link(v.tensor_copy(T[:, :, :], X[:, :, :]))
                                v.sem_inc(t_ready, 1)
                            elif s[1] == 3:
                                link(v.tensor_tensor(T[:, :, :], X[:, :, :], each_node("dis2"), ALU.mult))
                                v.sem_inc(t_ready, 1)
                        else:
                            v.wait_ge(z_free_act, free_count(z_k + NG - 1))
                            if s[1] == 0:
                                link(v.tensor_tensor(T[:, :, :], T[:, :, :], bn[:, 2:3, :].broadcast_to([P, NT, P]), ALU.mult))
                                link(v.tensor_tensor(T[:, :, :], T[:, :, :], bn[:, 3:4, :].broadcast_to([P, NT, P]), ALU.add))
                                link(v.tensor_tensor(T[:, :, :], T[:, :, :], each_node("dis"), ALU.mult))
                            v.sem_inc(t_ready, 1)
                        z_k += NG
                    elif s[0] == "sum":
                        kind = s[1]
                        if kind == ATTR:
                            v.wait_ge(table_done, 16 * k)
                            link(v.tensor_copy(Y[:, :, :], each_node("dis2")))
                            link(v.tensor_copy(T[:, :, :], Y[:, :, :]))
                            v.sem_inc(t_ready, 1)
                        base = n[0]
                        first = k * ET
                        with v.Fori(0, ET) as t:
                            def done(i):
                                v.wait_ge(dve_done, t * TD + (base + i))
                            v.wait_ge(tile_through, t + (first + 1))
                            v.tensor_copy(src_col[:, :], src_i[:, bass.ds(t, 1)]).then_inc(dve_done, 1)
                            v.tensor_copy(row_f[:, :], dst_f[:, bass.ds(t, 1)]).then_inc(dve_done, 1)
                            v.tensor_copy(pay_col[:, 0:EK], attr[:, bass.ds(t, 1), :].rearrange("p o k -> p (o k)")).then_inc(dve_done, 1)
                            v.tensor_copy(pay_col[:, EK:EK + 1], weight[:, bass.ds(t, 1)]).then_inc(dve_done, 1)
                            done(4)
                            v.tensor_scalar(diag[:, :], ident, row_f[:, 0:1], None, ALU.mult).then_inc(dve_done, 1)
                            done(5)
                            v.sem_inc(cols_ready, 1)
                            v.wait_ge(pe_row, t + (first + 1))
                            v.tensor_scalar(same[:, :], ps_row[:, 0:P], row_f[:, 0:1], None, ALU.is_equal).then_inc(dve_done, 1)
                            done(6)
                            v.tensor_tensor_reduce(before[:, :], same[:, :], tril, 1.0, 0.0, ALU.mult, ALU.add,
                                                   n_before[:, :]).then_inc(dve_done, 1)
                            v.wait_ge(pe_pay, t + (first + 1))
                            v.tensor_copy(pay_t[:, :], ps_mul[0:PK, 256:256 + P]).then_inc(pay_ready, 1)
                            done(7)
                            v.tensor_scalar(n_before[:, :], n_before[:, :], 1.0, None, ALU.min).then_inc(dve_done, 1)
                            v.tensor_tensor(to_dump[:, :], dump_row, row_f[:, :], ALU.subtract).then_inc(dve_done, 1)
                            done(9)
                            v.tensor_tensor(to_dump[:, :], to_dump[:, :], n_before[:, :], ALU.mult).then_inc(dve_done, 1)
                            done(10)
                            v.tensor_tensor(row_col[:, :], to_dump[:, :], row_f[:, :], ALU.add).then_inc(dve_done, 1)
                            v.wait_ge(gather_done[k], t * 16 + 16)
                            v.wait_ge(pe_mul, t + (first + 1))
                            v.tensor_tensor(msg[:, :], gathered[:, :], ps_mul[:, 0:P], ALU.mult).then_inc(msg_ready, 1)
                            v.wait_ge(pe_sum, t + (first + 1))
                            v.tensor_copy(joined[:, :], ps_sum[:, 0:P]).then_inc(dve_done, 1)
                            done(12)
                            v.sem_inc(joined_ready, 1)
                        n[0] += TD * ET
                        k += 1
                        v.wait_ge(summed, 16 * k)
                        if kind == PROD:
                            continue
                        if kind == ATTR:
                            link(v.tensor_tensor(AG[:, :, EK:EK + 1], AG[:, :, EK:EK + 1], T[:, :, 0:1], ALU.add))
                        elif s[3]:
                            link(v.tensor_tensor(AG[:, :, :], AG[:, :, :], T[:, :, :], ALU.add))
                        link(v.tensor_tensor(AG[:, :, :], AG[:, :, :], each_node(s[2]), ALU.mult))
                        v.sem_inc(ag_ready, 1)
                    elif s[0] == "final":
                        link(v.tensor_tensor(AG[:, :, :], AG[:, :, :], rows[:, 4:5, :].broadcast_to([P, NT, P]), ALU.add))
                        link(v.tensor_tensor(Y[:, :, :], AG[:, :, :], X[:, :, :], ALU.add))
                        norm_rows(AG)
            v.end_ifs()

        @block.scalar
        def _(act):
            with act.If(wanted(act) == 1):
                act.wait_ge(roots_asked, 1)
                act.activation(roots[:, 0:2 * NT], deg[:, 2:4, :].rearrange("p a b -> p (a b)"), ACT.Sqrt).then_inc(roots_done, 1)
                act.activation(roots[:, 64:64 + P], bn[:, 0, :], ACT.Sqrt).then_inc(roots_done, 1)
                z_k, k, norms = 2, 0, 0
                for s in order:
                    if s[0] == "turn":
                        to = {"PT": PT, "XT": XT, "AUG": AUG}[s[2]]
                        for g in range(NG):
                            act.wait_ge(z_ready, z_k + g + 1)
                            act.copy(to[:, g * GT * P:(g + 1) * GT * P], region(z_k + g)).then_inc(z_free_act, 1)
                        z_k += NG
                    elif s[0] == "dense":
                        st = s[1]
                        if st in LN_STAGES:
                            norms += 1
                            act.wait_ge(sd_asked, norms)
                            act.activation(sd[:, 1, :], sd[:, 0, :], ACT.Sqrt).then_inc(sd_root, 1)
                        else:
                            if k:
                                act.wait_ge(table_done, 16 * k)
                                act.wait_ge(ag_ready, k)
                            for g in range(NG):
                                act.wait_ge(z_ready, z_k + g + 1)
                                for i in range(GT):
                                    j = g * GT + i
                                    scale = 1.0 if st in (0, 9) else deg[:, 2 if st < 3 else 3, j:j + 1]
                                    ins = act.activation(T[:, j, :], tile(z_k + g, i), ACT.Copy if st == 9 else ACT.Relu, scale=scale)
                                ins.then_inc(z_free_act, 1)
                        z_k += NG
                    elif s[0] == "sum":
                        k += 1
                    elif s[0] == "final":
                        norms += 1
                        act.wait_ge(sd_asked, norms)
                        act.activation(sd[:, 1, :], sd[:, 0, :], ACT.Sqrt).then_inc(sd_root, 1)
            act.end_ifs()

        @block.tensor
        def _(pe):
            with pe.If(wanted(pe) == 1):
                pe.sem_inc(hot_used, 2)
                pe.wait_ge(loaded, 16 * len(N_LOADS))
                for h in range(2):
                    pe.matmul(ps_hist[:, 0:NT], zeros[:, :], zeros[:, 0:NT], start=True, stop=False, skip_group_check=True)
                    with pe.Fori(0, ET // 2) as t2:
                        for b in range(2):
                            t = t2 * 2 + b
                            pe.wait_ge(hot_ready, t + (h * ET + 1))
                            pe.matmul(ps_hist[:, 0:NT], hot_low[:, b, :], hot_high[:, b, 0:NT], start=False, stop=False,
                                      skip_group_check=True).then_inc(hot_used, 1)
                    if h == 0:
                        pe.wait_ge(counted, 1)
                pe.transpose(z[:, 0, 0:P], WRAW[:, 0, :], ident)
                pe.transpose(z[:, 0, P:2 * P], WRAW[:, 1, :], ident).then_inc(z_ready, 1)
                for i in range(5):
                    ins = pe.transpose(z[0:EK, 1, i * P:(i + 1) * P], EWR[:, i, :], ident)
                ins.then_inc(z_ready, 1)
                z_k, k, x_n = 2, 0, 0
                ag_k = 0
                last_pt = last_xt = last_aug = 0
                for s in order:
                    if s[0] == "turn":
                        src = {"X": X, "AG": AG}[s[1]]
                        if s[1] == "AG":
                            ag_k += 1
                            pe.wait_ge(ag_ready, ag_k)
                        elif x_n:
                            pe.wait_ge(x_ready, x_n)
                        for g in range(NG):
                            pe.wait_ge(z_free[fills[z_k + g - 2]], free_count(z_k + g - 2))
                            for i in range(GT):
                                ins = pe.transpose(tile(z_k + g, i), src[:, g * GT + i, :], ident)
                            ins.then_inc(z_ready, 1)
                        z_k += NG
                        turned = free_count(z_k - 1)
                    elif s[0] == "dense":
                        st = s[1]
                        pe.wait_ge(z_free_act, turned)
                        if st in LN_STAGES:
                            x_n += 1
                        for g in range(NG):
                            pe.wait_ge(z_free[fills[z_k + g - 2]], free_count(z_k + g - 2))
                            for i in range(GT):
                                c = slice((g * GT + i) * P, (g * GT + i + 1) * P)
                                to = tile(z_k + g, i)
                                ins = pe.matmul(to, PT[:, c], W[:, st, :], start=True, stop=(st == 9))
                                if st == 3:
                                    pe.matmul(to, XT[:, c], W[:, 10, :], start=False, stop=False)
                                if st >= 4 and st < 9:
                                    pe.matmul(to, AUG[0:EK + 1, c], WEDGE[:, st - 4, :], start=False, stop=False)
                                if st < 9:
                                    ins = pe.matmul(to, ones[0:1, :], bias[0:1, st, :], start=False, stop=True)
                            ins.then_inc(z_ready, 1)
                        z_k += NG
                    elif s[0] == "sum":
                        first = k * ET
                        with pe.Fori(0, ET) as t:
                            pe.wait_ge(cols_ready, t + (first + 1))
                            pe.matmul(ps_row[:, 0:P], ones, diag[:, :], start=True, stop=True).then_inc(pe_row, 1)
                            pe.transpose(ps_mul[0:PK, 256:256 + P], pay_col[:, :], ident).then_inc(pe_pay, 1)
                            pe.wait_ge(pay_ready, t + (first + 1))
                            pe.matmul(ps_mul[:, 0:P], pay_t[:, :], sels[:, s[1], :], start=True, stop=True).then_inc(pe_mul, 1)
                            pe.wait_ge(msg_ready, t + (first + 1))
                            pe.matmul(ps_sum[:, 0:P], same[:, :], msg[:, :], start=True, stop=True).then_inc(pe_sum, 1)
                        k += 1
            pe.end_ifs()


def build(nc, a, out):
    with ExitStack() as sems:
        verdict = sems.enter_context(nc.sbuf_tensor("verdict", [1, 1], I32))
        quick_program(nc, a, out, verdict, sems)
        general_program(nc, a, out, verdict, sems)


def host_arrays():
    c_mat, c_sel = host_constants()
    return {"c_mat": c_mat, "c_sel": c_sel, **host_fast()}


_OUT = "out_0_dram"


def kernel(**inputs):
    import concourse.bacc as bacc
    from concourse.bass_utils import run_bass_kernel_spmd

    nc = bacc.Bacc("TRN2", target_bir_lowering=False, num_devices=1)
    arrays, args = {}, {}
    for name, a in {**inputs, **host_arrays()}.items():
        a = np.ascontiguousarray(a)
        arrays[f"in_{name}_dram"] = a
        args[name] = nc.dram_tensor(f"in_{name}_dram", a.shape, mybir.dt.from_np(a.dtype), kind="ExternalInput").ap()
    out = nc.dram_tensor(_OUT, (N, P), F32, kind="ExternalOutput").ap()
    build(nc, args, out)
    return run_bass_kernel_spmd(nc, [arrays], core_ids=[0]).results[0][_OUT]
```

```python
from contextlib import ExitStack

import concourse.bass as bass
from concourse import mybir
import numpy as np

F32 = mybir.dt.float32
BF16 = mybir.dt.bfloat16
FP8 = mybir.dt.float8e4
I32 = mybir.dt.int32
ALU = mybir.AluOpType
ACT = mybir.ActivationFunctionType
AX = mybir.AxisListType

P = 128
N = 3125
NT = -(-N // P)
NP = NT * P
NLAST = N - (NT - 1) * P
E = 103125
EC = E // P
ET = EC + 1
ELAST = E - P * EC
EK = 16
EPS = 1e-5

SLOTS = 64
ROWS = E // SLOTS + 2
PAIRS = (NT + 1) // 2
COLS = PAIRS * P
CB = 8
CA_COUNT = 1
CA_WEIGHT = 2
CG = 16
CLAST = -(-NLAST // (2 * CG)) * 2 * CG
NGRP = ((PAIRS - 1) * P + CLAST) // CG
NBAT = NGRP * CG // CB
U = 8
NU = -(-ET // U)
ELU = E - (NU - 1) * U * P
WIN = 76
UB = 15
USTEP = 31
WOFF = 22
CH = 4
CHUNKS = [(c, min(CH, NT - c)) for c in range(0, NT, CH)]
GROUPS = [slice(a, b) for a, b in ((0, 1), (1, 3), (3, 7), (7, 13), (13, 19), (19, NT))]
NSG = len(GROUPS)


PK = EK + 2
GT = 5
NG = NT // GT
DUMP = NP

LN_STAGES = (2, 3, 8)
NONE, WEIGHT, ATTR, PROD = range(4)


def quick_constants():
    c = np.zeros((P, 4 * P), np.float32)
    c[:, 0:P] = np.eye(P)
    c[:, P:2 * P] = 1.0
    c[:, 2 * P:3 * P] = np.arange(P)[None, :]
    c[:, 3 * P:4 * P] = np.triu(np.ones((P, P)), 1)
    base = np.zeros((1, NU * U), np.float32)
    base[0] = np.repeat(USTEP * np.arange(NU) - WOFF, U)
    return {"c_quick": c, "c_base": base}


def dense_items():
    out = []
    for st, who in (("enc", "act"), ("gcn1", "act"), ("gcn2", "dve"), ("self", "dve")):
        out += [(st, c, w, who) for c, w in CHUNKS]
    out += [("neigh", 2 * q, min(2, NT - 2 * q), "dve") for q in range(PAIRS)]
    for l in range(5):
        out += [(f"edge{l}", c, w, "act" if l < 4 else "dve") for c, w in CHUNKS]
    out += [("last", c, w, "act") for c, w in CHUNKS]
    return out


def quick_program(nc, a, out, verdict, sems):
    with ExitStack() as ctx:
        def sb(name, shape, dt=F32):
            return ctx.enter_context(nc.sbuf_tensor("quick_" + name, shape, dt))

        def sem(name):
            return sems.enter_context(nc.semaphore("quick_" + name))

        const = sb("const", [P, 4 * P])
        ident, ones, iota, below = (const[:, i * P:(i + 1) * P] for i in range(4))
        A8 = sb("A8", [P, NT, NP], FP8)
        X = sb("X", [P, NT, P])
        T = sb("T", [P, NT, P])
        T3 = sb("T3", [P, NT, 3, P], BF16)
        PTc = sb("PTc", [P, 2, CH * P])
        W = sb("W", [P, 11, P])
        WEDGE = sb("WEDGE", [EK + 3, 5, P])
        big = sb("big", [P, 4 * NT * P])
        hot_low = sb("hot_low", [P, 2, CB * P], BF16)
        hot_high = sb("hot_high", [P, 2, 4, CB * NT], BF16)
        iota_b = sb("iota_b", [P, P], BF16)
        ident_b = sb("ident_b", [P, P], BF16)
        src_e = sb("src_e", [P, NU * U], I32)
        rel_e = sb("rel_e", [P, NU * U])
        dis_e = sb("dis_e", [P, NU * U])
        deg = sb("deg", [P, 10, NT])
        offs = sb("offs", [P, 8, NT])
        row_i = sb("row_i", [P, 3, NT], I32)
        stats = sb("stats", [P, NT, 6])
        mv = sb("mv", [P, NT, 2])
        sd = sb("sd", [P, 2, NT])
        flags = sb("flags", [P, 8 + NT])
        idx = sb("idx", [P, 3, U], I32)
        got = sb("got", [P, 3, U])
        zero_b = sb("zero_b", [1, 512], BF16)
        ones_b = sb("ones_b", [P, 1], BF16)
        root = sb("root", [P, 2, NT])

        DEG_IN, DEG_OUT1, DIS, DIS2, INV, DISSQ, DIS2SQ, SQ, SQ2, IN1 = range(10)

        work = A8[:, :, :].rearrange("p j n -> p (j n)")[:, 0:16 * NT * P].bitcast(F32)
        RAW = work[:, 0:2 * NT * P].bitcast(I32).rearrange("p (j s) -> p j s", j=NT)
        RAW_W = work[:, 0:2 * NT * P].rearrange("p (j s) -> p j s", j=NT)[:, :, 2 * SLOTS:4 * SLOTS]
        M1 = work[:, 2 * NT * P:3 * NT * P].rearrange("p (j s) -> p j s", j=NT)
        M2 = work[:, 3 * NT * P:4 * NT * P].rearrange("p (j s) -> p j s", j=NT)
        hist_hot = big[:, 0:3 * U * WIN // 2].bitcast(BF16).rearrange("p (b t w) -> p b t w", b=3, t=U)
        WRAW = big[:, 3800:4056].rearrange("p (b f) -> p b f", b=2)
        EWR = big[:, 4056:4136].rearrange("p (l k) -> p l k", l=5)
        rows = big[:, 4500:4500 + 4 * P].rearrange("p (r f) -> p r f", r=4)
        dst_p = big[:, 5050:5050 + ET].bitcast(I32)
        dst_n = big[:, 5860:5860 + ET].bitcast(I32)
        not_less = big[:, 6670:6670 + ET]
        count_row = big[0:1, 7500:7500 + NP]
        pos_i = big[0:NU, 1000:1000 + 2 * U * P].bitcast(I32).rearrange("p (a c) -> p a c", a=2)
        pos_f = T[0:NU, 0:2 * U, :].rearrange("p (a g) c -> p a (g c)", a=2)
        base = dis_e
        flat = T3[:, :, :, :].rearrange("p a b c -> p (a b c)")[:, 0:5 * 2 * PAIRS * SLOTS].rearrange(
            "p (k j s) -> p k j s", k=5, j=2 * PAIRS)
        wlists = T3[:, :, :, :].rearrange("p a b c -> p (a b c)")[:, 0:5 * COLS].rearrange("p (k m) -> p k m", k=5)
        t3_rest = T3[:, :, :, :].rearrange("p a b c -> p (a b c)")[:, 5 * COLS:]
        n_low = CA_WEIGHT * COLS // CB
        minus_low = t3_rest[:, 0:2 * n_low].bitcast(F32)
        squares = t3_rest[:, 2 * n_low:2 * n_low + CA_WEIGHT * P]
        lists = big[:, 0:5 * COLS // 2].bitcast(BF16).rearrange("p (k m) -> p k m", k=5)
        zero_i = big[0:3, 4200:4200 + 4 * SLOTS].bitcast(I32)
        bias = big[0:1, 11800:11800 + 4 * P].rearrange("p (r f) -> p r f", r=4)
        root_bn = big[:, 11284:11284 + 2 * P].rearrange("p (r f) -> p r f", r=2)
        bn = big[:, 10900:10900 + 3 * P].rearrange("p (r f) -> p r f", r=3)
        sq_row = big[0:1, 4500:4500 + NP]
        scratch = big[:, 7700:7700 + NP].bitcast(BF16).rearrange("p (b n) -> p b n", b=2)
        AW = big[:, :].rearrange("p (b j c) -> p b j c", b=4, j=NT)
        AUG = big[0:EK + 3, 0:NP]
        ea_u = big[:, NP:NP + 3 * P].rearrange("p (b t k) -> p b t k", b=3, t=U)
        eas = big[:, NP + 400:NP + 400 + 3 * 136].rearrange("p (b t k) -> p b t k", b=3, t=U)
        hot_d = big[:, NP + 900:NP + 900 + 3 * U * WIN].rearrange("p (b t w) -> p b t w", b=3, t=U)
        G = big[:, 2 * NP:2 * NP + 3 * U * P].rearrange("p (b t f) -> p b t f", b=3, t=U)
        EWB = big[:, 3 * NP:3 * NP + U * P].rearrange("p (t f) -> p t f", t=U)
        ea_t = big[:, 3 * NP + U * P:3 * NP + (U + 3) * P].rearrange("p (b c) -> p b c", b=3)
        b3_row = big[:, 3 * NP + 1500:3 * NP + 1500 + P]
        sum_t = T[:, :, :].rearrange("p j f -> p (j f)")

        ps = ctx.enter_context(nc.psum_tensor("quick_ps", [P, 8, 512], F32))
        psb = ps[:, :, :].rearrange("p b c -> p (b c)").bitcast(BF16).rearrange("p (b c) -> p b c", b=8)

        rows_d = nc.dram_tensor("quick_rows", [ROWS, 4 * SLOTS], I32).ap()
        dis_d = nc.dram_tensor("quick_dis", [NP, 1], F32).ap()
        roots_d = nc.dram_tensor("quick_roots", [3, NP], F32).ap()
        table_d = nc.dram_tensor("quick_table", [NP, P], F32).ap()
        wlist_d = nc.dram_tensor("quick_wlist", [P, 5, COLS], BF16).ap()

        loaded = sem("loaded")
        filled = sem("filled")
        pads_in = sem("pads_in")
        table_in = sem("table_in")
        pos_in = sem("pos_in")
        dst_in = sem("dst_in")
        pos_ready = sem("pos_ready")
        pos_turned = sem("pos_turned")
        turned_taken = sem("turned_taken")
        hist_ready = sem("hist_ready")
        hist_used = sem("hist_used")
        row_counted = sem("row_counted")
        ptr_ready = sem("ptr_ready")
        ptr_go = sem("ptr_go")
        w_turned = sem("w_turned")
        root_asked = sem("root_asked")
        root_done = sem("root_done")
        dve_done = sem("dve_done")
        rows_ready = sem("rows_ready")
        lists_in = sem("lists_in")
        flat_ready = sem("flat_ready")
        turn_ready = sem("turn_ready")
        turn_taken = sem("turn_taken")
        wl_out = sem("wl_out")
        wl_in = sem("wl_in")
        lows_ready = sem("lows_ready")
        squared = sem("squared")
        low_ready = sem("low_ready")
        high_ready = sem("high_ready")
        hot_ready = sem("hot_ready")
        hot_used = sem("hot_used")
        grp_free = sem("grp_free")
        adj_ready = sem("adj_ready")
        out_counted = sem("out_counted")
        out_taken = sem("out_taken")
        sums_in = sem("sums_in")
        max_free = sem("max_free")
        sq_out = sem("sq_out")
        sq_in = sem("sq_in")
        dis_out = sem("dis_out")
        row_in = sem("row_in")
        p_ready = sem("p_ready")
        pt_ready = sem("pt_ready")
        z_ready = sem("z_ready")
        z_free_act = sem("z_free_act")
        z_free_dve = sem("z_free_dve")
        hi_ready = sem("hi_ready")
        r_ready = sem("r_ready")
        mid_ready = sem("mid_ready")
        t3_ready = sem("t3_ready")
        x_ready = sem("x_ready")
        ea_taken = sem("ea_taken")
        dis_e_ready = sem("dis_e_ready")
        eas_ready = sem("eas_ready")
        unit_used = sem("unit_used")
        aug_ready = sem("aug_ready")
        aug_rows = sem("aug_rows")
        ewb_zero = sem("ewb_zero")
        idx_ready = sem("idx_ready")
        xw_out = sem("xw_out")
        et_ready = sem("et_ready")
        et_in = sem("et_in")
        e_ready = sem("e_ready")
        hotd_ready = sem("hotd_ready")
        msg_ready = sem("msg_ready")
        gathered_used = sem("gathered_used")
        sum_taken = sem("sum_taken")
        sum_done = sem("sum_done")
        out_ready = sem("out_ready")
        stored = sem("stored")
        flag_go = sem("flag_go")
        flag_mm = sem("flag_mm")
        flag_ready = sem("flag_ready")
        pool_turn = sem("pool_turn")
        scr = sem("scr")
        ea_in = [sem(f"ea_in{r}") for r in range(3)]
        dis_got = [sem(f"dis_got{r}") for r in range(3)]
        rows_got = [sem(f"rows_got{r}") for r in range(3)]

        items = dense_items()
        NI = len(items)
        first_item, item_count, place = {}, {}, []
        for k, it in enumerate(items):
            first_item.setdefault(it[0], k)
            place.append(item_count.get(it[0], 0))
            item_count[it[0]] = place[-1] + 1

        def z_taken(k):
            who = items[k][3]
            return {"act": z_free_act, "dve": z_free_dve}[who], sum(i[3] == who for i in items[:k + 1])

        def before(k):
            return max((i for i in range(k) if place[i] % 2 == place[k] % 2), default=None)

        STAGES = list(first_item)
        SPLITS = ["gcn1", "gcn2", "edge0", "edge1", "edge2", "edge3", "edge4"]
        SOURCE = {"gcn1": "enc", "gcn2": "gcn1", "edge0": "neigh", "edge1": "edge0", "edge2": "edge1",
                  "edge3": "edge2", "edge4": "edge3"}

        def p_bank(k):
            return ps[:, place[k] % 2, :]

        def z_bank(k):
            return ps[:, 2 + place[k] % 2, :]

        def tiles_done_act(st):
            return sum(item_count[s] for s in STAGES[:STAGES.index(st) + 1] if items[first_item[s]][3] == "act")

        LOADED = [0]
        block = ctx.enter_context(nc.Block())

        @block.sync
        def _(sp):
            def load(dst, src, arrived=loaded):
                LOADED[0] += arrived is loaded
                return sp.dma_start(dst, src).then_inc(arrived, 16)

            load(const[:, :], a["c_quick"], pos_in)
            load(base[:, :], a["c_base"].broadcast_to([P, NU * U]), pos_in)
            sp.wait_ge(filled, 1)
            for k, n in ((1, "dst"), (0, "src")):
                load(pos_i[0:NU - 1, k, :], a[n][0:(NU - 1) * U * P].rearrange("(u c) -> u c", c=U * P), pos_in)
                load(pos_i[NU - 1:NU, k, 0:ELU], a[n][(NU - 1) * U * P:E].rearrange("(o c) -> o c", o=1), pos_in)
            load(dst_p[:, 0:EC], a["dst"][0:P * EC].rearrange("(p t) -> p t", t=EC), dst_in)
            load(dst_p[0:ELAST, EC:ET], a["dst"][P * EC:E].rearrange("(p o) -> p o", o=1), dst_in)
            load(dst_n[:, 0:EC], a["dst"][1:P * EC + 1].rearrange("(p t) -> p t", t=EC), dst_in)
            load(dst_n[0:ELAST - 1, EC:ET], a["dst"][P * EC + 1:E].rearrange("(p o) -> p o", o=1), dst_in)
            load(X[:, 0:NT - 1, :], a["x"][0:(NT - 1) * P, :].rearrange("(j p) f -> p j f", p=P))
            load(X[0:NLAST, NT - 1, :], a["x"][(NT - 1) * P:N, :])
            for i, n in enumerate(("L0_gnn_W_enc", "L0_gnn_W1", "L0_gnn_W2")):
                load(W[:, i, :], a[n])
            load(W[:, 4:9, :], a["L2_gnn_weights"].rearrange("l a b -> a l b"))
            load(W[:, 9, :], a["L3_gnn_W"])
            load(WRAW[:, 0, :], a["L1_gnn_W_neigh"])
            load(WRAW[:, 1, :], a["L1_gnn_W_self"])
            load(EWR[:, :, :], a["L2_gnn_edge_ws"].rearrange("l d e -> d l e"))
            load(WEDGE[EK:EK + 1, :, :], a["L2_gnn_edge_bs"].rearrange("(o l) d -> o l d", o=1))
            load(WEDGE[EK + 1:EK + 2, :, :], a["L2_gnn_biases"].rearrange("(o l) d -> o l d", o=1))
            load(WEDGE[EK + 2:EK + 3, :, :], a["L2_gnn_edge_bs"].rearrange("(o l) d -> o l d", o=1))
            for i, n in enumerate(("L0_gnn_b_enc", "L0_gnn_b1", "L0_gnn_b2", "L1_gnn_b_self")):
                load(bias[:, i, :], a[n].rearrange("(o d) -> o d", o=1))
            for i, n in enumerate(("L0_gnn_bn_gamma", "L0_gnn_bn_beta", "L0_gnn_bn_mean", "L0_gnn_bn_var")):
                load(rows[:, i, :], a[n].rearrange("(o d) -> o d", o=1).broadcast_to([P, P]))
            n_full = E // SLOTS
            rest = E - n_full * SLOTS
            src_d = a["src"]
            w_d = a["edge_weight"].bitcast(I32)
            load(rows_d[n_full - 1:ROWS, :], zero_i[:, :], pads_in)
            sp.wait_ge(pads_in, 16)
            for col, d in ((0, src_d), (2 * SLOTS, w_d)):
                load(rows_d[0:n_full, col:col + SLOTS], d[0:n_full * SLOTS].rearrange("(r s) -> r s", s=SLOTS), table_in)
                load(rows_d[0:n_full - 1, col + SLOTS:col + 2 * SLOTS],
                     d[SLOTS:n_full * SLOTS].rearrange("(r s) -> r s", s=SLOTS), table_in)
                tail = d[n_full * SLOTS:E].rearrange("(o s) -> o s", o=1)
                load(rows_d[n_full:n_full + 1, col:col + rest], tail, table_in)
                load(rows_d[n_full - 1:n_full, col + SLOTS:col + SLOTS + rest], tail, table_in)
            sp.wait_ge(sq_out, 1)
            sp.dma_start(roots_d[0:1, :].rearrange("o (j p) -> p (o j)", p=P), deg[:, SQ, :],
                         allow_slow_non_contiguous=True).then_inc(sq_in, 16)
            sp.wait_ge(sq_in, 16)
            sp.wait_ge(turn_taken, 10)
            sp.dma_start(sq_row, roots_d[0:1, :]).then_inc(sq_in, 16)
            sp.dma_start(wlist_d[:, :, :], lists[:, :, :]).then_inc(wl_out, 16)
            sp.wait_ge(dis_out, 1)
            sp.dma_start(dis_d.rearrange("(j p) o -> p (j o)", p=P), deg[:, DIS2, :],
                         allow_slow_non_contiguous=True).then_inc(row_in, 16)
            sp.dma_start(roots_d[1:2, :].rearrange("o (j p) -> p (o j)", p=P), deg[:, SQ2, :],
                         allow_slow_non_contiguous=True).then_inc(row_in, 16)
            sp.dma_start(roots_d[2:3, :].rearrange("o (j p) -> p (o j)", p=P), deg[:, DIS2, :],
                         allow_slow_non_contiguous=True).then_inc(row_in, 16)
            sp.wait_ge(p_ready, first_item["gcn2"] + item_count["gcn2"])
            sp.wait_ge(wl_out, 16)
            sp.dma_start(wlists[:, :, :], wlist_d[:, :, :]).then_inc(wl_in, 16)
            sp.wait_ge(p_ready, first_item["neigh"] + item_count["neigh"])
            sp.wait_ge(row_in, 48)
            sp.dma_start(AUG[EK + 1:EK + 3, :], roots_d[1:3, :]).then_inc(aug_rows, 16)
            sp.dma_start(b3_row, a["L3_gnn_b"].rearrange("(o d) -> o d", o=1).broadcast_to([P, P])).then_inc(aug_rows, 16)

            ea_d = a["edge_attr_16"]

            def unit(u, r, taken):
                sp.wait_ge(ea_taken, taken)
                sp.dma_start(ea_u[:, r, :, :], ea_d[bass.ds(u * (U * P), U * P), :].rearrange(
                    "(p t) k -> p t k", p=P)).then_inc(ea_in[r], 16)

            def all_units(base):
                with sp.Fori(0, NU // 3) as i:
                    for r in range(3):
                        unit(i * 3 + r, r, i * 3 + (r + 1 + base))
                unit(NU - 2, 0, NU - 2 + 1 + base)
                sp.wait_ge(ea_taken, NU + base)
                first, full = (NU - 1) * U * P, ELU // U
                sp.dma_start(ea_u[0:full, 1, :, :], ea_d[first:first + full * U, :].rearrange(
                    "(p t) k -> p t k", t=U)).then_inc(ea_in[1], 16)
                sp.dma_start(ea_u[full:full + 1, 1, 0:ELU - full * U, :], ea_d[first + full * U:E, :].rearrange(
                    "(p t) k -> p t k", p=1)).then_inc(ea_in[1], 16)

            all_units(0)
            sp.wait_ge(ewb_zero, 1)
            for t in range(U):
                sp.dma_start(EWB[t * EK:(t + 1) * EK, t, :], a["L3_gnn_edge_w"]).then_inc(ewb_zero, 16)
            for k in range(first_item["last"], NI):
                c, w = items[k][1:3]
                sp.wait_ge(*z_taken(k))
                sp.dma_start(table_d[c * P:(c + w) * P, :].rearrange("(j p) f -> p j f", p=P),
                             T[:, c:c + w, :]).then_inc(xw_out, 16)
            sp.wait_ge(ea_taken, NU + 3)
            all_units(NU)
            sp.wait_ge(out_ready, 1)
            sp.dma_start(out[0:(NT - 1) * P, :].rearrange("(j p) f -> p j f", p=P),
                         X[:, 0:NT - 1, :]).then_inc(stored, 16)
            sp.dma_start(out[(NT - 1) * P:N, :], X[0:NLAST, NT - 1, :]).then_inc(stored, 16)
            sp.wait_ge(stored, 32)

        def wide(ap, n):
            return ap.unsqueeze(2).broadcast_to([ap.shape[0], ap.shape[1], n])

        def windows():
            step, over = USTEP * UB, WIN - USTEP
            copies, adds = [], []
            for b in range(-(-NU // UB)):
                lo = over if b else WOFF
                hi = min(step + over, NP - (step * b - WOFF))
                copies.append((b, lo, hi, step * b - WOFF + lo))
                if b:
                    adds.append((b, 0, over, step * b - WOFF))
            return copies, adds

        @block.gpsimd
        def _(pool):
            turns = [0]

            def fetch(k, r, u, out_of, table, arrived):
                pool.tensor_copy(idx[:, r, :], src_e[:, bass.ds(u * U, U)]).then_inc(pool_turn, 1)
                pool.wait_ge(pool_turn, k)
                gather(r, out_of, table, arrived)

            def gather(r, out_of, table, arrived):
                pool.sem_inc(scr, 1)
                for t in range(U):
                    pool.indirect_dma_start(out=out_of(r, t), out_offset=None, in_=table[:, :],
                                            in_offset=bass.IndirectOffsetOnAxis(ap=idx[:, r, t:t + 1], axis=0)
                                            ).then_inc(arrived[r], 16)

            pool.wait_ge(rows_ready, 1)
            pool.wait_ge(table_in, 8 * 16)
            for j in range(NT):
                pool.indirect_dma_start(out=RAW[:, j, :], out_offset=None, in_=rows_d[:, :],
                                        in_offset=bass.IndirectOffsetOnAxis(ap=row_i[:, 1, j:j + 1], axis=0)
                                        ).then_inc(lists_in, 16)
            pool.wait_ge(row_in, 48)
            pool.wait_ge(turned_taken, 1)

            def keep(r, u, n):
                pool.wait_ge(dis_got[r], n)
                pool.tensor_copy(dis_e[:, bass.ds(u * U, U)], got[:, r, :]).then_inc(dis_e_ready, 1)

            fetch(1, 0, 0, lambda r, t: got[:, r, t:t + 1], dis_d, dis_got)
            with pool.Fori(0, NU // 3) as i:
                for d in (1, 2, 3):
                    u = i * 3 + d
                    fetch(i * 3 + (d + 1), d % 3, u, lambda r, t: got[:, r, t:t + 1], dis_d, dis_got)
                    keep((d - 1) % 3, i * 3 + (d - 1), i * (16 * U) + 16 * U)
            fetch(NU, (NU - 1) % 3, NU - 1, lambda r, t: got[:, r, t:t + 1], dis_d, dis_got)
            keep((NU - 2) % 3, NU - 2, 16 * U * ((NU - 2) // 3 + 1))
            keep((NU - 1) % 3, NU - 1, 16 * U * ((NU - 1) // 3 + 1))
            pool.wait_ge(xw_out, 16 * item_count["last"])

            def rows_of(r, k):
                pool.wait_ge(gathered_used, k)
                pool.wait_ge(idx_ready, k)
                gather(r, lambda r, t: G[:, r, t, :], table_d, rows_got)

            with pool.Fori(0, NU // 3) as i:
                for r in range(3):
                    rows_of(r, i * 3 + (r + 1))
            rows_of(0, NU - 1)
            rows_of(1, NU)

        @block.vector
        def _(v):
            n = [0]

            def link(ins, wait=True):
                n[0] += 1
                ins.then_inc(dve_done, 1)
                if wait:
                    v.wait_ge(dve_done, n[0])

            tt, ts = v.tensor_tensor, v.tensor_scalar
            link(v.memset(dst_p[:, EC:ET], NP), False)
            link(v.memset(dst_n[:, EC:ET], NP), False)
            link(v.memset(pos_i[96:NU, 0, :], 0), False)
            link(v.memset(pos_i[96:NU, 1, :], -1000), False)
            link(v.memset(ones_b[:, :], 1.0), False)
            link(v.memset(zero_i[:, :], 0), False)
            link(v.memset(zero_b[:, :], 0.0), False)
            link(v.memset(deg[:, :, :], 1.0), False)
            link(v.memset(X[:, NT - 1, :], 0.0))
            v.sem_inc(filled, 1)
            v.sem_inc(ea_taken, 3)
            v.wait_ge(pos_in, 6 * 16)
            link(v.tensor_copy(pos_f[:, 1, :], pos_i[:, 1, :]))
            v.sem_inc(pos_ready, 1)
            link(v.tensor_copy(pos_f[:, 0, :], pos_i[:, 0, :]))
            v.sem_inc(pos_ready, 1)
            v.wait_ge(pos_turned, 1)

            def units_of(ap, half):
                return ap.rearrange("p (u t) -> p t u", t=U)[:, 4 * half:4 * half + 4, :]

            def turned(a_i, half):
                return ps[:, 4 + 2 * a_i + half, :].rearrange("p (t u) -> p t u", t=4)[:, :, 0:NU]

            for half in range(2):
                link(tt(units_of(rel_e[:, :], half), turned(1, half), units_of(base[:, :], half), ALU.subtract), False)
            v.wait_ge(pos_turned, 2)
            for half in range(2):
                link(v.tensor_copy(units_of(src_e[:, :], half), turned(0, half)), half == 1)
            v.sem_inc(turned_taken, 1)

            def window_of(to, u):
                return tt(to, iota[:, 0:WIN].unsqueeze(1).broadcast_to([P, U, WIN]),
                          wide(rel_e[:, bass.ds(u * U, U)], WIN), ALU.is_equal)

            def hist_unit(u, r, k):
                v.wait_ge(hist_used, k)
                window_of(hist_hot[:, r, :, :], u).then_inc(hist_ready, 1)

            with v.Fori(0, NU // 3) as i:
                for r in range(3):
                    hist_unit(i * 3 + r, r, i * 3 + (r + 1))
            hist_unit(NU - 2, 0, NU - 1)
            hist_unit(NU - 1, 1, NU)
            v.wait_ge(hist_used, NU + 3)
            copies, adds = windows()
            for b, lo, hi, node in copies:
                link(v.tensor_copy(count_row[:, node:node + hi - lo], ps[0:1, b, lo:hi]), False)
            v.wait_ge(dve_done, n[0])
            for b, lo, hi, node in adds:
                link(tt(count_row[:, node:node + hi - lo], count_row[:, node:node + hi - lo], ps[0:1, b, lo:hi], ALU.add), False)
            v.wait_ge(dve_done, n[0])
            v.sem_inc(row_counted, 1)
            v.wait_ge(dst_in, 64)
            link(tt(not_less[:, :], dst_n[:, :], dst_p[:, :], ALU.is_lt))
            link(v.memset(flags[:, 2:8], 0.0), False)
            link(v.tensor_reduce(flags[:, 0:1], not_less[:, :], AX.X, ALU.max), False)
            v.wait_ge(loaded, LOADED[0] * 16)
            link(v.tensor_copy(iota_b[:, :], iota), False)
            link(v.tensor_copy(ident_b[:, :], ident))
            v.wait_ge(ptr_ready, 1)
            link(v.tensor_copy(deg[:, DEG_IN, :], ps[:, 4, 0:NT]))
            v.sem_inc(ptr_go, 1)
            link(v.tensor_reduce(flags[:, 1:2], deg[:, DEG_IN, :], AX.X, ALU.max), False)
            link(ts(deg[:, IN1, :], deg[:, DEG_IN, :], 1.0, None, ALU.add))
            link(ts(deg[:, INV, :], deg[:, DEG_IN, :], 1.0, None, ALU.max))
            link(v.reciprocal(deg[:, INV, :], deg[:, INV, :]), False)
            link(v.reciprocal(deg[:, DISSQ, :], deg[:, IN1, :]), False)
            link(v.tensor_copy(root[:, 0, 0:NT], deg[:, IN1, :]), False)
            link(ts(root_bn[:, 0, :], rows[:, 3, :], EPS, None, ALU.add))
            v.sem_inc(root_asked, 1)
            v.wait_ge(ptr_ready, 2)
            link(v.tensor_copy(offs[:, 0, :], ps[:, 4, 64:64 + NT]), False)
            link(v.tensor_copy(offs[:, 1, :], ps[:, 4, 32:32 + NT]))
            link(tt(offs[:, 1, :], offs[:, 1, :], offs[:, 0, :], ALU.subtract))
            cur, nxt = 0, 2
            for sh in (1, 2, 4, 8, 16):
                link(v.tensor_copy(offs[:, nxt, 0:sh], offs[:, cur, 0:sh]), False)
                link(tt(offs[:, nxt, sh:NT], offs[:, cur, sh:NT], offs[:, cur, 0:NT - sh], ALU.add))
                cur, nxt = nxt, cur
            link(tt(offs[:, 3, :], offs[:, cur, :], offs[:, 1, :], ALU.add))
            link(ts(flags[:, 2:3], offs[:, cur, NT - 1:NT], float(E), None, ALU.is_lt), False)
            link(v.tensor_copy(row_i[:, 0, :], offs[:, 3, :]))
            link(ts(row_i[:, 1, :], row_i[:, 0, :], 6, None, ALU.logical_shift_right), False)
            link(ts(row_i[:, 2, :], row_i[:, 0, :], SLOTS - 1, None, ALU.bitwise_and))
            link(v.tensor_copy(offs[:, 4, :], row_i[:, 2, :]))
            link(tt(offs[:, 5, :], offs[:, 4, :], deg[:, DEG_IN, :], ALU.add))
            v.wait_ge(w_turned, 1)
            link(v.tensor_copy(W[:, 3, :], ps[:, 5, 0:P]), False)
            link(v.tensor_copy(W[:, 10, :], ps[:, 5, P:2 * P]), False)
            link(v.tensor_copy(WEDGE[0:EK, 0:4, :], ps[0:EK, 6, :].rearrange("p (l d) -> p l d", l=4)), False)
            link(v.tensor_copy(WEDGE[0:EK, 4, :], ps[0:EK, 7, 0:P]))
            v.wait_ge(root_done, 1)
            link(v.tensor_copy(deg[:, SQ, :], root[:, 1, 0:NT]), False)
            link(v.reciprocal(deg[:, DIS, :], root[:, 1, 0:NT]), False)
            link(v.reciprocal(bn[:, 0, :], root_bn[:, 1, :]))
            link(tt(bn[:, 1, :], bn[:, 0, :], rows[:, 0, :], ALU.mult))
            link(tt(bn[:, 2, :], bn[:, 1, :], rows[:, 2, :], ALU.mult))
            link(tt(bn[:, 2, :], rows[:, 1, :], bn[:, 2, :], ALU.subtract))
            v.sem_inc(rows_ready, 1)
            v.sem_inc(sq_out, 1)
            v.wait_ge(z_free_act, tiles_done_act("enc"))
            link(tt(T[:, :, :], T[:, :, :], bn[:, 1:2, :].broadcast_to([P, NT, P]), ALU.mult))
            link(tt(T[:, :, :], T[:, :, :], bn[:, 2:3, :].broadcast_to([P, NT, P]), ALU.add))
            link(tt(T[:, :, :], T[:, :, :], wide(deg[:, DIS, :], P), ALU.mult))
            v.sem_inc(x_ready, 1)

            spread = iota.unsqueeze(1).broadcast_to([P, NT, P])
            link(tt(M1, spread, wide(offs[:, 4, :], P), ALU.is_ge), False)
            link(tt(M2, spread, wide(offs[:, 5, :], P), ALU.is_lt))
            link(tt(M1, M1, M2, ALU.mult))
            v.wait_ge(lists_in, NT * 16)
            link(v.scalar_tensor_tensor(out=M2, in0=RAW[:, :, 0:2 * SLOTS], scalar=1.0, in1=M1, op0=ALU.add, op1=ALU.mult))
            one, two = M2[:, :, 0:SLOTS], M2[:, :, SLOTS:2 * SLOTS]
            link(tt(one, one, two, ALU.add))
            link(ts(two.bitcast(I32), one, -1.0, None, ALU.add))
            link(v.memset(flat[:, :, NT, :], 0.0), False)
            link(ts(one.bitcast(I32), two.bitcast(I32), P - 1, None, ALU.bitwise_and))
            link(v.tensor_copy(flat[:, 0, 0:NT, :], one.bitcast(I32)))
            link(ts(one.bitcast(I32), two.bitcast(I32), 7, None, ALU.arith_shift_right))
            link(v.tensor_copy(flat[:, 1, 0:NT, :], one.bitcast(I32)))
            link(v.memset(flat[:, 1, NT, :], -1.0))
            v.sem_inc(flat_ready, 1)
            link(tt(M2, RAW_W, M1, ALU.mult))
            link(tt(one, one, two, ALU.add))
            link(v.tensor_copy(flat[:, 2, 0:NT, :], one))
            link(tt(two, one, flat[:, 2, 0:NT, :], ALU.subtract))
            link(v.tensor_copy(flat[:, 3, 0:NT, :], two))
            link(tt(flat[:, 4, 0:NT, :], two, flat[:, 3, 0:NT, :], ALU.subtract))
            v.sem_inc(flat_ready, 1)

            def low_hot(b, m, lists, n_c):
                return tt(hot_low[:, b, 0:n_c * P].rearrange("p (c l) -> p c l", c=n_c),
                          iota_b[:, :].unsqueeze(1).broadcast_to([P, n_c, P]),
                          wide(lists[:, 0, bass.ds(m, n_c)], P), ALU.is_equal)

            def high_hot(b, m, lists=lists):
                return tt(hot_high[:, b, 0, :].rearrange("p (c j) -> p c j", c=CB),
                          iota_b[:, 0:NT].unsqueeze(1).broadcast_to([P, CB, NT]),
                          wide(lists[:, 1, bass.ds(m, CB)], NT), ALU.is_equal)

            A8_words = A8[:, :, :].rearrange("p j n -> p (j n)").bitcast(I32).rearrange("p (j n) -> p j n", j=NT)
            link(v.memset(A8_words[:, :, ((NT - 1) * P + CLAST) // 4:], 0))
            v.wait_ge(turn_taken, 4)
            with v.Fori(0, NBAT // 2) as i:
                for b in range(2):
                    v.wait_ge(hot_used, i * 2 + (b + 1))
                    low_hot(b, (i * 2 + b) * CB, lists, CB - CA_COUNT)
                    high_hot(b, (i * 2 + b) * CB).then_inc(hot_ready, 1)
            v.wait_ge(out_counted, 1)
            v.wait_ge(hot_used, NBAT + 2)
            link(ts(deg[:, DEG_OUT1, :], ps[:, 0, 0:NT], 1.0, None, ALU.add))
            v.sem_inc(out_taken, 1)
            link(v.tensor_copy(root[:, 0, 0:NT], deg[:, DEG_OUT1, :]))
            v.sem_inc(root_asked, 1)
            v.wait_ge(grp_free, NGRP + 2)
            for j in range(NT):
                tt(A8[:, j, j * P:(j + 1) * P], A8[:, j, j * P:(j + 1) * P], ident_b[:, :], ALU.add, saturate=False).then_inc(adj_ready, 1)

            def split(st):
                base = SPLITS.index(st) * NSG

                def rest(g):
                    v.wait_ge(hi_ready, base + g + 1)
                    sl = GROUPS[g]
                    tt(T[:, sl, :], T[:, sl, :], T3[:, sl, 0, :], ALU.subtract).then_inc(r_ready, 1)

                def last(g):
                    v.wait_ge(mid_ready, base + g + 1)
                    sl = GROUPS[g]
                    tt(T3[:, sl, 2, :], T[:, sl, :], T3[:, sl, 1, :], ALU.subtract).then_inc(t3_ready, 1)

                for g in range(NSG):
                    rest(g)
                    if g:
                        last(g - 1)
                last(NSG - 1)

            def take(st, scale, tiles=None):
                for k in range(first_item[st], first_item[st] + item_count[st]):
                    if tiles is not None and k != tiles:
                        continue
                    c, w = items[k][1:3]
                    v.wait_ge(z_ready, k + 1)
                    for i in range(w):
                        ins = v.scalar_tensor_tensor(out=X[:, c + i, :], in0=z_bank(k)[:, i * P:(i + 1) * P],
                                                     scalar=deg[:, scale, c + i:c + i + 1], in1=X[:, c + i, :],
                                                     op0=ALU.mult, op1=ALU.add)
                    ins.then_inc(z_free_dve, 1)
                    v.wait_ge(*z_taken(k))
                    stats_of(c, w)

            def stats_of(c, w):
                for i in range(w):
                    ins = v.bn_stats(stats[:, c + i, :], X[:, c + i, :])
                link(ins)
                for i in range(w):
                    ins = v.bn_aggr(mv[:, c + i, :], stats[:, c + i, :])
                link(ins, False)

            roots = [2]

            def norm(out_t):
                v.wait_ge(dve_done, n[0])
                link(ts(root[:, 0, 0:NT], mv[:, :, 1], EPS, None, ALU.add))
                v.sem_inc(root_asked, 1)
                roots[0] += 1
                v.wait_ge(root_done, roots[0])
                link(v.reciprocal(sd[:, 0, :], root[:, 1, 0:NT]))
                for j in range(NT):
                    ins = ts(out_t[:, j, :], X[:, j, :], mv[:, j, 0:1], sd[:, 0, j:j + 1], ALU.subtract, ALU.mult)
                link(ins)

            link(v.reciprocal(deg[:, DIS2SQ, :], deg[:, DEG_OUT1, :]), False)
            v.wait_ge(root_done, 2)
            link(v.tensor_copy(deg[:, SQ2, :], root[:, 1, 0:NT]), False)
            link(v.reciprocal(deg[:, DIS2, :], root[:, 1, 0:NT]))
            v.sem_inc(dis_out, 1)
            split("gcn1")
            for j in range(NT):
                v.wait_ge(sums_in, j + 1)
                v.tensor_reduce(flags[:, 8 + j:9 + j], scratch[:, j % 2, 0:N], AX.X, ALU.max).then_inc(max_free, 1)
            v.wait_ge(max_free, NT)
            split("gcn2")
            take("gcn2", DIS)
            norm(T)
            v.sem_inc(x_ready, 1)
            for k in range(first_item["self"], first_item["self"] + item_count["self"]):
                c, w = items[k][1:3]
                v.wait_ge(z_ready, k + 1)
                tt(X[:, c:c + w, :], z_bank(k)[:, 0:w * P].rearrange("p (t f) -> p t f", t=w), T[:, c:c + w, :],
                   ALU.add).then_inc(z_free_dve, 1)
            v.wait_ge(wl_in, 16)
            done0 = NBAT
            for q in range(PAIRS):
                with v.Fori(0, (CLAST if q == PAIRS - 1 else P) // CB // 2) as i:
                    for b in range(2):
                        at = i * 2 + (b + q * (P // CB))
                        m = (i * 2 + b) * CB + q * P
                        v.wait_ge(hot_used, i * 2 + (b + q * (P // CB) + done0 + 1))
                        high_hot(b, m, wlists).then_inc(high_ready, 1)
                        low_hot(b, m, wlists, CB - CA_WEIGHT)
                        v.wait_ge(high_ready, i * 2 + (b + q * (P // CB) + 1))
                        tt(hot_high[:, b, 1:4, :].rearrange("p k (c j) -> p k c j", c=CB),
                           hot_high[:, b, 0:1, :].rearrange("p k (c j) -> p k c j", c=CB).broadcast_to([P, 3, CB, NT]),
                           wlists[:, 2:5, bass.ds(m, CB)].unsqueeze(3).broadcast_to([P, 3, CB, NT]),
                           ALU.mult).then_inc(hot_ready, 1)
                if q > 1:
                    take("neigh", INV, first_item["neigh"] + q - 2)
            for q in (PAIRS - 2, PAIRS - 1):
                take("neigh", INV, first_item["neigh"] + q)
            norm(X)
            link(tt(T[:, :, :], X[:, :, :], wide(deg[:, DIS2, :], P), ALU.mult))
            v.sem_inc(x_ready, 1)

            v.wait_ge(aug_rows, 32)
            link(v.memset(EWB[:, :, :], 0.0))
            v.sem_inc(ewb_zero, 1)

            def windows_of_unit(u, r):
                return window_of(hot_d[:, r, :, :], u)

            def attr_unit(u, r, k, got_n):
                v.wait_ge(ea_in[r], got_n)
                v.wait_ge(dis_e_ready, k)
                v.wait_ge(unit_used, k)
                tt(eas[:, r, :, 0:EK], ea_u[:, r, :, :], wide(dis_e[:, bass.ds(u * U, U)], EK), ALU.mult).then_inc(ea_taken, 1)
                v.tensor_copy(eas[:, r, :, EK], dis_e[:, bass.ds(u * U, U)])
                windows_of_unit(u, r).then_inc(eas_ready, 1)

            with v.Fori(0, NU // 3) as i:
                for r in range(3):
                    attr_unit(i * 3 + r, r, i * 3 + (r + 1), i * 16 + 16)
            attr_unit(NU - 2, 0, NU - 1, 16 * (NU // 3 + 1))
            attr_unit(NU - 1, 1, NU, 16 * (NU // 3) + 32)
            v.wait_ge(unit_used, NU + 3)
            for b, lo, hi, node in copies:
                link(v.tensor_copy(AUG[0:EK + 1, node:node + hi - lo], ps[0:EK + 1, b, lo:hi]), False)
            v.wait_ge(dve_done, n[0])
            for b, lo, hi, node in adds:
                link(tt(AUG[0:EK + 1, node:node + hi - lo], AUG[0:EK + 1, node:node + hi - lo], ps[0:EK + 1, b, lo:hi], ALU.add), False)
            v.wait_ge(dve_done, n[0])
            v.sem_inc(aug_ready, 1)

            for l in range(5):
                split(f"edge{l}")
            take("edge4", DIS2)
            norm(X)
            v.sem_inc(x_ready, 1)
            link(ts(flags[:, 5:6], flags[:, 1:2], float(SLOTS), None, ALU.is_gt))
            link(ts(flags[:, 8:8 + NT], flags[:, 8:8 + NT], 15.0, None, ALU.is_gt))
            link(v.memset(flags[:, 1:2], 0.0))
            link(v.tensor_reduce(sd[:, 1, 0:1], flags[:, :], AX.X, ALU.max))
            v.sem_inc(flag_go, 1)
            v.wait_ge(flag_mm, 1)
            link(ts(verdict[0:1, 0:1], ps[0:1, 4, 0:1], 0.0, None, ALU.is_gt))
            v.sem_inc(flag_ready, 1)
            v.wait_ge(pt_ready, NI)
            link(tt(X[:, :, :], X[:, :, :], b3_row.unsqueeze(1).broadcast_to([P, NT, P]), ALU.add))
            v.sem_inc(msg_ready, 1)

            v.wait_ge(dis_e_ready, NU)
            for r in range(3):
                v.tensor_copy(idx[:, r, :], src_e[:, r * U:(r + 1) * U]).then_inc(idx_ready, 1)

            def product_unit(u, r, k, k2, got_n, more=True):
                v.wait_ge(gathered_used, k)
                windows_of_unit(u, r).then_inc(hotd_ready, 1)
                v.wait_ge(rows_got[r], got_n)
                if more:
                    v.tensor_copy(idx[:, r, :], src_e[:, bass.ds((u + 3) * U, U)]).then_inc(idx_ready, 1)
                for h in range(2):
                    v.wait_ge(e_ready, k2 + h)
                    sl = G[:, r, 4 * h:4 * h + 4, :]
                    tt(sl, sl, ps[:, 7, :].rearrange("p (t f) -> p t f", t=4), ALU.mult).then_inc(msg_ready, 1)
                    if h == 0:
                        v.sem_inc(ea_taken, 1)

            with v.Fori(0, NU // 3 - 1) as i:
                for r in range(3):
                    product_unit(i * 3 + r, r, i * 3 + (r + 1), i * 6 + (2 * r + 1), i * (16 * U) + 16 * U)
            for u in range(NU // 3 * 3 - 3, NU):
                product_unit(u, u % 3, u + 1, 2 * u + 1, 16 * U * (u // 3 + 1), more=u + 3 < NU)
            v.wait_ge(gathered_used, NU + 3)
            for b, lo, hi, node in copies:
                link(v.tensor_copy(sum_t[:, node:node + hi - lo], ps[:, b, lo:hi]), False)
            v.wait_ge(dve_done, n[0])
            for b, lo, hi, node in adds:
                link(tt(sum_t[:, node:node + hi - lo], sum_t[:, node:node + hi - lo], ps[:, b, lo:hi], ALU.add), False)
            v.wait_ge(dve_done, n[0])
            v.sem_inc(sum_taken, 1)
            for m, (c, w) in enumerate(CHUNKS):
                v.wait_ge(sum_done, m + 1)
                link(tt(X[:, c:c + w, :], X[:, c:c + w, :], ps[:, m, 0:w * P].rearrange("p (t f) -> p t f", t=w), ALU.add))
                stats_of(c, w)
            norm(X)
            v.sem_inc(out_ready, 1)

        @block.scalar
        def _(act):
            def root_of():
                roots[0] += 1
                act.wait_ge(root_asked, roots[0])
                if roots[0] == 1:
                    act.activation(root_bn[:, 1, :], root_bn[:, 0, :], ACT.Sqrt)
                act.activation(root[:, 1, :], root[:, 0, :], ACT.Sqrt).then_inc(root_done, 1)

            def move(k):
                act.wait_ge(p_ready, k + 1)
                if before(k) is not None:
                    act.wait_ge(z_ready, before(k) + 1)
                w = items[k][2] * P
                act.copy(PTc[:, place[k] % 2, 0:w], p_bank(k)[:, 0:w]).then_inc(pt_ready, 1)

            def take(k):
                st, c, w, _ = items[k]
                act.wait_ge(z_ready, k + 1)
                scale = {"gcn1": DISSQ}.get(st, DIS2SQ)
                if st in ("enc", "last"):
                    ins = act.activation(T[:, c:c + w, :].rearrange("p t f -> p (t f)"), z_bank(k)[:, 0:w * P],
                                         ACT.Relu if st == "enc" else ACT.Copy)
                    ins.then_inc(z_free_act, 1)
                else:
                    for i in range(w):
                        ins = act.activation(T[:, c + i, :], z_bank(k)[:, i * P:(i + 1) * P], ACT.Relu,
                                             scale=deg[:, scale, c + i:c + i + 1])
                    ins.then_inc(z_free_act, 1)

            def stage(st, extra=None):
                ks = range(first_item[st], first_item[st] + item_count[st])
                for k in ks:
                    move(k)
                    if items[k][3] == "act" and k > ks[0]:
                        take(k - 1)
                    if extra:
                        extra(k - ks[0])
                if items[ks[-1]][3] == "act":
                    take(ks[-1])

            def split(st):
                base = SPLITS.index(st) * NSG
                src_st = SOURCE[st]
                if src_st == "enc":
                    act.wait_ge(x_ready, 1)
                    act.wait_ge(turn_taken, 10)
                elif src_st == "neigh":
                    act.wait_ge(x_ready, 3)
                else:
                    act.wait_ge(*z_taken(first_item[src_st] + item_count[src_st] - 1))
                for g in range(NSG):
                    sl = GROUPS[g]
                    act.copy(T3[:, sl, 0, :], T[:, sl, :]).then_inc(hi_ready, 1)
                    if g:
                        mid(base, g - 1)
                mid(base, NSG - 1)

            def mid(base, g):
                sl = GROUPS[g]
                act.wait_ge(r_ready, base + g + 1)
                act.copy(T3[:, sl, 1, :], T[:, sl, :]).then_inc(mid_ready, 1)

            roots = [0]
            act.sem_inc(grp_free, 2)
            root_of()
            stage("enc")
            for m in range(10):
                k, half = m // 2, m % 2
                w = (8 if half == 0 else PAIRS - 8) * P
                act.wait_ge(turn_ready, m + 1)
                to = lists[:, k, half * 8 * P:half * 8 * P + w]
                act.copy(to, psb[:, 4 + m % 4, 0:w]).then_inc(turn_taken, 1)

            def from_group(g, out_a, out_b, **narrow):
                for h, to in enumerate((out_a, out_b)):
                    if to is not None:
                        ins = act.activation(to, ps[:, 4 + 2 * g + h, 0:CG * NT].rearrange("p (c j) -> p j c", c=CG),
                                             ACT.Copy, **narrow)
                ins.then_inc(grp_free, 1)

            def minus_lows(lists, ca):
                theirs = lists[:, 0, :].rearrange("p (m c) -> p m c", c=CB)[:, :, CB - ca:CB]
                lows[0] += 1
                act.activation(minus_low[:, 0:ca * COLS // CB].rearrange("p (m c) -> p m c", c=ca), theirs, ACT.Copy,
                               scale=-1.0).then_inc(lows_ready, 1)
                act.wait_ge(lows_ready, lows[0])

            def low_hots(k, b, m, ca):
                act.wait_ge(hot_used, k + 1)
                act.wait_ge(low_ready, k + 1)
                for c in range(ca):
                    ins = act.activation(squares[:, c * P:(c + 1) * P], iota_b[:, :], ACT.Square,
                                         bias=minus_low[:, bass.ds(m * ca + c, 1)])
                ins.then_inc(squared, 1)
                act.wait_ge(squared, k + 1)
                act.activation(hot_low[:, b, (CB - ca) * P:], squares[:, 0:ca * P], ACT.Relu, bias=ones[:, 0:1],
                               scale=-1.0).then_inc(low_ready, 1)

            lows = [0]
            act.sem_inc(low_ready, 1)
            minus_lows(lists, CA_COUNT)
            low_hots(0, 0, 0, CA_COUNT)
            low_hots(1, 1, 1, CA_COUNT)
            for m in range(NGRP):
                q, g = m // (P // CG), m % 2
                col = q * 2 * P + m % (P // CG) * CG
                second = None if q == PAIRS - 1 else A8[:, :, col + P:col + P + CG]
                for b in range(2 if m + 1 < NGRP else 0):
                    low_hots(2 * m + 2 + b, b, 2 * m + 2 + b, CA_COUNT)
                act.wait_ge(hot_used, 2 * m + 2 + 2)
                from_group(g, A8[:, :, col:col + CG], second, saturate=False)
            root_of()
            split("gcn1")

            def row_copies(i):
                for j in range(4 * i, min(4 * i + 4, NT)):
                    act.wait_ge(adj_ready, NT)
                    if j >= 2:
                        act.wait_ge(max_free, j - 1)
                    act.copy(scratch[:, j % 2, 0:N], A8[:, j, 0:N]).then_inc(sums_in, 1)

            stage("gcn1", row_copies)
            split("gcn2")
            stage("gcn2")
            root_of()
            stage("self")
            act.wait_ge(wl_in, 16)
            k0 = first_item["neigh"]
            act.wait_ge(z_ready, k0)

            def sums_out(q, par, w):
                act.wait_ge(p_ready, q + (k0 + 1))
                act.wait_ge(z_ready, q + (k0 - 1))
                act.copy(PTc[:, par, 0:w * P], p_bank(k0 + par)[:, 0:w * P]).then_inc(pt_ready, 1)

            def pair_out(q, par, follow, last=False):
                n_g = CLAST // CG if last else P // CG
                for g in range(n_g):
                    if follow and g == n_g - 1:
                        sums_out(q - 1, 1 - par, 2)
                    if not (last and g == n_g - 1):
                        for b in range(2):
                            m = q * (P // CB) + (2 * g + 2 + b)
                            low_hots(m + NBAT, b, m, CA_WEIGHT)
                    act.wait_ge(hot_used, q * (P // CB) + (2 * g + 2 + 2 + NBAT))
                    from_group(g % 2, AW[:, 2 * par, :, g * CG:(g + 1) * CG], AW[:, 2 * par + 1, :, g * CG:(g + 1) * CG])

            minus_lows(wlists, CA_WEIGHT)
            low_hots(NBAT, 0, 0, CA_WEIGHT)
            low_hots(NBAT + 1, 1, 1, CA_WEIGHT)
            pair_out(0, 0, False)
            with act.Fori(0, (PAIRS - 1) // 2 - 1) as i:
                pair_out(i * 2 + 1, 1, True)
                pair_out(i * 2 + 2, 0, True)
            pair_out(PAIRS - 2, 1, True)
            pair_out(PAIRS - 1, 0, True, last=True)
            sums_out(PAIRS - 1, 0, NT - 2 * (PAIRS - 1))
            root_of()
            for l in range(5):
                split(f"edge{l}")
                stage(f"edge{l}")
            root_of()
            stage("last")

            def turn_unit(r, k):
                act.wait_ge(et_ready, k)
                act.copy(ea_t[:, r, :], ps[:, 7, 0:P]).then_inc(et_in, 1)

            with act.Fori(0, NU // 3) as i:
                for r in range(3):
                    turn_unit(r, i * 3 + (r + 1))
            turn_unit(0, NU - 1)
            turn_unit(1, NU)
            root_of()

        @block.tensor
        def _(pe):
            mm = pe.matmul
            pe.sem_inc(hist_used, 3)
            pe.sem_inc(hot_used, 2)
            pe.sem_inc(unit_used, 3)
            pe.sem_inc(gathered_used, 3)

            def zero_bank(b):
                return mm(ps[:, b, :], zero_b[0:1, 0:P], zero_b[0:1, :], start=True, stop=False, skip_group_check=True)

            def by_bank(unit):
                for b in range(-(-NU // UB)):
                    m = min(UB, NU - b * UB)
                    with pe.Fori(0, m // 3) as i:
                        for r in range(3):
                            unit(b, i * (3 * USTEP) + r * USTEP, r, i * 3 + (b * UB + r), i)
                    for r in range(m % 3):
                        unit(b, (m // 3 * 3 + r) * USTEP, r, b * UB + m // 3 * 3 + r, None)

            for a_i in (1, 0):
                pe.wait_ge(pos_ready, 2 - a_i)
                by_tile = pos_f[:, a_i, :].rearrange("p (c t) -> p t c", t=U)
                for t in range(U):
                    ins = pe.transpose(ps[:, 4 + 2 * a_i + t // 4, (t % 4) * P:(t % 4) * P + NU], by_tile[:, t, :],
                                       ident[0:NU, 0:NU])
                ins.then_inc(pos_turned, 1)
            pe.wait_ge(turned_taken, 1)
            for b in range(7):
                zero_bank(b)

            def hist_unit(b, col, r, u, _):
                pe.wait_ge(hist_ready, u + 1)
                for t in range(U):
                    ins = mm(ps[0:1, b, bass.ds(col, WIN)], ones_b[:, :], hist_hot[:, r, t, :],
                             start=False, stop=False, skip_group_check=True)
                ins.then_inc(hist_used, 1)

            by_bank(hist_unit)
            pe.wait_ge(row_counted, 1)
            for j in range(NT):
                ins = mm(ps[:, 4, j:j + 1], count_row[:, j * P:(j + 1) * P], ones[0:1, 0:1], start=True, stop=True)
            ins.then_inc(ptr_ready, 1)
            pe.wait_ge(loaded, LOADED[0] * 16)
            pe.transpose(ps[:, 5, 0:P], WRAW[:, 0, :], ident)
            pe.transpose(ps[:, 5, P:2 * P], WRAW[:, 1, :], ident)
            for l in range(5):
                ins = pe.transpose(ps[0:EK, 6 + l // 4, (l % 4) * P:(l % 4 + 1) * P], EWR[:, l, :], ident)
            ins.then_inc(w_turned, 1)
            pe.wait_ge(ptr_go, 1)
            mm(ps[:, 4, 32:32 + NT], below, deg[:, DEG_IN, :], start=True, stop=True)
            mm(ps[:, 4, 64:64 + NT], ones, deg[:, DEG_IN, :], start=True, stop=True).then_inc(ptr_ready, 1)

            def product(k):
                st, c, w, _ = items[k]
                pe.wait_ge(pt_ready, k + 1)
                if before(k) is not None:
                    pe.wait_ge(*z_taken(before(k)))
                if st == "edge0" and place[k] == 0:
                    pe.wait_ge(aug_rows, 32)
                for i in range(w):
                    to = z_bank(k)[:, i * P:(i + 1) * P]
                    rows_in = PTc[:, place[k] % 2, i * P:(i + 1) * P]
                    nodes = slice((c + i) * P, (c + i + 1) * P)
                    wi = {"enc": 0, "gcn1": 1, "gcn2": 2, "neigh": 3, "self": 10, "last": 9}.get(st)
                    if wi is None:
                        wi = 4 + int(st[4:])
                    alone = st in ("neigh", "last")
                    ins = mm(to, rows_in, W[:, wi, :], start=True, stop=alone)
                    if st in ("enc", "self"):
                        ins = mm(to, ones[0:1, :], bias[:, 0 if st == "enc" else 3, :], start=False, stop=True)
                    elif st in ("gcn1", "gcn2"):
                        ins = mm(to, sq_row[:, nodes], bias[:, wi, :], start=False, stop=True)
                    elif not alone:
                        ins = mm(to, AUG[:, nodes], WEDGE[:, wi - 4, :], start=False, stop=True)
                ins.then_inc(z_ready, 1)

            def buffers_free(k):
                if before(k) is not None:
                    pe.wait_ge(pt_ready, before(k) + 1)

            def turn(k, src):
                _, c, w, _ = items[k]
                buffers_free(k)
                for i in range(w):
                    ins = pe.transpose(p_bank(k)[:, i * P:(i + 1) * P], src[:, c + i, :], ident)
                ins.then_inc(p_ready, 1)

            def spread(k):
                st, c, w, _ = items[k]
                buffers_free(k)
                for j in range(NT):
                    if place[k] == 0:
                        for g, tiles in enumerate(GROUPS):
                            if tiles.start == j:
                                pe.wait_ge(t3_ready, SPLITS.index(st) * NSG + g + 1)
                    for part in range(3):
                        ins = mm(p_bank(k)[:, 0:w * P], T3[:, j, part, :], A8[:, j, c * P:(c + w) * P],
                                 start=(j == 0 and part == 0), stop=(j == NT - 1 and part == 2))
                ins.then_inc(p_ready, 1)

            def stage(st, fill):
                ks = range(first_item[st], first_item[st] + item_count[st])
                for k in ks:
                    fill(k)
                    if k > ks[0]:
                        product(k - 1)
                product(ks[-1])

            stage("enc", lambda k: turn(k, X))
            for m in range(10):
                k, half = m // 2, m % 2
                if m in (0, 4):
                    pe.wait_ge(flat_ready, 1 + m // 4)
                if m >= 4:
                    pe.wait_ge(turn_taken, m - 3)
                for q in range(8 * half, min(8 * half + 8, PAIRS)):
                    ins = pe.transpose(psb[:, 4 + m % 4, (q % 8) * P:(q % 8 + 1) * P],
                                       flat[:, k, 2 * q:2 * q + 2, :].rearrange("p j s -> p (j s)"), ident_b[:, :])
                ins.then_inc(turn_ready, 1)
            pe.wait_ge(turn_taken, 10)

            def group(g, b0, first, parts):
                pe.wait_ge(grp_free, first)
                for b in range(2):
                    pe.wait_ge(hot_ready, b0 + b)
                    pe.wait_ge(low_ready, b0 + b + 1)
                    for c in range(CB):
                        at = (b * CB + c) * NT
                        for h in range(2):
                            sl = slice(h * SLOTS, (h + 1) * SLOTS)
                            for n_p, part in enumerate(parts):
                                ins = mm(ps[:, 4 + 2 * g + h, at:at + NT], hot_low[sl, b, c * P:(c + 1) * P],
                                         hot_high[sl, b, part, c * NT:(c + 1) * NT],
                                         start=(n_p == 0), stop=(n_p == len(parts) - 1))
                        if parts == (0,):
                            ins = mm(ps[:, 0, 0:NT], hot_low[:, b, c * P:(c + 1) * P],
                                     hot_high[:, b, 0, c * NT:(c + 1) * NT], start=False, stop=False,
                                     skip_group_check=True)
                    ins.then_inc(hot_used, 1)

            pe.wait_ge(pt_ready, first_item["enc"] + item_count["enc"])
            zero_bank(0)
            with pe.Fori(0, NGRP // 2) as i:
                for g in range(2):
                    group(g, i * 4 + (2 * g + 1), i * 2 + (g + 1), (0,))
            pe.sem_inc(out_counted, 1)
            pe.wait_ge(adj_ready, NT)
            pe.wait_ge(out_taken, 1)
            pe.wait_ge(sq_in, 32)
            stage("gcn1", spread)
            stage("gcn2", spread)
            pe.wait_ge(x_ready, 2)
            stage("self", lambda k: turn(k, T))

            k0 = first_item["neigh"]

            def neigh(par, w, js):
                for j in js:
                    for i in range(w):
                        ins = mm(p_bank(k0 + par)[:, i * P:(i + 1) * P], T[:, j, :], AW[:, 2 * par + i, j, :],
                                 start=False, stop=False, skip_group_check=True)
                return ins

            def neigh_start(q, par, last=False):
                pe.wait_ge(grp_free, 2 * NGRP + 2 if last else q * (P // CG) + (NGRP + P // CG + 2))
                pe.wait_ge(pt_ready, q + (k0 - 1))
                zero_bank(par)

            def neigh_product(q, par, w):
                pe.wait_ge(pt_ready, q + (k0 + 1))
                pe.wait_ge(z_free_dve, q + (z_taken(k0 - 1)[1] - 1))
                for i in range(w):
                    ins = mm(z_bank(k0 + par)[:, i * P:(i + 1) * P], PTc[:, par, i * P:(i + 1) * P], W[:, 3, :],
                             start=True, stop=True)
                ins.then_inc(z_ready, 1)

            def pair_groups(q, par, follow, n_g=P // CG):
                done = 0
                for g in range(n_g):
                    group(g % 2, q * (P // CB) + (2 * g + 1 + NBAT), q * (P // CG) + (g + 1 + NGRP), (1, 2, 3))
                    if follow and g < n_g - 1:
                        if g == 0:
                            neigh_start(q - 1, 1 - par)
                        upto = -(-NT * (g + 1) // (n_g - 1))
                        ins = neigh(1 - par, 2, range(done, upto))
                        done = upto
                        if upto == NT:
                            ins.then_inc(p_ready, 1)
                if follow:
                    neigh_product(q - 1, 1 - par, 2)

            pe.wait_ge(pt_ready, k0)
            pe.wait_ge(*z_taken(k0 - 1))
            pair_groups(0, 0, False)
            with pe.Fori(0, (PAIRS - 1) // 2 - 1) as i:
                pair_groups(i * 2 + 1, 1, True)
                pair_groups(i * 2 + 2, 0, True)
            pair_groups(PAIRS - 2, 1, True)
            pair_groups(PAIRS - 1, 0, True, CLAST // CG)
            w_last = NT - 2 * (PAIRS - 1)
            neigh_start(PAIRS - 1, 0, last=True)
            neigh(0, w_last, range(NT)).then_inc(p_ready, 1)
            neigh_product(PAIRS - 1, 0, w_last)

            pe.wait_ge(x_ready, 3)
            pe.wait_ge(grp_free, 2 * NGRP + 2)
            for b in range(7):
                zero_bank(b)

            def attr_unit(b, col, r, u, _):
                pe.wait_ge(eas_ready, u + 1)
                for t in range(U):
                    ins = mm(ps[0:EK + 1, b, bass.ds(col, WIN)], eas[:, r, t, :], hot_d[:, r, t, :],
                             start=False, stop=False, skip_group_check=True)
                ins.then_inc(unit_used, 1)

            by_bank(attr_unit)
            pe.wait_ge(aug_ready, 1)
            for l in range(5):
                stage(f"edge{l}", spread)
            pe.wait_ge(x_ready, 4)
            stage("last", lambda k: turn(k, X))
            pe.wait_ge(flag_go, 1)
            mm(ps[0:1, 4, 0:1], sd[:, 1, 0:1], ones[:, 0:1], start=True, stop=True).then_inc(flag_mm, 1)
            pe.wait_ge(flag_ready, 1)
            pe.wait_ge(*z_taken(NI - 1))
            pe.wait_ge(ewb_zero, 1 + 16 * U)
            for b in range(7):
                zero_bank(b)
            per_ring = [16 * 34, 16 * 33 + 32, 16 * 33]

            def product_unit(b, col, r, u, i):
                if i is None:
                    pe.wait_ge(ea_in[r], per_ring[r] + (16 * (u // 3) + 16 if u < NU - 1 else 16 * (u // 3) + 32))
                else:
                    pe.wait_ge(ea_in[r], i * 16 + (per_ring[r] + 16 + 16 * (b * UB // 3)))
                pe.wait_ge(msg_ready, u * 2 + 1)
                pe.transpose(ps[:, 7, 0:P], ea_u[:, r, :, :].rearrange("p t k -> p (t k)"), ident).then_inc(et_ready, 1)
                pe.wait_ge(et_in, u + 1)
                for h in range(2):
                    if h:
                        pe.wait_ge(msg_ready, u * 2 + 2)
                    for t in range(4):
                        ins = mm(ps[:, 7, t * P:(t + 1) * P], ea_t[:, r, :], EWB[:, 4 * h + t, :], start=True, stop=True)
                    ins.then_inc(e_ready, 1)
                pe.wait_ge(hotd_ready, u + 1)
                for t in range(U):
                    if t == 4:
                        pe.wait_ge(msg_ready, u * 2 + 3)
                    ins = mm(ps[:, b, bass.ds(col, WIN)], G[:, r, t, :], hot_d[:, r, t, :],
                             start=False, stop=False, skip_group_check=True)
                ins.then_inc(gathered_used, 1)

            by_bank(product_unit)
            pe.wait_ge(sum_taken, 1)
            for m, (c, w) in enumerate(CHUNKS):
                for i in range(w):
                    ins = pe.transpose(ps[:, m, i * P:(i + 1) * P], sum_t[:, (c + i) * P:(c + i + 1) * P], ident)
                ins.then_inc(sum_done, 1)


def steps():
    out = [("turn", "X", "PT"), ("dense", 0)]
    for st, kind, scale, loop in ((1, NONE, "dis", True), (2, NONE, "dis", True)):
        out += [("sum", kind, scale, loop), ("turn", "AG", "PT"), ("dense", st)]
    out += [("turn", "X", "XT"), ("sum", WEIGHT, "inv", False), ("turn", "AG", "PT")]
    out += [("sum", ATTR, "dis2", False), ("turn", "AG", "AUG"), ("dense", 3)]
    for st in range(4, 9):
        out += [("sum", NONE, "dis2", True), ("turn", "AG", "PT"), ("dense", st)]
    out += [("turn", "X", "PT"), ("dense", 9), ("sum", PROD, None, False), ("final",)]
    return out


def general_constants():
    c = np.zeros((P, 4 * P + 1), np.float32)
    c[:, 0:P] = np.eye(P)
    c[:, P:2 * P] = 1.0
    c[:, 2 * P:3 * P] = np.arange(P)[None, :]
    c[:, 3 * P:4 * P] = np.tril(np.ones((P, P)), -1)
    c[:, 4 * P] = np.arange(P) + DUMP
    s = np.zeros((PK, 3, P), np.float32)
    s[EK + 1, NONE, :] = 1.0
    s[EK, WEIGHT, :] = 1.0
    s[:EK, ATTR, :EK] = np.eye(EK)
    s[EK + 1, ATTR, EK] = 1.0
    return c, s


def general_program(nc, a, out, verdict, sems):
    with ExitStack() as ctx:
        def sb(name, shape, dt=F32):
            return ctx.enter_context(nc.sbuf_tensor(name, shape, dt))

        def sem(name):
            return sems.enter_context(nc.semaphore(name))

        const = sb("const", [P, 4 * P + 1])
        ident, ones, iota, tril = (const[:, i * P:(i + 1) * P] for i in range(4))
        dump_row = const[:, 4 * P:4 * P + 1]
        sels = sb("sels", [PK, 4, P])
        X = sb("X", [P, NT, P])
        T = sb("T", [P, NT, P])
        AG = sb("AG", [P, NT, P])
        Y = sb("Y", [P, NT, P])
        PT = sb("PT", [P, NP])
        XT = sb("XT", [P, NP])
        AUG = sb("AUG", [P, NP])
        W = sb("W", [P, 11, P])
        WRAW = sb("WRAW", [P, 2, P])
        EWR = sb("EWR", [P, 5, EK])
        WEDGE = sb("WEDGE", [EK + 1, 5, P])
        bias = sb("bias", [1, 10, P])
        rows = sb("rows", [P, 5, P])
        bn = sb("bn", [P, 4, P])
        src_i = sb("src_i", [P, ET], I32)
        dst_i = sb("dst_i", [P, ET], I32)
        part_i = sb("part_i", [P, ET], I32)
        dst_f = sb("dst_f", [P, ET])
        low = sb("low", [P, ET], BF16)
        high = sb("high", [P, ET], BF16)
        weight = sb("weight", [P, ET])
        attr = sb("attr", [P, ET, EK])
        deg = sb("deg", [P, 6, NT])
        hot_low = sb("hot_low", [P, 2, P], BF16)
        hot_high = sb("hot_high", [P, 2, 32], BF16)
        iota_b = sb("iota_b", [P, P], BF16)
        src_col = sb("src_col", [P, 1], I32)
        pay_col = sb("pay_col", [P, PK])
        diag = sb("diag", [P, P])
        same = sb("same", [P, P])
        before = sb("before", [P, P])
        n_before = sb("n_before", [P, 1])
        to_dump = sb("to_dump", [P, 1])
        row_f = sb("row_f", [P, 1])
        row_col = sb("row_col", [P, 1], I32)
        pay_t = sb("pay_t", [PK, P])
        gathered = sb("gathered", [P, P])
        msg = sb("msg", [P, P])
        joined = sb("joined", [P, P])
        zeros = sb("zeros", [P, P])
        stats = sb("stats", [P, NT, 6])
        mv = sb("mv", [P, NT, 2])
        sd = sb("sd", [P, 2, NT])
        roots = sb("roots", [P, 256])

        z = ctx.enter_context(nc.psum_tensor("z", [P, 2, 2 * 512], F32))
        ps_hist = ctx.enter_context(nc.psum_tensor("ps_hist", [P, 512], F32))
        ps_row = ctx.enter_context(nc.psum_tensor("ps_row", [P, 512], F32))
        ps_mul = ctx.enter_context(nc.psum_tensor("ps_mul", [P, 512], F32))
        ps_sum = ctx.enter_context(nc.psum_tensor("ps_sum", [P, 512], F32))

        table = nc.dram_tensor("table", [NP, P], F32).ap()
        sums = nc.dram_tensor("sums", [NP + P, P], F32).ap()

        loaded = sem("loaded")
        x_loaded = sem("x_loaded")
        dve_done = sem("dve_done")
        act_done = sem("act_done")
        z_ready = sem("z_ready")
        z_free_act = sem("z_free_act")
        z_free_dve = sem("z_free_dve")
        hot_ready = sem("hot_ready")
        hot_used = sem("hot_used")
        pe_row = sem("pe_row")
        pe_pay = sem("pe_pay")
        pe_mul = sem("pe_mul")
        pe_sum = sem("pe_sum")
        cols_ready = sem("cols_ready")
        pay_ready = sem("pay_ready")
        same_ready = sem("same_ready")
        msg_ready = sem("msg_ready")
        joined_ready = sem("joined_ready")
        stored = sem("stored")
        roots_asked = sem("roots_asked")
        counted = sem("counted")
        tile_through = sem("tile_through")
        pool_turn = sem("pool_turn")
        roots_done = sem("roots_done")
        sd_asked = sem("sd_asked")
        sd_root = sem("sd_root")

        order = steps()
        n_sums = sum(s[0] == "sum" for s in order)
        gather_done = [sem(f"gather_done{i}") for i in range(n_sums)]
        scatter_done = [sem(f"scatter_done{i}") for i in range(n_sums)]
        table_done = sem("table_done")
        zeroed = sem("zeroed")
        summed = sem("summed")
        t_ready = sem("t_ready")
        ag_ready = sem("ag_ready")
        x_ready = sem("x_ready")

        fills = ["dve"] * 2
        for s in order:
            if s[0] == "turn":
                fills += ["act"] * NG
            elif s[0] == "dense":
                fills += (["dve"] if s[1] in LN_STAGES else ["act"]) * NG

        def free_count(k):
            return sum(f == fills[k] for f in fills[:k + 1])

        z_free = {"act": z_free_act, "dve": z_free_dve}

        def tile(k, i):
            return z[:, k % 2, i * P:(i + 1) * P]

        def region(k):
            return z[:, k % 2, 0:GT * P]

        ag_turned = []
        kk = 2
        for s in order:
            if s[0] == "turn":
                kk += NG
                if s[1] == "AG":
                    ag_turned.append(free_count(kk - 1))
            elif s[0] == "dense":
                kk += NG

        block = ctx.enter_context(nc.Block())
        N_LOADS = []

        def wanted(engine):
            return engine.value_load(verdict[0:1, 0:1], min_val=0, max_val=1)

        @block.sync
        def _(sp):
            with sp.If(wanted(sp) == 1):
                def load(dst, src, s=loaded):
                    sp.dma_start(dst, src).then_inc(s, 16)
                    if s is loaded:
                        N_LOADS.append(1)
                load(const[:, :], a["c_general"])
                load(sels[:, 0:3, :], a["c_sel"])
                for i, n in enumerate(("L0_gnn_W_enc", "L0_gnn_W1", "L0_gnn_W2")):
                    load(W[:, i, :], a[n])
                load(W[:, 4:9, :], a["L2_gnn_weights"].rearrange("l a b -> a l b"))
                load(W[:, 9, :], a["L3_gnn_W"])
                load(WRAW[:, 0, :], a["L1_gnn_W_neigh"])
                load(WRAW[:, 1, :], a["L1_gnn_W_self"])
                load(EWR[:, :, :], a["L2_gnn_edge_ws"].rearrange("l d e -> d l e"))
                load(WEDGE[EK:EK + 1, :, :], a["L2_gnn_edge_bs"].rearrange("(o l) d -> o l d", o=1))
                for i, n in ((0, "L0_gnn_b_enc"), (1, "L0_gnn_b1"), (2, "L0_gnn_b2"), (3, "L1_gnn_b_self")):
                    load(bias[:, i, :], a[n].rearrange("(o d) -> o d", o=1))
                load(bias[:, 4:9, :], a["L2_gnn_biases"].rearrange("(o l) d -> o l d", o=1))
                for i, n in enumerate(("L0_gnn_bn_gamma", "L0_gnn_bn_beta", "L0_gnn_bn_mean", "L0_gnn_bn_var", "L3_gnn_b")):
                    load(rows[:, i, :], a[n].rearrange("(o d) -> o d", o=1).broadcast_to([P, P]))
                sp.wait_ge(dve_done, 8)
                load(X[:, 0:NT - 1, :], a["x"][0:(NT - 1) * P, :].rearrange("(j p) f -> p j f", p=P))
                load(X[0:NLAST, NT - 1, :], a["x"][(NT - 1) * P:N, :])
                load(sels[0:EK, PROD, :], a["L3_gnn_edge_w"])
                for dst, name in ((src_i, "src"), (dst_i, "dst"), (weight, "edge_weight")):
                    load(dst[:, 0:EC], a[name][0:P * EC].rearrange("(p t) -> p t", t=EC))
                    load(dst[0:ELAST, EC:ET], a[name][P * EC:E].rearrange("(p o) -> p o", o=1))
                attr_d = a["edge_attr_16"]
                load(attr[:, 0:EC, :], attr_d[0:P * EC, :].rearrange("(p t) k -> p t k", t=EC))
                load(attr[0:ELAST, EC, :], attr_d[P * EC:E, :])
                k = 0
                for s in order:
                    if s[0] == "sum":
                        sp.wait_ge(t_ready, k + 1)
                        if k:
                            sp.wait_ge(summed, 16 * k)
                        sp.dma_start(table.rearrange("(j p) f -> p j f", p=P), T[:, :, :]).then_inc(table_done, 16)
                        sp.dma_start(sums.rearrange("(j p) f -> p j f", p=P),
                                     zeros[:, :].unsqueeze(1).broadcast_to([P, NT + 1, P])).then_inc(zeroed, 16)
                        sp.wait_ge(scatter_done[k], 16 * ET)
                        if k:
                            sp.wait_ge(ag_ready, k)
                            sp.wait_ge(z_free_act, ag_turned[k - 1])
                        sp.dma_start(AG[:, :, :], sums[0:NP, :].rearrange("(j p) f -> p j f", p=P)).then_inc(summed, 16)
                        k += 1
                sp.wait_ge(x_ready, 4)
                sp.dma_start(out[0:(NT - 1) * P, :].rearrange("(j p) f -> p j f", p=P),
                             AG[:, 0:NT - 1, :]).then_inc(stored, 16)
                sp.dma_start(out[(NT - 1) * P:N, :], AG[0:NLAST, NT - 1, :]).then_inc(stored, 16)
                sp.wait_ge(stored, 32)
            sp.end_ifs()

        @block.gpsimd
        def _(pool):
            with pool.If(wanted(pool) == 1):
                pool.sem_inc(tile_through, 1)
                k = 0
                for s in order:
                    if s[0] != "sum":
                        continue
                    with pool.Fori(0, ET) as t:
                        pool.wait_ge(cols_ready, t + (k * ET + 1))
                        pool.sem_inc(pool_turn, 1)
                        pool.wait_ge(table_done, 16 * (k + 1))
                        pool.indirect_dma_start(
                            out=gathered[:, :], out_offset=None, in_=table[:, :],
                            in_offset=bass.IndirectOffsetOnAxis(ap=src_col[:, 0:1], axis=0)).then_inc(gather_done[k], 16)
                        pool.wait_ge(joined_ready, t + (k * ET + 1))
                        pool.sem_inc(pool_turn, 1)
                        pool.wait_ge(zeroed, 16 * (k + 1))
                        pool.indirect_dma_start(
                            out=sums[:, :], out_offset=bass.IndirectOffsetOnAxis(ap=row_col[:, 0:1], axis=0),
                            in_=joined[:, :], in_offset=None, compute_op=ALU.add).then_inc(scatter_done[k], 16)
                        pool.wait_ge(scatter_done[k], t * 16 + 16)
                        pool.sem_inc(tile_through, 1)
                    k += 1
            pool.end_ifs()

        TD = 12

        @block.vector
        def _(v):
            with v.If(wanted(v) == 1):
                n = [0]

                def link(ins, wait=True):
                    n[0] += 1
                    ins.then_inc(dve_done, 1)
                    if wait:
                        v.wait_ge(dve_done, n[0])

                link(v.memset(X[:, NT - 1, :], 0.0), False)
                link(v.memset(src_i[:, EC:ET], N), False)
                link(v.memset(sels[:, PROD, :], 0.0), False)
                link(v.memset(dst_i[:, EC:ET], N), False)
                link(v.memset(weight[:, EC:ET], 0.0), False)
                link(v.memset(attr[:, EC:ET, :], 0.0), False)
                link(v.memset(zeros[:, :], 0.0), False)
                link(v.memset(pay_col[:, EK + 1:PK], 1.0))
                v.wait_ge(loaded, 16 * len(N_LOADS))
                link(v.tensor_copy(iota_b[:, :], iota))
                link(v.tensor_copy(dst_f[:, :], dst_i[:, :]))

                def histogram(which, slot, base):
                    link(v.tensor_scalar(part_i[:, :], which[:, :], P - 1, None, ALU.bitwise_and))
                    link(v.tensor_copy(low[:, :], part_i[:, :]))
                    link(v.tensor_scalar(part_i[:, :], which[:, :], 7, None, ALU.logical_shift_right))
                    link(v.tensor_copy(high[:, :], part_i[:, :]))
                    with v.Fori(0, ET // 2) as t2:
                        for b in range(2):
                            t = t2 * 2 + b
                            v.wait_ge(hot_used, t + (base + 1))
                            v.tensor_tensor(hot_low[:, b, :], iota_b[:, :],
                                            low[:, bass.ds(t, 1)].broadcast_to([P, P]), ALU.is_equal)
                            v.tensor_tensor(hot_high[:, b, 0:NT], iota_b[:, 0:NT],
                                            high[:, bass.ds(t, 1)].broadcast_to([P, NT]), ALU.is_equal).then_inc(hot_ready, 1)
                    v.wait_ge(hot_used, base + ET + 2)
                    link(v.tensor_copy(deg[:, slot, :], ps_hist[:, 0:NT]))
                    v.sem_inc(counted, 1)
                histogram(dst_i, 0, 0)
                histogram(src_i, 1, ET)
                link(v.tensor_scalar(deg[:, 5, :], deg[:, 0, :], 1.0, None, ALU.max))
                link(v.reciprocal(deg[:, 4, :], deg[:, 5, :]))
                link(v.tensor_scalar(deg[:, 2:4, :], deg[:, 0:2, :], 1.0, None, ALU.add))
                link(v.tensor_scalar(bn[:, 0, :], rows[:, 3, :], EPS, None, ALU.add), False)
                v.wait_ge(dve_done, n[0])
                v.sem_inc(roots_asked, 1)
                v.wait_ge(roots_done, 2)
                link(v.reciprocal(deg[:, 2:4, :], roots[:, 0:2 * NT].rearrange("p (a b) -> p a b", a=2)))
                link(v.reciprocal(bn[:, 1, :], roots[:, 64:64 + P]))
                link(v.tensor_tensor(bn[:, 2, :], bn[:, 1, :], rows[:, 0, :], ALU.mult))
                link(v.tensor_tensor(bn[:, 3, :], bn[:, 2, :], rows[:, 2, :], ALU.mult))
                link(v.tensor_tensor(bn[:, 3, :], rows[:, 1, :], bn[:, 3, :], ALU.subtract))
                v.wait_ge(z_ready, 1)
                link(v.tensor_copy(W[:, 3, :], z[:, 0, 0:P]))
                link(v.tensor_copy(W[:, 10, :], z[:, 0, P:2 * P]))
                v.sem_inc(z_free_dve, 1)
                v.wait_ge(z_ready, 2)
                link(v.tensor_copy(WEDGE[0:EK, :, :], z[0:EK, 1, 0:5 * P].rearrange("p (l d) -> p l d", l=5)))
                v.sem_inc(z_free_dve, 1)

                def scale_of(name):
                    return {"dis": 2, "dis2": 3, "inv": 4}[name]

                def each_node(kind):
                    return deg[:, scale_of(kind), :].unsqueeze(2).broadcast_to([P, NT, P])

                def norm(k0, out):
                    for g in range(NG):
                        v.wait_ge(z_ready, k0 + g + 1)
                        sl = slice(g * GT, (g + 1) * GT)
                        link(v.tensor_tensor(Y[:, sl, :], region(k0 + g).rearrange("p (t f) -> p t f", t=GT),
                                             X[:, sl, :], ALU.add))
                        v.sem_inc(z_free_dve, 1)
                    norm_rows(out)

                def norm_rows(out):
                    for j in range(NT):
                        v.bn_stats(stats[:, j, :], Y[:, j, :]).then_inc(dve_done, 1)
                    n[0] += NT
                    v.wait_ge(dve_done, n[0])
                    for j in range(NT):
                        v.bn_aggr(mv[:, j, :], stats[:, j, :]).then_inc(dve_done, 1)
                    n[0] += NT
                    v.wait_ge(dve_done, n[0])
                    link(v.tensor_scalar(sd[:, 0, :], mv[:, :, 1], EPS, None, ALU.add))
                    v.sem_inc(sd_asked, 1)
                    norms[0] += 1
                    v.wait_ge(sd_root, norms[0])
                    link(v.reciprocal(sd[:, 0, :], sd[:, 1, :]))
                    for j in range(NT):
                        v.tensor_scalar(out[:, j, :], Y[:, j, :], mv[:, j, 0:1], sd[:, 0, j:j + 1],
                                        ALU.subtract, ALU.mult).then_inc(dve_done, 1)
                    n[0] += NT
                    v.wait_ge(dve_done, n[0])
                    v.sem_inc(x_ready, 1)

                norms = [0]
                k, z_k = 0, 2
                for s in order:
                    if s[0] == "turn":
                        z_k += NG
                    elif s[0] == "dense":
                        if s[1] in LN_STAGES:
                            if k:
                                v.wait_ge(table_done, 16 * k)
                            norm(z_k, X)
                            if s[1] == 2:
                                link(v.tensor_copy(T[:, :, :], X[:, :, :]))
                                v.sem_inc(t_ready, 1)
                            elif s[1] == 3:
                                link(v.tensor_tensor(T[:, :, :], X[:, :, :], each_node("dis2"), ALU.mult))
                                v.sem_inc(t_ready, 1)
                        else:
                            v.wait_ge(z_free_act, free_count(z_k + NG - 1))
                            if s[1] == 0:
                                link(v.tensor_tensor(T[:, :, :], T[:, :, :], bn[:, 2:3, :].broadcast_to([P, NT, P]), ALU.mult))
                                link(v.tensor_tensor(T[:, :, :], T[:, :, :], bn[:, 3:4, :].broadcast_to([P, NT, P]), ALU.add))
                                link(v.tensor_tensor(T[:, :, :], T[:, :, :], each_node("dis"), ALU.mult))
                            v.sem_inc(t_ready, 1)
                        z_k += NG
                    elif s[0] == "sum":
                        kind = s[1]
                        if kind == ATTR:
                            v.wait_ge(table_done, 16 * k)
                            link(v.tensor_copy(Y[:, :, :], each_node("dis2")))
                            link(v.tensor_copy(T[:, :, :], Y[:, :, :]))
                            v.sem_inc(t_ready, 1)
                        base = n[0]
                        first = k * ET
                        with v.Fori(0, ET) as t:
                            def done(i):
                                v.wait_ge(dve_done, t * TD + (base + i))
                            v.wait_ge(tile_through, t + (first + 1))
                            v.tensor_copy(src_col[:, :], src_i[:, bass.ds(t, 1)]).then_inc(dve_done, 1)
                            v.tensor_copy(row_f[:, :], dst_f[:, bass.ds(t, 1)]).then_inc(dve_done, 1)
                            v.tensor_copy(pay_col[:, 0:EK], attr[:, bass.ds(t, 1), :].rearrange("p o k -> p (o k)")).then_inc(dve_done, 1)
                            v.tensor_copy(pay_col[:, EK:EK + 1], weight[:, bass.ds(t, 1)]).then_inc(dve_done, 1)
                            done(4)
                            v.tensor_scalar(diag[:, :], ident, row_f[:, 0:1], None, ALU.mult).then_inc(dve_done, 1)
                            done(5)
                            v.sem_inc(cols_ready, 1)
                            v.wait_ge(pe_row, t + (first + 1))
                            v.tensor_scalar(same[:, :], ps_row[:, 0:P], row_f[:, 0:1], None, ALU.is_equal).then_inc(dve_done, 1)
                            done(6)
                            v.tensor_tensor_reduce(before[:, :], same[:, :], tril, 1.0, 0.0, ALU.mult, ALU.add,
                                                   n_before[:, :]).then_inc(dve_done, 1)
                            v.wait_ge(pe_pay, t + (first + 1))
                            v.tensor_copy(pay_t[:, :], ps_mul[0:PK, 256:256 + P]).then_inc(pay_ready, 1)
                            done(7)
                            v.tensor_scalar(n_before[:, :], n_before[:, :], 1.0, None, ALU.min).then_inc(dve_done, 1)
                            v.tensor_tensor(to_dump[:, :], dump_row, row_f[:, :], ALU.subtract).then_inc(dve_done, 1)
                            done(9)
                            v.tensor_tensor(to_dump[:, :], to_dump[:, :], n_before[:, :], ALU.mult).then_inc(dve_done, 1)
                            done(10)
                            v.tensor_tensor(row_col[:, :], to_dump[:, :], row_f[:, :], ALU.add).then_inc(dve_done, 1)
                            v.wait_ge(gather_done[k], t * 16 + 16)
                            v.wait_ge(pe_mul, t + (first + 1))
                            v.tensor_tensor(msg[:, :], gathered[:, :], ps_mul[:, 0:P], ALU.mult).then_inc(msg_ready, 1)
                            v.wait_ge(pe_sum, t + (first + 1))
                            v.tensor_copy(joined[:, :], ps_sum[:, 0:P]).then_inc(dve_done, 1)
                            done(12)
                            v.sem_inc(joined_ready, 1)
                        n[0] += TD * ET
                        k += 1
                        v.wait_ge(summed, 16 * k)
                        if kind == PROD:
                            continue
                        if kind == ATTR:
                            link(v.tensor_tensor(AG[:, :, EK:EK + 1], AG[:, :, EK:EK + 1], T[:, :, 0:1], ALU.add))
                        elif s[3]:
                            link(v.tensor_tensor(AG[:, :, :], AG[:, :, :], T[:, :, :], ALU.add))
                        link(v.tensor_tensor(AG[:, :, :], AG[:, :, :], each_node(s[2]), ALU.mult))
                        v.sem_inc(ag_ready, 1)
                    elif s[0] == "final":
                        link(v.tensor_tensor(AG[:, :, :], AG[:, :, :], rows[:, 4:5, :].broadcast_to([P, NT, P]), ALU.add))
                        link(v.tensor_tensor(Y[:, :, :], AG[:, :, :], X[:, :, :], ALU.add))
                        norm_rows(AG)
            v.end_ifs()

        @block.scalar
        def _(act):
            with act.If(wanted(act) == 1):
                act.wait_ge(roots_asked, 1)
                act.activation(roots[:, 0:2 * NT], deg[:, 2:4, :].rearrange("p a b -> p (a b)"), ACT.Sqrt).then_inc(roots_done, 1)
                act.activation(roots[:, 64:64 + P], bn[:, 0, :], ACT.Sqrt).then_inc(roots_done, 1)
                z_k, k, norms = 2, 0, 0
                for s in order:
                    if s[0] == "turn":
                        to = {"PT": PT, "XT": XT, "AUG": AUG}[s[2]]
                        for g in range(NG):
                            act.wait_ge(z_ready, z_k + g + 1)
                            act.copy(to[:, g * GT * P:(g + 1) * GT * P], region(z_k + g)).then_inc(z_free_act, 1)
                        z_k += NG
                    elif s[0] == "dense":
                        st = s[1]
                        if st in LN_STAGES:
                            norms += 1
                            act.wait_ge(sd_asked, norms)
                            act.activation(sd[:, 1, :], sd[:, 0, :], ACT.Sqrt).then_inc(sd_root, 1)
                        else:
                            if k:
                                act.wait_ge(table_done, 16 * k)
                                act.wait_ge(ag_ready, k)
                            for g in range(NG):
                                act.wait_ge(z_ready, z_k + g + 1)
                                for i in range(GT):
                                    j = g * GT + i
                                    scale = 1.0 if st in (0, 9) else deg[:, 2 if st < 3 else 3, j:j + 1]
                                    ins = act.activation(T[:, j, :], tile(z_k + g, i), ACT.Copy if st == 9 else ACT.Relu, scale=scale)
                                ins.then_inc(z_free_act, 1)
                        z_k += NG
                    elif s[0] == "sum":
                        k += 1
                    elif s[0] == "final":
                        norms += 1
                        act.wait_ge(sd_asked, norms)
                        act.activation(sd[:, 1, :], sd[:, 0, :], ACT.Sqrt).then_inc(sd_root, 1)
            act.end_ifs()

        @block.tensor
        def _(pe):
            with pe.If(wanted(pe) == 1):
                pe.sem_inc(hot_used, 2)
                pe.wait_ge(loaded, 16 * len(N_LOADS))
                for h in range(2):
                    pe.matmul(ps_hist[:, 0:NT], zeros[:, :], zeros[:, 0:NT], start=True, stop=False, skip_group_check=True)
                    with pe.Fori(0, ET // 2) as t2:
                        for b in range(2):
                            t = t2 * 2 + b
                            pe.wait_ge(hot_ready, t + (h * ET + 1))
                            pe.matmul(ps_hist[:, 0:NT], hot_low[:, b, :], hot_high[:, b, 0:NT], start=False, stop=False,
                                      skip_group_check=True).then_inc(hot_used, 1)
                    if h == 0:
                        pe.wait_ge(counted, 1)
                pe.transpose(z[:, 0, 0:P], WRAW[:, 0, :], ident)
                pe.transpose(z[:, 0, P:2 * P], WRAW[:, 1, :], ident).then_inc(z_ready, 1)
                for i in range(5):
                    ins = pe.transpose(z[0:EK, 1, i * P:(i + 1) * P], EWR[:, i, :], ident)
                ins.then_inc(z_ready, 1)
                z_k, k, x_n = 2, 0, 0
                ag_k = 0
                last_pt = last_xt = last_aug = 0
                for s in order:
                    if s[0] == "turn":
                        src = {"X": X, "AG": AG}[s[1]]
                        if s[1] == "AG":
                            ag_k += 1
                            pe.wait_ge(ag_ready, ag_k)
                        elif x_n:
                            pe.wait_ge(x_ready, x_n)
                        for g in range(NG):
                            pe.wait_ge(z_free[fills[z_k + g - 2]], free_count(z_k + g - 2))
                            for i in range(GT):
                                ins = pe.transpose(tile(z_k + g, i), src[:, g * GT + i, :], ident)
                            ins.then_inc(z_ready, 1)
                        z_k += NG
                        turned = free_count(z_k - 1)
                    elif s[0] == "dense":
                        st = s[1]
                        pe.wait_ge(z_free_act, turned)
                        if st in LN_STAGES:
                            x_n += 1
                        for g in range(NG):
                            pe.wait_ge(z_free[fills[z_k + g - 2]], free_count(z_k + g - 2))
                            for i in range(GT):
                                c = slice((g * GT + i) * P, (g * GT + i + 1) * P)
                                to = tile(z_k + g, i)
                                ins = pe.matmul(to, PT[:, c], W[:, st, :], start=True, stop=(st == 9))
                                if st == 3:
                                    pe.matmul(to, XT[:, c], W[:, 10, :], start=False, stop=False)
                                if st >= 4 and st < 9:
                                    pe.matmul(to, AUG[0:EK + 1, c], WEDGE[:, st - 4, :], start=False, stop=False)
                                if st < 9:
                                    ins = pe.matmul(to, ones[0:1, :], bias[0:1, st, :], start=False, stop=True)
                            ins.then_inc(z_ready, 1)
                        z_k += NG
                    elif s[0] == "sum":
                        first = k * ET
                        with pe.Fori(0, ET) as t:
                            pe.wait_ge(cols_ready, t + (first + 1))
                            pe.matmul(ps_row[:, 0:P], ones, diag[:, :], start=True, stop=True).then_inc(pe_row, 1)
                            pe.transpose(ps_mul[0:PK, 256:256 + P], pay_col[:, :], ident).then_inc(pe_pay, 1)
                            pe.wait_ge(pay_ready, t + (first + 1))
                            pe.matmul(ps_mul[:, 0:P], pay_t[:, :], sels[:, s[1], :], start=True, stop=True).then_inc(pe_mul, 1)
                            pe.wait_ge(msg_ready, t + (first + 1))
                            pe.matmul(ps_sum[:, 0:P], same[:, :], msg[:, :], start=True, stop=True).then_inc(pe_sum, 1)
                        k += 1
            pe.end_ifs()


def build(nc, a, out):
    with ExitStack() as sems:
        verdict = sems.enter_context(nc.sbuf_tensor("verdict", [1, 1], I32))
        quick_program(nc, a, out, verdict, sems)
        general_program(nc, a, out, verdict, sems)


def host_arrays():
    c_general, c_sel = general_constants()
    return {"c_general": c_general, "c_sel": c_sel, **quick_constants()}


_OUT = "out_0_dram"


def kernel(**inputs):
    import concourse.bacc as bacc
    from concourse.bass_utils import run_bass_kernel_spmd

    nc = bacc.Bacc("TRN2", target_bir_lowering=False, num_devices=1)
    arrays, args = {}, {}
    for name, a in {**inputs, **host_arrays()}.items():
        a = np.ascontiguousarray(a)
        arrays[f"in_{name}_dram"] = a
        args[name] = nc.dram_tensor(f"in_{name}_dram", a.shape, mybir.dt.from_np(a.dtype), kind="ExternalInput").ap()
    out = nc.dram_tensor(_OUT, (N, P), F32, kind="ExternalOutput").ap()
    build(nc, args, out)
    return run_bass_kernel_spmd(nc, [arrays], core_ids=[0]).results[0][_OUT]
```
